# Optimizing a Trainium2 kernel written in Bass

```python
import numpy as np
import jax
import jax.numpy as jnp

def _softmax(x, axis=-1):
    return jax.nn.softmax(x, axis=axis)

def _gelu(x):
    return jax.nn.gelu(x, approximate=True)

def _silu(x):
    return jax.nn.silu(x)

def _sigmoid(x):
    return jax.nn.sigmoid(x)

def _layernorm(x, axis=-1, eps=1e-05):
    m = jnp.mean(x, axis=axis, keepdims=True)
    v = jnp.var(x, axis=axis, keepdims=True)
    return (x - m) / jnp.sqrt(v + eps)

def _scatter_add(tgt, idx, src, axis=0):
    return tgt.at[idx].add(src)

def _segment_sum(src, seg, n):
    return jax.ops.segment_sum(src, seg, n)
kernel_name = 'mk_hybrid_d2_jaxref_r8_baf13a'

def setup_inputs(seed: int=0):
    np.random.seed(seed)
    _w = jnp.asarray

    def _L0_attn_a_setup():
        import jax, jax.numpy as jnp
        import numpy as np
        B, S, D = (2, 256, 128)
        H = 16
        DK = 128
        DV = 128
        EPS = 1e-05
        key = jax.random.key(seed)
        k1, k2, k3, k4 = jax.random.split(key, 4)
        x = jax.random.normal(k1, (B, S, D), dtype=jnp.float32)
        Wq = jax.random.normal(k2, (DK, D), dtype=jnp.float32) * 0.02
        Wk = jax.random.normal(k3, (DK, D), dtype=jnp.float32) * 0.02
        Wv = jax.random.normal(k4, (DV, D), dtype=jnp.float32) * 0.02
        return {'x': x, 'Wq': Wq, 'Wk': Wk, 'Wv': Wv}
    _L0_attn_a_in = _L0_attn_a_setup()

    def _L0_attn_b_setup():
        import jax, jax.numpy as jnp
        import numpy as np
        HEADS = 16
        DIM_HEAD = 64
        B, T, C = (4, 256, 128)

        def apply_rope(x):
            d = x.shape[-1]
            seq_len = x.shape[1]
            inv_freq = 1.0 / 10000.0 ** (jnp.arange(0, d, 2, dtype=jnp.float32) / d)
            pos = jnp.arange(seq_len, dtype=jnp.float32)
            ang = pos[:, None] * inv_freq[None, :]
            sin = jnp.sin(ang)[None]
            cos = jnp.cos(ang)[None]
            x1, x2 = (x[..., 0::2], x[..., 1::2])
            rot = jnp.stack([x1 * cos - x2 * sin, x1 * sin + x2 * cos], axis=-1)
            return rot.reshape(x.shape)
        key = jax.random.key(seed)
        ks = jax.random.split(key, 6)
        inner = HEADS * DIM_HEAD
        w = 0.02
        return {'x': jax.random.normal(ks[0], (B, T, C), dtype=jnp.float32), 'Wq': jax.random.normal(ks[1], (C, inner), dtype=jnp.float32) * w, 'Wk': jax.random.normal(ks[2], (C, inner), dtype=jnp.float32) * w, 'Wv': jax.random.normal(ks[3], (C, inner), dtype=jnp.float32) * w, 'Wo': jax.random.normal(ks[4], (inner, C), dtype=jnp.float32) * w, 'bo': jnp.zeros((C,), dtype=jnp.float32)}
    _L0_attn_b_in = _L0_attn_b_setup()

    def _L0_ffn_setup():
        import jax, jax.numpy as jnp
        import numpy as np
        B, S, D, F, E = (1, 128, 128, 512, 8)
        EPS = 1e-05

        def _sublayer(xs, g, b, W1e, b1e, W2e, b2e):
            mu = jnp.mean(xs, axis=-1, keepdims=True)
            var = jnp.mean(jnp.square(xs - mu), axis=-1, keepdims=True)
            h = (xs - mu) * jax.lax.rsqrt(var + EPS) * g + b
            return xs + jax.nn.relu(h @ W1e.T + b1e) @ W2e.T + b2e
        key = jax.random.key(seed)
        ks = jax.random.split(key, 4)
        x = jax.random.normal(ks[0], (B, S, D), jnp.float32)
        centroids = jax.random.normal(ks[1], (E, D), jnp.float32) * 0.1
        gamma = jnp.ones((E, D), jnp.float32)
        beta = jnp.zeros((E, D), jnp.float32)
        W1 = jax.random.normal(ks[2], (E, F, D), jnp.float32) * 0.02
        b1 = jnp.zeros((E, F), jnp.float32)
        W2 = jax.random.normal(ks[3], (E, D, F), jnp.float32) * 0.02
        b2 = jnp.zeros((E, D), jnp.float32)
        return {'x': x, 'centroids': centroids, 'gamma': gamma, 'beta': beta, 'W1': W1, 'b1': b1, 'W2': W2, 'b2': b2}
    _L0_ffn_in = _L0_ffn_setup()

    def _L1_attn_a_setup():
        import jax, jax.numpy as jnp
        import numpy as np
        B, T, D = (2, 256, 128)
        H, DK, DV, M = (4, 32, 32, 32)
        GATE_NORM = 8.0
        SCALE = 1.0
        EPS = 1e-05

        def _gsa(q, k, v, s, f, scale):
            Bb, Hh = (q.shape[1], q.shape[2])
            gk = jnp.exp(f)

            def step1(S, inp):
                qt, kt, st, gt = inp
                S = S * gt[..., None, :] + kt[..., :, None] * st[..., None, :]
                return (S, jnp.einsum('bhk,bhkm->bhm', qt * scale, S))
            S0k = jnp.zeros((Bb, Hh, DK, M), q.dtype)
            _, ok = jax.lax.scan(step1, S0k, (q, k, s, gk))
            qv = jax.nn.softmax(ok, axis=-1)

            def step2(S, inp):
                qt, st, vt, gt = inp
                S = S * gt[..., :, None] + st[..., :, None] * vt[..., None, :]
                return (S, jnp.einsum('bhm,bhmv->bhv', qt, S))
            S0v = jnp.zeros((Bb, Hh, M, DV), q.dtype)
            _, ov = jax.lax.scan(step2, S0v, (qv, s, v, gk))
            return ov
        key = jax.random.key(seed)
        ks = jax.random.split(key, 7)
        w = lambda k, shp: jax.random.normal(k, shp, dtype=jnp.float32) * 0.02
        return {'hidden_states': jax.random.normal(ks[0], (B, T, D), dtype=jnp.float32), 'Wq': w(ks[1], (H * DK, D)), 'Wk': w(ks[2], (H * DK, D)), 'Wv': w(ks[3], (H * DV, D)), 'Wf': w(ks[4], (H * M, D)), 'g_w': jnp.ones((H * DV,), dtype=jnp.float32), 'Wo': w(ks[5], (D, H * DV))}
    _L1_attn_a_in = _L1_attn_a_setup()

    def _L1_attn_b_setup():
        import jax, jax.numpy as jnp
        import numpy as np
        LN_EPS = 1e-05
        key = jax.random.key(seed)
        ks = jax.random.split(key, 7)
        B, L, D, N = (8, 256, 128, 16)
        x = jax.random.normal(ks[0], (B, L, D), jnp.float32)
        A = jax.random.normal(ks[1], (D, N, N), jnp.float32) * (0.2 / np.sqrt(N))
        Bp = jax.random.normal(ks[2], (D, N), jnp.float32)
        Cp = jax.random.normal(ks[3], (D, N), jnp.float32)
        Dp = jax.random.normal(ks[4], (D,), jnp.float32)
        Wg = jax.random.normal(ks[5], (D, D), jnp.float32) / np.sqrt(D)
        bg = jnp.zeros((D,), jnp.float32)
        gamma = jnp.ones((D,), jnp.float32)
        beta = jnp.zeros((D,), jnp.float32)
        return dict(x=x, A=A, Bp=Bp, Cp=Cp, Dp=Dp, Wg=Wg, bg=bg, gamma=gamma, beta=beta)
    _L1_attn_b_in = _L1_attn_b_setup()

    def _L1_ffn_setup():
        import jax, jax.numpy as jnp
        import numpy as np
        EPS = 1e-06
        LN_EPS = 1e-05

        def _absmean_core(W):
            gamma = jnp.mean(jnp.abs(W)) + EPS
            Ws = W / gamma
            Wq = jnp.sign(Ws) * jnp.minimum(jnp.round(jnp.abs(Ws)), 1.0)
            return (Wq, gamma)

        @jax.custom_vjp
        def absmean(W):
            return _absmean_core(W)[0]

        def _absmean_fwd(W):
            Wq, gamma = _absmean_core(W)
            return (Wq, gamma)

        def _absmean_bwd(gamma, g):
            return (g / gamma,)
        absmean.defvjp(_absmean_fwd, _absmean_bwd)

        def layernorm(x, w, b, eps=LN_EPS):
            mu = jnp.mean(x, axis=-1, keepdims=True)
            var = jnp.mean((x - mu) ** 2, axis=-1, keepdims=True)
            return (x - mu) * jax.lax.rsqrt(var + eps) * w + b
        key = jax.random.key(seed)
        k1, k2, k3 = jax.random.split(key, 3)
        d, h = (128, 512)
        B, T = (8, 256)
        return {'x': jax.random.normal(k1, (B, T, d), jnp.float32), 'W_fc': jax.random.normal(k2, (h, d), jnp.float32), 'ln_w': jnp.ones((h,), jnp.float32), 'ln_b': jnp.zeros((h,), jnp.float32), 'W_proj': jax.random.normal(k3, (d, h), jnp.float32)}
    _L1_ffn_in = _L1_ffn_setup()
    _d = {'L0_attn_a_x': _L0_attn_a_in['x'], 'L0_attn_a_Wq': _L0_attn_a_in['Wq'], 'L0_attn_a_Wk': _L0_attn_a_in['Wk'], 'L0_attn_a_Wv': _L0_attn_a_in['Wv'], 'L0_attn_b_Wq': _L0_attn_b_in['Wq'], 'L0_attn_b_Wk': _L0_attn_b_in['Wk'], 'L0_attn_b_Wv': _L0_attn_b_in['Wv'], 'L0_attn_b_Wo': _L0_attn_b_in['Wo'], 'L0_attn_b_bo': _L0_attn_b_in['bo'], 'L0_ffn_centroids': _L0_ffn_in['centroids'], 'L0_ffn_gamma': _L0_ffn_in['gamma'], 'L0_ffn_beta': _L0_ffn_in['beta'], 'L0_ffn_W1': _L0_ffn_in['W1'], 'L0_ffn_b1': _L0_ffn_in['b1'], 'L0_ffn_W2': _L0_ffn_in['W2'], 'L0_ffn_b2': _L0_ffn_in['b2'], 'L1_attn_a_Wq': _L1_attn_a_in['Wq'], 'L1_attn_a_Wk': _L1_attn_a_in['Wk'], 'L1_attn_a_Wv': _L1_attn_a_in['Wv'], 'L1_attn_a_Wf': _L1_attn_a_in['Wf'], 'L1_attn_a_g_w': _L1_attn_a_in['g_w'], 'L1_attn_a_Wo': _L1_attn_a_in['Wo'], 'L1_attn_b_A': _L1_attn_b_in['A'], 'L1_attn_b_Bp': _L1_attn_b_in['Bp'], 'L1_attn_b_Cp': _L1_attn_b_in['Cp'], 'L1_attn_b_Dp': _L1_attn_b_in['Dp'], 'L1_attn_b_Wg': _L1_attn_b_in['Wg'], 'L1_attn_b_bg': _L1_attn_b_in['bg'], 'L1_attn_b_gamma': _L1_attn_b_in['gamma'], 'L1_attn_b_beta': _L1_attn_b_in['beta'], 'L1_ffn_W_fc': _L1_ffn_in['W_fc'], 'L1_ffn_ln_w': _L1_ffn_in['ln_w'], 'L1_ffn_ln_b': _L1_ffn_in['ln_b'], 'L1_ffn_W_proj': _L1_ffn_in['W_proj']}
    _x0 = _d['L0_attn_a_x']
    _d['L0_attn_a_x'] = jax.random.normal(jax.random.fold_in(jax.random.key(seed), 1), (16, 512, 128), dtype=_x0.dtype)
    del _x0
    return _d

def reference(L0_attn_a_x, L0_attn_a_Wq, L0_attn_a_Wk, L0_attn_a_Wv, L0_attn_b_Wq, L0_attn_b_Wk, L0_attn_b_Wv, L0_attn_b_Wo, L0_attn_b_bo, L0_ffn_centroids, L0_ffn_gamma, L0_ffn_beta, L0_ffn_W1, L0_ffn_b1, L0_ffn_W2, L0_ffn_b2, L1_attn_a_Wq, L1_attn_a_Wk, L1_attn_a_Wv, L1_attn_a_Wf, L1_attn_a_g_w, L1_attn_a_Wo, L1_attn_b_A, L1_attn_b_Bp, L1_attn_b_Cp, L1_attn_b_Dp, L1_attn_b_Wg, L1_attn_b_bg, L1_attn_b_gamma, L1_attn_b_beta, L1_ffn_W_fc, L1_ffn_ln_w, L1_ffn_ln_b, L1_ffn_W_proj):

    def _L0_attn_a_ref(x, Wq, Wk, Wv):
        import jax, jax.numpy as jnp
        import numpy as np
        B, S, D = (2, 256, 128)
        H = 16
        DK = 128
        DV = 128
        EPS = 1e-05
        b, s, d = x.shape
        dkh = DK // H
        dvh = DV // H
        Q = (x @ Wq.T).reshape(H, b, s, dkh)
        K = (x @ Wk.T).reshape(H, b, s, dkh)
        V = (x @ Wv.T).reshape(H, b, s, dvh)
        scores = jnp.einsum('hbqd,hbkd->hbqk', Q, K)
        atten = jax.nn.softmax(scores, axis=-1)
        out = jnp.einsum('hbqk,hbkd->hbqd', atten, V).reshape(b, s, -1)
        y = out + x
        mu = jnp.mean(y, axis=(1, 2), keepdims=True)
        var = jnp.var(y, axis=(1, 2), keepdims=True)
        return (y - mu) / jnp.sqrt(var + EPS)

    def _L0_attn_b_ref(x, Wq, Wk, Wv, Wo, bo):
        import jax, jax.numpy as jnp
        import numpy as np
        HEADS = 16
        DIM_HEAD = 64
        B, T, C = (4, 256, 128)

        def apply_rope(x):
            d = x.shape[-1]
            seq_len = x.shape[1]
            inv_freq = 1.0 / 10000.0 ** (jnp.arange(0, d, 2, dtype=jnp.float32) / d)
            pos = jnp.arange(seq_len, dtype=jnp.float32)
            ang = pos[:, None] * inv_freq[None, :]
            sin = jnp.sin(ang)[None]
            cos = jnp.cos(ang)[None]
            x1, x2 = (x[..., 0::2], x[..., 1::2])
            rot = jnp.stack([x1 * cos - x2 * sin, x1 * sin + x2 * cos], axis=-1)
            return rot.reshape(x.shape)
        b, t, c = x.shape
        h, d = (HEADS, DIM_HEAD)
        scale = d ** (-0.5)

        def split_heads(z):
            return z.reshape(b, t, h, d).transpose(0, 2, 1, 3).reshape(b * h, t, d)
        q = split_heads(x @ Wq)
        k = split_heads(x @ Wk)
        v = split_heads(x @ Wv)
        q = apply_rope(q)
        k = apply_rope(k)
        sim = jnp.einsum('bid,bjd->bij', q, k) * scale
        causal = jnp.tril(jnp.ones((t, t), dtype=bool))
        sim = jnp.where(causal[None], sim, -jnp.inf)
        attn = jax.nn.softmax(sim, axis=-1)
        out = jnp.einsum('bij,bjd->bid', attn, v)
        out = out.reshape(b, h, t, d).transpose(0, 2, 1, 3).reshape(b, t, h * d)
        return out @ Wo + bo

    def _L0_ffn_ref(x, centroids, gamma, beta, W1, b1, W2, b2):
        import jax, jax.numpy as jnp
        import numpy as np
        B, S, D, F, E = (1, 128, 128, 512, 8)
        EPS = 1e-05

        def _sublayer(xs, g, b, W1e, b1e, W2e, b2e):
            mu = jnp.mean(xs, axis=-1, keepdims=True)
            var = jnp.mean(jnp.square(xs - mu), axis=-1, keepdims=True)
            h = (xs - mu) * jax.lax.rsqrt(var + EPS) * g + b
            return xs + jax.nn.relu(h @ W1e.T + b1e) @ W2e.T + b2e
        feats = x.reshape(-1, x.shape[-1])
        scores = jax.lax.stop_gradient(feats @ centroids.T)
        expert = jnp.argmax(scores, axis=1)
        onehot = jax.nn.one_hot(expert, E, dtype=feats.dtype)
        alpha = jax.nn.sigmoid(jnp.sum(feats * centroids[expert], axis=-1, keepdims=True))
        ys = jax.vmap(_sublayer, in_axes=(None, 0, 0, 0, 0, 0, 0))(feats, gamma, beta, W1, b1, W2, b2)
        y = jnp.einsum('te,etd->td', onehot, ys)
        out = alpha * y + (1.0 - alpha) * feats
        return out.reshape(x.shape)

    def _L1_attn_a_ref(hidden_states, Wq, Wk, Wv, Wf, g_w, Wo):
        import jax, jax.numpy as jnp
        import numpy as np
        B, T, D = (2, 256, 128)
        H, DK, DV, M = (4, 32, 32, 32)
        GATE_NORM = 8.0
        SCALE = 1.0
        EPS = 1e-05

        def _gsa(q, k, v, s, f, scale):
            Bb, Hh = (q.shape[1], q.shape[2])
            gk = jnp.exp(f)

            def step1(S, inp):
                qt, kt, st, gt = inp
                S = S * gt[..., None, :] + kt[..., :, None] * st[..., None, :]
                return (S, jnp.einsum('bhk,bhkm->bhm', qt * scale, S))
            S0k = jnp.zeros((Bb, Hh, DK, M), q.dtype)
            _, ok = jax.lax.scan(step1, S0k, (q, k, s, gk))
            qv = jax.nn.softmax(ok, axis=-1)

            def step2(S, inp):
                qt, st, vt, gt = inp
                S = S * gt[..., :, None] + st[..., :, None] * vt[..., None, :]
                return (S, jnp.einsum('bhm,bhmv->bhv', qt, S))
            S0v = jnp.zeros((Bb, Hh, M, DV), q.dtype)
            _, ov = jax.lax.scan(step2, S0v, (qv, s, v, gk))
            return ov
        Bb, Tt, Dd = hidden_states.shape
        q = (hidden_states @ Wq.T).reshape(Bb, Tt, H, DK)
        k = (hidden_states @ Wk.T).reshape(Bb, Tt, H, DK)
        v = (hidden_states @ Wv.T).reshape(Bb, Tt, H, DV)
        f = (hidden_states @ Wf.T).reshape(Bb, Tt, H, M)
        q = jax.nn.silu(q)
        k = jax.nn.silu(k)
        v = jax.nn.silu(v)
        f = jax.nn.log_sigmoid(f) / GATE_NORM
        s = 1.0 - jnp.exp(f)
        tm = lambda x: jnp.transpose(x, (1, 0, 2, 3))
        ov = _gsa(tm(q), tm(k), tm(v), tm(s), tm(f), SCALE)
        o = jnp.transpose(ov, (1, 0, 2, 3)).reshape(Bb, Tt, H * DV)
        o = jax.nn.silu(o)
        o32 = o.astype(jnp.float32)
        rms = o32 * jax.lax.rsqrt(jnp.mean(o32 * o32, axis=-1, keepdims=True) + EPS)
        return (rms * g_w).astype(hidden_states.dtype) @ Wo.T

    def _L1_attn_b_ref(x, A, Bp, Cp, Dp, Wg, bg, gamma, beta):
        import jax, jax.numpy as jnp
        import numpy as np
        LN_EPS = 1e-05
        gate = jax.nn.sigmoid(jnp.einsum('bld,ed->ble', x, Wg) + bg)
        xg = x * gate
        Bsz, L, D = xg.shape
        N = A.shape[-1]

        def step(s, xt):
            s = jnp.einsum('bdn,dnm->bdm', s, A) + xt[..., None] * Bp
            y = jnp.einsum('bdn,dn->bd', s, Cp) + Dp * xt
            return (s, y)
        s0 = jnp.zeros((Bsz, D, N), xg.dtype)
        _, ys = jax.lax.scan(step, s0, jnp.moveaxis(xg, 1, 0))
        y = jnp.moveaxis(ys, 0, 1) + xg
        mu = jnp.mean(y, axis=-1, keepdims=True)
        var = jnp.var(y, axis=-1, keepdims=True)
        return (y - mu) * jax.lax.rsqrt(var + LN_EPS) * gamma + beta

    def _L1_ffn_ref(x, W_fc, ln_w, ln_b, W_proj):
        import jax, jax.numpy as jnp
        import numpy as np
        EPS = 1e-06
        LN_EPS = 1e-05

        def _absmean_core(W):
            gamma = jnp.mean(jnp.abs(W)) + EPS
            Ws = W / gamma
            Wq = jnp.sign(Ws) * jnp.minimum(jnp.round(jnp.abs(Ws)), 1.0)
            return (Wq, gamma)

        @jax.custom_vjp
        def absmean(W):
            return _absmean_core(W)[0]

        def _absmean_fwd(W):
            Wq, gamma = _absmean_core(W)
            return (Wq, gamma)

        def _absmean_bwd(gamma, g):
            return (g / gamma,)
        absmean.defvjp(_absmean_fwd, _absmean_bwd)

        def layernorm(x, w, b, eps=LN_EPS):
            mu = jnp.mean(x, axis=-1, keepdims=True)
            var = jnp.mean((x - mu) ** 2, axis=-1, keepdims=True)
            return (x - mu) * jax.lax.rsqrt(var + eps) * w + b
        h = jnp.einsum('btd,hd->bth', x, absmean(W_fc))
        h = jax.nn.gelu(h, approximate=False)
        h = layernorm(h, ln_w, ln_b)
        return jnp.einsum('bth,dh->btd', h, absmean(W_proj))
    x = L0_attn_a_x
    x = x + _L0_attn_a_ref(_layernorm(x, axis=-1), L0_attn_a_Wq, L0_attn_a_Wk, L0_attn_a_Wv)
    x = x + _L0_ffn_ref(_layernorm(x, axis=-1), L0_ffn_centroids, L0_ffn_gamma, L0_ffn_beta, L0_ffn_W1, L0_ffn_b1, L0_ffn_W2, L0_ffn_b2)
    x = x + _L0_attn_b_ref(_layernorm(x, axis=-1), L0_attn_b_Wq, L0_attn_b_Wk, L0_attn_b_Wv, L0_attn_b_Wo, L0_attn_b_bo)
    x = x + _L0_ffn_ref(_layernorm(x, axis=-1), L0_ffn_centroids, L0_ffn_gamma, L0_ffn_beta, L0_ffn_W1, L0_ffn_b1, L0_ffn_W2, L0_ffn_b2)
    x = x + _L1_attn_a_ref(_layernorm(x, axis=-1), L1_attn_a_Wq, L1_attn_a_Wk, L1_attn_a_Wv, L1_attn_a_Wf, L1_attn_a_g_w, L1_attn_a_Wo)
    x = x + _L1_ffn_ref(_layernorm(x, axis=-1), L1_ffn_W_fc, L1_ffn_ln_w, L1_ffn_ln_b, L1_ffn_W_proj)
    x = x + _L1_attn_b_ref(_layernorm(x, axis=-1), L1_attn_b_A, L1_attn_b_Bp, L1_attn_b_Cp, L1_attn_b_Dp, L1_attn_b_Wg, L1_attn_b_bg, L1_attn_b_gamma, L1_attn_b_beta)
    x = x + _L1_ffn_ref(_layernorm(x, axis=-1), L1_ffn_W_fc, L1_ffn_ln_w, L1_ffn_ln_b, L1_ffn_W_proj)
    return x

_drawn_inputs = setup_inputs


def setup_inputs(seed=0):
    import zlib

    import numpy as np

    out = dict(_drawn_inputs(seed))
    spreads = {'L0_attn_b_bo': (0.0, 0.1),
     'L0_ffn_gamma': (1.0, 0.2),
     'L0_ffn_beta': (0.0, 0.1),
     'L0_ffn_b1': (0.0, 0.1),
     'L0_ffn_b2': (0.0, 0.1),
     'L1_attn_a_g_w': (1.0, 0.2),
     'L1_attn_b_bg': (0.0, 0.1),
     'L1_attn_b_gamma': (1.0, 0.2),
     'L1_attn_b_beta': (0.0, 0.1),
     'L1_ffn_ln_w': (1.0, 0.2),
     'L1_ffn_ln_b': (0.0, 0.1)}
    factors = {}
    for name, (base, spread) in spreads.items():
        noise = np.random.default_rng([zlib.crc32(name.encode()), seed]).standard_normal(out[name].shape)
        drawn = base * np.exp(spread * noise) if base else spread * noise
        out[name] = jnp.asarray(drawn.astype(out[name].dtype))
    for name, factor in factors.items():
        out[name] = (out[name] * factor).astype(out[name].dtype)
    return out
```

```python
import numpy as np
import concourse.bass as bass
from concourse import mybir
from contextlib import ExitStack

F32 = mybir.dt.float32
BF16 = mybir.dt.bfloat16
U32 = mybir.dt.uint32
I32 = mybir.dt.int32
ALU = mybir.AluOpType
ACT = mybir.ActivationFunctionType
AX = mybir.AxisListType

P = 128
D = 128
NB, S = 16, 512
T = NB * S // P
EPS = 1e-5


def pipeline(engine, n, unroll, stages):
    lag = max(l for _, l in stages)
    head = -(-(lag + unroll) // unroll) * unroll
    head = min(head, n)

    def step(s, at):
        for stage, l in stages:
            if not isinstance(s, int) or 0 <= s - l < n:
                stage(s - l, (at - l) % unroll)

    for s in range(head):
        step(s, s)
    if n > head:
        with engine.Fori(0, (n - head) // unroll) as i:
            for j in range(unroll):
                step(i * unroll + (head + j), j)
    for s in range(n, n + lag):
        step(s, s)


def wait(engine, sem, count):
    if not isinstance(count, int) or count > 0:
        engine.wait_ge(sem, count)


class Core:

    def __init__(self, nc, ctx):
        self.nc = nc
        self.held = []
        sb = lambda n, s, d: ctx.enter_context(nc.sbuf_tensor(n, s, d))
        self.X = sb("X", [P, T, D], F32)
        self.ident = sb("ident", [P, P], F32)
        self.identb = sb("identb", [P, P], BF16)
        self.ones = sb("ones", [P, P], F32)
        self.minus_half = sb("minus_half", [P, 8], F32)
        self.minus_eighth = sb("minus_eighth", [P, 1], F32)

    def semaphore(self, name):
        s = self.nc.alloc_semaphore(name=name)
        self.held.append(s)
        return s

    def release_semaphores(self):
        self.nc.clear_and_free_semaphores(self.held)
        self.held = []
        self.nc.all_engine_barrier()

    def load(self, x):
        nc = self.nc
        with ExitStack() as ctx:
            loaded = ctx.enter_context(nc.semaphore("x_loaded"))
            zeroed = ctx.enter_context(nc.semaphore("consts_zeroed"))
            with nc.Block() as block:
                @block.sync
                def _(sp):
                    xt = x.rearrange("(n p) d -> p n d", p=P)
                    for q in range(4):
                        sp.dma_start(self.X[:, q * 16:(q + 1) * 16, :], xt[:, q * 16:(q + 1) * 16, :]).then_inc(loaded, 16)
                    sp.wait_ge(loaded, 64)

                @block.gpsimd
                def _(pool):
                    nc.gpsimd.memset(self.ident[:], 0.0).then_inc(zeroed, 1)
                    nc.gpsimd.memset(self.identb[:], 0.0).then_inc(zeroed, 1)
                    nc.gpsimd.memset(self.ones[:], 1.0).then_inc(zeroed, 1)
                    nc.gpsimd.memset(self.minus_half[:], -0.5).then_inc(zeroed, 1)
                    nc.gpsimd.memset(self.minus_eighth[:], -0.125).then_inc(zeroed, 1)
                    pool.wait_ge(zeroed, 5)
                    for m in (self.ident, self.identb):
                        nc.gpsimd.affine_select(out=m[:], in_=m[:], compare_op=ALU.not_equal, fill=1.0, base=0,
                                                pattern=[[-1, P]], channel_multiplier=1).then_inc(zeroed, 1)
                    pool.wait_ge(zeroed, 7)

    def store(self, out):
        nc = self.nc
        with ExitStack() as ctx:
            stored = ctx.enter_context(nc.semaphore("x_stored"))
            with nc.Block() as block:
                @block.sync
                def _(sp):
                    xt = out.rearrange("(n p) d -> p n d", p=P)
                    for q in range(4):
                        sp.dma_start(xt[:, q * 16:(q + 1) * 16, :], self.X[:, q * 16:(q + 1) * 16, :]).then_inc(stored, 16)
                    sp.wait_ge(stored, 64)


class RowNorm:

    def __init__(self, core, ctx, name, slots=2):
        nc = self.nc = core.nc
        self.core, self.slots = core, slots
        sb = lambda n, s: ctx.enter_context(nc.sbuf_tensor(f"{name}_{n}", s, F32))
        sem = lambda n: core.semaphore(f"{name}_{n}")
        self.parts = sb("parts", [P, slots, 6])
        self.mv = sb("mv", [P, slots, 2])
        self.var = sb("var", [P, slots])
        self.rs = sb("rs", [P, slots])
        self.held = sem("held")
        self.parts_done, self.mean_done, self.var_done, self.rstd_done = (
            sem(n) for n in ("parts_done", "mean_done", "var_done", "rstd_done"))

    def stats(self, dve, t, s, rows):
        nc = self.nc
        nc.vector.bn_stats(self.parts[:, s, :], rows).then_inc(self.parts_done, 1)
        dve.wait_ge(self.parts_done, t + 1)
        dve.sem_inc(self.held, 1)
        nc.vector.bn_aggr(self.mv[:, s, :], self.parts[:, s, :]).then_inc(self.mean_done, 1)
        dve.wait_ge(self.mean_done, t + 1)
        nc.vector.tensor_scalar(self.var[:, s:s + 1], self.mv[:, s, 1:2], EPS, None, ALU.add).then_inc(self.var_done, 1)

    def rstd(self, pool, t, s):
        pool.wait_ge(self.var_done, t + 1)
        self.nc.gpsimd.tensor_tensor(self.rs[:, s:s + 1], self.var[:, s:s + 1], self.core.minus_half[:, 0:1], ALU.pow)\
            .then_inc(self.rstd_done, 1)

    def apply(self, out, rows, s):
        return self.nc.vector.tensor_scalar(out, rows, self.mv[:, s, 0:1], self.rs[:, s:s + 1], ALU.subtract, ALU.mult)


def tile_of(buf, t):
    return buf[:, bass.ds(t, 1), :].rearrange("p a d -> p (a d)")


def staggered(engine, n, unroll, lags, body):
    lag = max(lags)
    head = min(-(-(lag + unroll) // unroll) * unroll, n)

    def step(s, at):
        body(*[(None if isinstance(s, int) and not 0 <= s - l < n else s - l, (at - l) % unroll) for l in lags])

    for s in range(head):
        step(s, s)
    if n > head:
        with engine.Fori(0, (n - head) // unroll) as i:
            for j in range(unroll):
                step(i * unroll + (head + j), j)
    for s in range(n, n + lag):
        step(s, s)


def item_steps(engine, per_seq, last_lag, body):
    def step(b, p):
        def item(lag):
            part, seq = (p - lag) % per_seq, b + (p - lag) // per_seq
            if isinstance(b, int) and not 0 <= seq < NB:
                return None
            return seq * per_seq + part, seq, part
        body(item)

    head = -(-last_lag // per_seq)
    for b in range(head):
        for p in range(per_seq):
            step(b, p)
    with engine.Fori(0, NB - head) as i:
        for p in range(per_seq):
            step(i + head, p)
    for s in range(last_lag):
        step(NB + s // per_seq, s % per_seq)


def ternary_ffn(core, name, w_fc, ln_w, ln_b, w_proj):
    nc, X = core.nc, core.X
    H = w_fc.shape[0]
    HC = H // P
    WEIGHT_EPS = 1e-6
    with ExitStack() as ctx:
        ctx.callback(core.release_semaphores)
        sb = lambda n, s, d=F32: ctx.enter_context(nc.sbuf_tensor(f"{name}_{n}", s, d))
        pb = lambda n, k=1: ctx.enter_context(nc.psum_tensor(f"{name}_{n}", [P, 512 * k], F32))
        sem = lambda n: core.semaphore(f"{name}_{n}")
        wfc = sb("wfc", [P, HC, D])
        wpj = sb("wpj", [P, HC, P])
        lnw = sb("lnw", [P, HC])
        lnb = sb("lnb", [P, HC])
        lnb_wide = sb("lnb_wide", [P, HC, P])
        mean_abs = sb("mean_abs", [P, 2])
        bound = sb("bound", [P, 2, 2])
        low = sb("low", [P, H])
        wfcT = sb("wfcT", [P, H])
        wpjT = sb("wpjT", [P, HC, D])
        wpjT_raw = sb("wpjT_raw", [P, HC, D])
        offset = sb("offset", [P, D])
        st = sb("st", [P, 2, 6])
        mv = sb("mv", [P, 2, 2])
        ve = sb("ve", [P, 2])
        rs = sb("rs", [P, 2])
        xn = sb("xn", [P, 2, D])
        xnT = sb("xnT", [P, 2, P])
        g = sb("g", [P, 2, H])
        st2 = sb("st2", [P, 2, 6])
        mv2 = sb("mv2", [P, 2, 2])
        ve2 = sb("ve2", [P, 2])
        rs2 = sb("rs2", [P, 2])
        gn = sb("gn", [P, 2, H])
        gT = sb("gT", [P, 2, H])
        ps_a = [pb(f"ps_a{i}") for i in range(2)]
        ps_h = [pb(f"ps_h{i}") for i in range(2)]
        ps_t = [pb(f"ps_t{i}") for i in range(2)]
        ps_y = [pb(f"ps_y{i}") for i in range(2)]
        loaded = sem("loaded")
        held = sem("held")
        prep = sem("prep")
        prep_pe = sem("prep_pe")
        mean_done, rstd_done, x_normed, x_turned, xT_ready, hidden = (
            sem(n) for n in ("mean_done", "rstd_done", "x_normed", "x_turned", "xT_ready", "hidden"))
        gelu_done, mean2_done, rstd2_done, g_normed, g_turned, gT_ready, projected, added = (
            sem(n) for n in ("gelu_done", "mean2_done", "rstd2_done", "g_normed", "g_turned", "gT_ready", "projected", "added"))
        stats_in, stats2_in = sem("stats_in"), sem("stats2_in")
        var_in, var2_in = sem("var_in"), sem("var2_in")

        with nc.Block() as block:
            @block.sync
            def _(sp):
                sp.dma_start(wfc[:], w_fc.rearrange("(c p) d -> p c d", p=P)).then_inc(loaded, 16)
                sp.dma_start(wpj[:], w_proj.rearrange("d (c p) -> d c p", p=P)).then_inc(loaded, 16)
                with nc.allow_non_contiguous_dma(reason="small vectors"):
                    sp.dma_start(lnw[:], ln_w.rearrange("(c p) -> p c", p=P)).then_inc(loaded, 16)
                    sp.dma_start(lnb[:], ln_b.rearrange("(c p) -> p c", p=P)).then_inc(loaded, 16)

            @block.vector
            def _(dve):
                n = [0]

                def done(ins):
                    n[0] += 1
                    ins.then_inc(prep, 1)
                    dve.wait_ge(prep, n[0])
                dve.wait_ge(loaded, 64)
                for k, w in enumerate((wfc, wpj)):
                    done(nc.vector.tensor_reduce(mean_abs[:, k:k + 1], w[:], AX.XY, ALU.add, apply_absolute_value=True))
                dve.wait_ge(prep_pe, 1)
                done(nc.vector.tensor_scalar(bound[:, 0, :], ps_a[0][:, 0:2], 1.0 / (H * D), WEIGHT_EPS, ALU.mult, ALU.add))
                done(nc.vector.tensor_scalar(bound[:, 1, :], bound[:, 0, :], -0.5, None, ALU.mult))
                done(nc.vector.tensor_scalar(bound[:, 0, :], bound[:, 0, :], 0.5, None, ALU.mult))
                for k, w in enumerate((wfc, wpj)):
                    flat = w[:].rearrange("p c d -> p (c d)")
                    done(nc.vector.tensor_scalar(low[:], flat, bound[:, 1, k:k + 1], None, ALU.is_lt))
                    done(nc.vector.scalar_tensor_tensor(flat, flat, bound[:, 0, k:k + 1], low[:], ALU.is_gt, ALU.subtract))
                dve.wait_ge(prep_pe, 2)
                done(nc.vector.tensor_copy(wfcT[:], ps_h[0][:, 0:H]))
                done(nc.vector.tensor_copy(wpjT_raw[:].rearrange("p c d -> p (c d)"), ps_h[1][:, 0:H]))
                for c in range(HC):
                    done(nc.vector.tensor_scalar(wpjT[:, c, :], wpjT_raw[:, c, :], lnw[:, c:c + 1], None, ALU.mult))
                    done(nc.vector.tensor_scalar(lnb_wide[:, c, :], core.ones[:], lnb[:, c:c + 1], None, ALU.mult))
                dve.wait_ge(prep_pe, 3)
                done(nc.vector.tensor_copy(offset[:], ps_t[0][:, 0:D]))

                def token_stats(t, s):
                    wait(dve, x_normed, t - 1)
                    nc.vector.bn_stats(st[:, s, :], X[:, bass.ds(t, 1), :].rearrange("p a d -> p (a d)")).then_inc(stats_in, 1)
                    dve.wait_ge(stats_in, t + 1)
                    dve.sem_inc(held, 1)
                    nc.vector.bn_aggr(mv[:, s, :], st[:, s, :]).then_inc(var_in, 1)
                    dve.wait_ge(var_in, t + 1)
                    nc.vector.tensor_scalar(ve[:, s:s + 1], mv[:, s, 1:2], EPS, None, ALU.add).then_inc(mean_done, 1)

                def norm_x(t, s):
                    dve.wait_ge(rstd_done, t + 1)
                    wait(dve, x_turned, t - 1)
                    nc.vector.tensor_scalar(xn[:, s, :], X[:, bass.ds(t, 1), :].rearrange("p a d -> p (a d)"), mv[:, s, 0:1], rs[:, s:s + 1],
                                            ALU.subtract, ALU.mult).then_inc(x_normed, 1)

                def g_stats(t, s):
                    dve.wait_ge(gelu_done, t + 1)
                    wait(dve, g_normed, t - 1)
                    nc.vector.bn_stats(st2[:, s, :], g[:, s, :]).then_inc(stats2_in, 1)
                    dve.wait_ge(stats2_in, t + 1)
                    dve.sem_inc(held, 1)
                    nc.vector.bn_aggr(mv2[:, s, :], st2[:, s, :]).then_inc(var2_in, 1)
                    dve.wait_ge(var2_in, t + 1)
                    nc.vector.tensor_scalar(ve2[:, s:s + 1], mv2[:, s, 1:2], EPS, None, ALU.add).then_inc(mean2_done, 1)

                def norm_g(t, s):
                    dve.wait_ge(rstd2_done, t + 1)
                    wait(dve, g_turned, t - 1)
                    nc.vector.tensor_scalar(gn[:, s, :], g[:, s, :], mv2[:, s, 0:1], rs2[:, s:s + 1],
                                            ALU.subtract, ALU.mult).then_inc(g_normed, 1)

                def add(t, s):
                    dve.wait_ge(projected, t + 1)
                    xt = X[:, bass.ds(t, 1), :].rearrange("p a d -> p (a d)")
                    nc.vector.tensor_tensor(xt, ps_y[s][:, 0:D], xt, ALU.add).then_inc(added, 1)

                pipeline(dve, T, 2, [(add, 6), (norm_g, 4), (g_stats, 3), (norm_x, 1), (token_stats, 0)])

            @block.gpsimd
            def _(pool):
                def rstd(t, s):
                    pool.wait_ge(mean_done, t + 1)
                    nc.gpsimd.tensor_tensor(rs[:, s:s + 1], ve[:, s:s + 1], core.minus_half[:, 0:1], ALU.pow).then_inc(rstd_done, 1)

                def rstd2(t, s):
                    pool.wait_ge(mean2_done, t + 1)
                    nc.gpsimd.tensor_tensor(rs2[:, s:s + 1], ve2[:, s:s + 1], core.minus_half[:, 0:1], ALU.pow).then_inc(rstd2_done, 1)

                pipeline(pool, T, 2, [(rstd2, 3), (rstd, 0)])

            @block.tensor
            def _(pe):
                pe.wait_ge(prep, 2)
                nc.tensor.matmul(ps_a[0][:, 0:2], core.ones[:], mean_abs[:], start=True, stop=True).then_inc(prep_pe, 1)
                pe.wait_ge(prep, 9)
                for c in range(HC):
                    nc.tensor.transpose(ps_h[0][:, c * P:(c + 1) * P], wfc[:, c, :], core.ident[:])
                for c in range(HC):
                    last = nc.tensor.transpose(ps_h[1][:, c * P:(c + 1) * P], wpj[:, c, :], core.ident[:])
                last.then_inc(prep_pe, 1)
                pe.wait_ge(prep, 9 + 2 + 2 * HC)
                for c in range(HC):
                    last = nc.tensor.matmul(ps_t[0][:, 0:D], lnb_wide[:, c, :], wpjT_raw[:, c, :], start=(c == 0), stop=(c == HC - 1))
                last.then_inc(prep_pe, 1)
                pe.wait_ge(prep, 9 + 2 + 2 * HC + 1)

                def turn_x(t, s):
                    pe.wait_ge(x_normed, t + 1)
                    wait(pe, xT_ready, t - 1)
                    nc.tensor.transpose(ps_a[s][:, 0:P], xn[:, s, :], core.ident[:]).then_inc(x_turned, 1)

                def expand(t, s):
                    pe.wait_ge(xT_ready, t + 1)
                    wait(pe, gelu_done, t - 1)
                    nc.tensor.matmul(ps_h[s][:, 0:H], xnT[:, s, :], wfcT[:], start=True, stop=True).then_inc(hidden, 1)

                def turn_g(t, s):
                    pe.wait_ge(g_normed, t + 1)
                    wait(pe, gT_ready, t - 1)
                    for c in range(HC):
                        last = nc.tensor.transpose(ps_t[s][:, c * P:(c + 1) * P], gn[:, s, c * P:(c + 1) * P], core.ident[:])
                    last.then_inc(g_turned, 1)

                def contract(t, s):
                    pe.wait_ge(gT_ready, t + 1)
                    wait(pe, added, t - 1)
                    nc.tensor.matmul(ps_y[s][:, 0:D], core.ones[0:1, :], offset[0:1, :], start=True, stop=False)
                    for c in range(HC):
                        last = nc.tensor.matmul(ps_y[s][:, 0:D], gT[:, s, c * P:(c + 1) * P], wpjT[:, c, :], start=False, stop=(c == HC - 1))
                    last.then_inc(projected, 1)

                pipeline(pe, T, 2, [(contract, 5), (turn_g, 4), (expand, 2), (turn_x, 1)])

            @block.scalar
            def _(act):
                def copy_xT(t, s):
                    act.wait_ge(x_turned, t + 1)
                    wait(act, hidden, t - 1)
                    nc.scalar.copy(xnT[:, s, :], ps_a[s][:, 0:P]).then_inc(xT_ready, 1)

                def gelu(t, s):
                    act.wait_ge(hidden, t + 1)
                    wait(act, g_normed, t - 1)
                    nc.scalar.activation(g[:, s, :], ps_h[s][:, 0:H], ACT.Gelu).then_inc(gelu_done, 1)

                def copy_gT(t, s):
                    act.wait_ge(g_turned, t + 1)
                    wait(act, projected, t - 1)
                    nc.scalar.copy(gT[:, s, :], ps_t[s][:, 0:H]).then_inc(gT_ready, 1)

                pipeline(act, T, 2, [(copy_gT, 4), (gelu, 2), (copy_xT, 1)])


def expert_ffn(core, name, centroids, gamma, beta, W1, b1, W2, b2):
    nc, X = core.nc, core.X
    E, H = W1.shape[0], W1.shape[1]
    HC = H // P
    TC = S // P
    EXPAND, CONTRACT, ADD = E, E + 1, E + 2
    with ExitStack() as ctx:
        ctx.callback(core.release_semaphores)
        sb = lambda n, s, d=F32: ctx.enter_context(nc.sbuf_tensor(f"{name}_{n}", s, d))
        pb = lambda n, k=1: ctx.enter_context(nc.psum_tensor(f"{name}_{n}", [P, 512 * k], F32))
        sem = lambda n: core.semaphore(f"{name}_{n}")
        norm, norm2 = RowNorm(core, ctx, f"{name}_n", TC), RowNorm(core, ctx, f"{name}_m", TC)
        raw = sb("raw", [P, 2, H])
        w1T = sb("w1T", [P, E, H])
        w2T = sb("w2T", [P, E, HC, D])
        small = sb("small", [E, 3, D])
        cgb = sb("cgb", [P, 3, E])
        b1T = sb("b1T", [P, E, HC])
        b1_beta = sb("b1_beta", [P, E, HC])
        b2_row = sb("b2_row", [1, E, D])
        rank = sb("rank", [P, E])
        xn, xnT = sb("xn", [P, TC, D]), sb("xnT", [P, S])
        xn_add = sb("xn_add", [P, TC, D])
        h, hT = sb("h", [P, TC, D]), sb("hT", [P, S])
        scores, top = sb("scores", [P, TC, E]), sb("top", [P, TC])
        ranked, best = sb("ranked", [P, TC, E]), sb("best", [P, TC])
        alpha, coef_next, coef = sb("alpha", [P, TC]), sb("coef_next", [P, TC, E]), sb("coef", [P, TC, E])
        act_h = sb("act_h", [P, 2, HC, S])
        ps_x, ps_c = pb("ps_x"), pb("ps_c")
        ps_h = [pb(f"ps_h{i}") for i in range(4)]
        ps_y = [pb(f"ps_y{i}") for i in range(2)]
        loaded, prep, prep_pe, raw_in = sem("loaded"), sem("prep"), sem("prep_pe"), sem("raw_in")
        names = ("x_normed", "h_normed", "x_turned", "xnT_ready", "scored", "scores_done", "top_done", "ranked_done", "best_done", "alpha_done",
                 "sel_done", "coef_next_done", "coef_done", "h_turned", "hT_ready", "hidden", "relu_act", "relu_dve", "y_in", "added", "kept", "skip")
        sg = {n: sem(n) for n in names}

        with nc.Block() as block:
            @block.sync
            def _(sp):
                sp.dma_start(small[:, 0, :], centroids).then_inc(loaded, 16)
                sp.dma_start(small[:, 1, :], gamma).then_inc(loaded, 16)
                sp.dma_start(small[:, 2, :], beta).then_inc(loaded, 16)
                sp.dma_start(b2_row[:], b2.rearrange("(a e) d -> a e d", a=1)).then_inc(loaded, 16)
                with nc.allow_non_contiguous_dma(reason="small vectors"):
                    for e in range(E):
                        sp.dma_start(b1T[:, e, :], b1[e].rearrange("(c p) -> p c", p=P)).then_inc(loaded, 16)
                for k in range(2 * E):
                    if k >= 2:
                        sp.wait_ge(prep_pe, k - 1 + 1)
                    src = W1[k // 2].rearrange("(c p) d -> p c d", p=P) if k % 2 == 0 else W2[k // 2]
                    dst = raw[:, k % 2].rearrange("p (c d) -> p c d", c=HC) if k % 2 == 0 else raw[:, k % 2]
                    sp.dma_start(dst, src).then_inc(raw_in, 16)
                    sp.wait_ge(raw_in, 16 * (k + 1))

            @block.tensor
            def _(pe):
                pe.wait_ge(loaded, 16 * (4 + E))
                for k in range(3):
                    last = nc.tensor.transpose(ps_x[:, k * E:(k + 1) * E], small[:, k, :], core.ident[0:E, 0:E])
                last.then_inc(prep_pe, 1)
                for k in range(2 * E):
                    pe.wait_ge(raw_in, 16 * (k + 1))
                    if k >= 2:
                        pe.wait_ge(prep, 1 + k - 1)
                    for c in range(HC):
                        last = nc.tensor.transpose(ps_h[k % 2][:, c * P:(c + 1) * P], raw[:, k % 2, c * P:(c + 1) * P], core.ident[:])
                    last.then_inc(prep_pe, 1)
                pe.wait_ge(prep, 1 + 2 * E)
                for e in range(E):
                    for c in range(HC):
                        at = (e * HC + c) * E
                        last = nc.tensor.matmul(ps_y[0][:, at:at + E], w1T[:, e, c * P:(c + 1) * P], cgb[:, 2, :], start=True, stop=True)
                last.then_inc(prep_pe, 1)
                pe.wait_ge(prep, 1 + 2 * E + 2 * E)

                def body(item):
                    front, up, down = item(0), item(EXPAND), item(CONTRACT)
                    if front:
                        b, p = front[1], front[2]
                        if p == 4:
                            pe.wait_ge(sg["x_normed"], TC * (b + 1))
                            wait(pe, sg["hT_ready"], b)
                            for c in range(TC):
                                last = nc.tensor.transpose(ps_x[:, c * P:(c + 1) * P], xn[:, c, :], core.ident[:])
                            last.then_inc(sg["x_turned"], 1)
                        if p == 5:
                            pe.wait_ge(sg["xnT_ready"], b + 1)
                            wait(pe, sg["scores_done"], b)
                            for c in range(TC):
                                last = nc.tensor.matmul(ps_c[:, c * E:(c + 1) * E], xnT[:, c * P:(c + 1) * P], cgb[:, 0, :], start=True, stop=True)
                            last.then_inc(sg["scored"], 1)
                        if p == 7:
                            pe.wait_ge(sg["h_normed"], TC * (b + 1))
                            for c in range(TC):
                                last = nc.tensor.transpose(ps_x[:, c * P:(c + 1) * P], h[:, c, :], core.ident[:])
                            last.then_inc(sg["h_turned"], 1)
                    for c in range(HC):
                        if up:
                            n, b, e = up
                            if e == 0:
                                pe.wait_ge(sg["hT_ready"], b + 1)
                            wait(pe, sg["relu_dve" if c % 2 else "relu_act"], 2 * (n - 1) + c // 2 + 1)
                            nc.tensor.matmul(ps_h[c][:], w1T[:, e, c * P:(c + 1) * P], hT[:], start=True, stop=True).then_inc(sg["hidden"], 1)
                        if down:
                            n, b, e = down
                            if c == 0:
                                pe.wait_ge(sg["relu_act"], 2 * (n + 1))
                                pe.wait_ge(sg["relu_dve"], 2 * (n + 1))
                                wait(pe, sg["added"], TC * (n - 1))
                            at = slice(c * P, (c + 1) * P)
                            out = ps_y[e % 2][:, at]
                            nc.tensor.matmul(out, core.ones[0:1, :], b2_row[:, e, :], start=True, stop=False)
                            for k in range(HC):
                                last = nc.tensor.matmul(out, act_h[:, e % 2, k, at], w2T[:, e, k, :], start=False, stop=(k == HC - 1))
                            last.then_inc(sg["y_in"], 1)
                item_steps(pe, E, ADD, body)

            @block.scalar
            def _(act):
                def body(item):
                    front, up = item(0), item(EXPAND)
                    if front and front[2] == 4:
                        act.wait_ge(sg["x_turned"], front[1] + 1)
                        wait(act, sg["scored"], front[1])
                        nc.scalar.copy(xnT[:], ps_x[:]).then_inc(sg["xnT_ready"], 1)
                    if front and front[2] == 6:
                        act.wait_ge(sg["top_done"], front[1] + 1)
                        wait(act, sg["coef_next_done"], front[1])
                        nc.scalar.activation(alpha[:], top[:], ACT.Sigmoid).then_inc(sg["alpha_done"], 1)
                    if up:
                        n, b, e = up
                        if e == 0:
                            act.wait_ge(sg["h_turned"], b + 1)
                            wait(act, sg["hidden"], HC * n)
                            nc.scalar.copy(hT[:], ps_x[:]).then_inc(sg["hT_ready"], 1)
                        for c in (0, 2):
                            act.wait_ge(sg["hidden"], HC * n + c + 1)
                            wait(act, sg["y_in"], TC * (n - 1))
                            nc.scalar.activation(act_h[:, e % 2, c, :], ps_h[c][:], ACT.Relu, bias=b1_beta[:, e, c:c + 1]).then_inc(sg["relu_act"], 1)
                item_steps(act, E, ADD, body)

            @block.gpsimd
            def _(pool):
                def body(item):
                    front = item(0)
                    if front:
                        b, p = front[1], front[2]
                        if p == 0 or p == 2:
                            for c in range(TC):
                                (norm if p == 0 else norm2).rstd(pool, TC * b + c, c)
                item_steps(pool, E, ADD, body)

            @block.vector
            def _(dve):
                for e in range(E):
                    nc.vector.memset(rank[:, e:e + 1], float(E - e))
                dve.wait_ge(prep_pe, 1)
                nc.vector.tensor_copy(cgb[:].rearrange("p k e -> p (k e)"), ps_x[:, 0:3 * E]).then_inc(prep, 1)
                for k in range(2 * E):
                    dve.wait_ge(prep_pe, k + 2)
                    dst = w1T[:, k // 2, :] if k % 2 == 0 else w2T[:, k // 2].rearrange("p c d -> p (c d)")
                    nc.vector.tensor_copy(dst, ps_h[k % 2][:]).then_inc(prep, 1)
                dve.wait_ge(prep_pe, 2 + 2 * E)
                dve.wait_ge(prep, 1 + 2 * E)
                for e in range(E):
                    beta_part = ps_y[0][:, e * HC * E:(e + 1) * HC * E].rearrange("p (c f) -> p c f", f=E)[:, :, e]
                    nc.vector.tensor_tensor(b1_beta[:, e, :], beta_part, b1T[:, e, :], ALU.add).then_inc(prep, 1)
                    nc.vector.tensor_scalar(w1T[:, e, :], w1T[:, e, :], cgb[:, 1, e:e + 1], None, ALU.mult).then_inc(prep, 1)
                dve.wait_ge(prep, 1 + 4 * E)

                wide = lambda m: m.unsqueeze(2).broadcast_to([P, TC, E])

                def front_part(b, p):
                    for q, nrm in ((0, norm), (2, norm2)):
                        if p == q:
                            for c in range(TC):
                                if q == 2:
                                    dve.wait_ge(sg["x_normed"], TC * (b + 1))
                                nrm.stats(dve, TC * b + c, c, tile_of(X, TC * b + c) if q == 0 else xn[:, c, :])
                    if p == 1:
                        wait(dve, sg["x_turned"], b)
                        wait(dve, sg["skip"], b)
                        for c in range(TC):
                            dve.wait_ge(norm.rstd_done, TC * b + c + 1)
                            norm.apply(xn[:, c, :], tile_of(X, TC * b + c), c).then_inc(sg["x_normed"], 1)
                    if p == 3:
                        wait(dve, sg["h_turned"], b)
                        for c in range(TC):
                            dve.wait_ge(norm2.rstd_done, TC * b + c + 1)
                            norm2.apply(h[:, c, :], xn[:, c, :], c).then_inc(sg["h_normed"], 1)
                    if p == 6:
                        dve.wait_ge(sg["scored"], b + 1)
                        wait(dve, sg["coef_next_done"], b)
                        nc.vector.tensor_copy(scores[:].rearrange("p c e -> p (c e)"), ps_c[:, 0:TC * E]).then_inc(sg["scores_done"], 1)
                        dve.wait_ge(sg["scores_done"], b + 1)
                        nc.vector.tensor_reduce(top[:], scores[:], AX.X, ALU.max).then_inc(sg["top_done"], 1)
                        dve.wait_ge(sg["top_done"], b + 1)
                        nc.vector.tensor_tensor(ranked[:], scores[:], wide(top[:]), ALU.is_equal).then_inc(sg["ranked_done"], 1)
                        dve.wait_ge(sg["ranked_done"], 2 * b + 1)
                        nc.vector.tensor_tensor(ranked[:], ranked[:], rank[:].unsqueeze(1).broadcast_to([P, TC, E]), ALU.mult)\
                            .then_inc(sg["ranked_done"], 1)
                        dve.wait_ge(sg["ranked_done"], 2 * b + 2)
                        nc.vector.tensor_reduce(best[:], ranked[:], AX.X, ALU.max).then_inc(sg["best_done"], 1)
                        dve.wait_ge(sg["best_done"], b + 1)
                        wait(dve, sg["coef_done"], b)
                        nc.vector.tensor_tensor(coef_next[:], ranked[:], wide(best[:]), ALU.is_equal).then_inc(sg["sel_done"], 1)
                        dve.wait_ge(sg["sel_done"], b + 1)
                        dve.wait_ge(sg["alpha_done"], b + 1)
                        nc.vector.tensor_tensor(coef_next[:], coef_next[:], wide(alpha[:]), ALU.mult).then_inc(sg["coef_next_done"], 1)

                def body(item):
                    front, up, down, add = item(0), item(EXPAND), item(CONTRACT), item(ADD)
                    if down and down[2] == 0:
                        b = down[1]
                        xb = X[:, bass.ds(b * TC, TC), :]
                        nc.vector.tensor_tensor(xb, xb, xn[:], ALU.add).then_inc(sg["skip"], 1)
                    if front:
                        front_part(front[1], front[2])
                    if add and add[2] == 0:
                        b = add[1]
                        wait(dve, sg["added"], E * TC * b)
                        dve.wait_ge(sg["coef_next_done"], b + 1)
                        nc.vector.tensor_copy(coef[:], coef_next[:]).then_inc(sg["coef_done"], 1)
                        dve.wait_ge(sg["coef_done"], b + 1)
                        dve.wait_ge(sg["skip"], b + 1)
                    for c in range(HC):
                        if up and c % 2:
                            n, b, e = up
                            dve.wait_ge(sg["hidden"], HC * n + c + 1)
                            wait(dve, sg["y_in"], TC * (n - 1))
                            nc.vector.tensor_scalar(act_h[:, e % 2, c, :], ps_h[c][:], b1_beta[:, e, c:c + 1], 0.0, ALU.add, ALU.max)\
                                .then_inc(sg["relu_dve"], 1)
                        if add:
                            n, b, e = add
                            dve.wait_ge(sg["y_in"], TC * (n + 1))
                            wait(dve, sg["added"], TC * (n - 1) + c + 1)
                            xt = tile_of(X, b * TC + c)
                            nc.vector.scalar_tensor_tensor(xt, ps_y[e % 2][:, c * P:(c + 1) * P], coef[:, c, e:e + 1], xt, ALU.mult, ALU.add)\
                                .then_inc(sg["added"], 1)
                item_steps(dve, E, ADD, body)


def ssm_tables():
    p = np.arange(P)
    same = (p[:, None] // 16 == p[None, :] // 16).astype(np.float32)
    j, t = np.arange(16)[:, None], np.arange(16)[None, :]
    shift = (t[None] - (p % 16)[:, None, None] == j[None]).astype(np.float32)
    return same, shift.reshape(P, 256)


def channel_ssm(core, name, A, Bp, Cp, Dp, Wg, bg, gamma, beta, same_in, shift_in):
    nc, X = core.nc, core.X
    C = 16
    G, DG = 16, D // 16
    NCH = S // C
    LV = 5
    J = NB * NCH // P
    KM = LV + 3
    xg_dram = nc.dram_tensor(f"{name}_xg", (T * P, D), F32, kind="Internal").ap()
    y_dram = nc.dram_tensor(f"{name}_y", (T * P, D), F32, kind="Internal").ap()

    with ExitStack() as ctx:
        ctx.callback(core.release_semaphores)
        sb = lambda n, s, d=F32: ctx.enter_context(nc.sbuf_tensor(f"{name}_{n}", s, d))
        pb = lambda n: ctx.enter_context(nc.psum_tensor(f"{name}_{n}", [P, 512], F32))
        sem = lambda n: core.semaphore(f"{name}_{n}")
        norm = RowNorm(core, ctx, f"{name}_n1", 4)
        wg, wgT, bgr = sb("wg", [P, D]), sb("wgT", [P, D]), sb("bgr", [1, D])
        xn, xnT, gate, xg = sb("xn", [P, 4, D]), sb("xnT", [P, 2, P]), sb("gate", [P, 2, D]), sb("xgb", [P, 4, D])
        ps_t, ps_z = [pb(f"pt{i}") for i in range(2)], [pb(f"pz{i}") for i in range(2)]
        loaded, prep, x_normed, x_turned, xT_ready, gate_in, gated, product, stored = (
            sem(n) for n in ("loaded", "prep", "x_normed", "x_turned", "xT_ready", "gate_in", "gated", "product", "stored"))
        sent = [sem(f"sent{i}") for i in range(4)]
        with nc.Block() as block:
            @block.sync
            def _(sp):
                sp.dma_start(wg[:], Wg).then_inc(loaded, 16)
                sp.dma_start(bgr[:], bg.rearrange("(a d) -> a d", a=1)).then_inc(loaded, 16)
                rows = xg_dram.rearrange("(n p) d -> n p d", p=P)

                def send(t, s):
                    sp.wait_ge(product, t + 1)
                    sp.dma_start(rows[bass.ds(t, 1), :, :].rearrange("a p d -> (a p) d"), xg[:, s, :]).then_inc(sent[s], 16)
                pipeline(sp, T, 4, [(send, 4)])
                for s in range(4):
                    sp.wait_ge(sent[s], 16 * (T // 4))

            @block.vector
            def _(dve):
                dve.wait_ge(prep, 1)
                nc.vector.tensor_copy(wgT[:], ps_t[0][:, 0:D]).then_inc(prep, 1)
                dve.wait_ge(prep, 2)

                def stats(t, s):
                    wait(dve, x_normed, t - 3)
                    norm.stats(dve, t, s, tile_of(X, t))

                def norm_x(t, s):
                    dve.wait_ge(norm.rstd_done, t + 1)
                    wait(dve, product, t - 3)
                    norm.apply(xn[:, s, :], tile_of(X, t), s).then_inc(x_normed, 1)

                def multiply(t, s):
                    dve.wait_ge(gated, t + 1)
                    if isinstance(t, int) and t < 4:
                        pass
                    else:
                        dve.wait_ge(sent[s], (t - s) * 4)
                    nc.vector.tensor_tensor(xg[:, s, :], xn[:, s, :], gate[:, s % 2, :], ALU.mult).then_inc(product, 1)
                pipeline(dve, T, 4, [(multiply, 3), (norm_x, 1), (stats, 0)])

            @block.gpsimd
            def _(pool):
                pipeline(pool, T, 4, [(lambda t, s: norm.rstd(pool, t, s), 0)])

            @block.tensor
            def _(pe):
                pe.wait_ge(loaded, 32)
                nc.tensor.transpose(ps_t[0][:, 0:D], wg[:], core.ident[:]).then_inc(prep, 1)
                pe.wait_ge(prep, 2)

                def turn(t, s):
                    pe.wait_ge(x_normed, t + 1)
                    wait(pe, xT_ready, t - 1)
                    nc.tensor.transpose(ps_t[s % 2][:, 0:P], xn[:, s, :], core.ident[:]).then_inc(x_turned, 1)

                def gates(t, s):
                    pe.wait_ge(xT_ready, t + 1)
                    wait(pe, gated, t - 1)
                    nc.tensor.matmul(ps_z[s % 2][:, 0:D], core.ones[0:1, :], bgr[:], start=True, stop=False)
                    nc.tensor.matmul(ps_z[s % 2][:, 0:D], xnT[:, s % 2, :], wgT[:], start=False, stop=True).then_inc(gate_in, 1)
                pipeline(pe, T, 4, [(gates, 2), (turn, 1)])

            @block.scalar
            def _(act):
                def copy_xT(t, s):
                    act.wait_ge(x_turned, t + 1)
                    wait(act, gate_in, t - 1)
                    nc.scalar.copy(xnT[:, s % 2, :], ps_t[s % 2][:, 0:P]).then_inc(xT_ready, 1)

                def sigmoid(t, s):
                    act.wait_ge(gate_in, t + 1)
                    wait(act, product, t - 1)
                    nc.scalar.activation(gate[:, s % 2, :], ps_z[s % 2][:, 0:D], ACT.Sigmoid).then_inc(gated, 1)
                pipeline(act, T, 4, [(sigmoid, 2), (copy_xT, 1)])

    with ExitStack() as ctx:
        ctx.callback(core.release_semaphores)
        sb = lambda n, s, d=F32: ctx.enter_context(nc.sbuf_tensor(f"{name}_{n}", s, d))
        sem = lambda n: core.semaphore(f"{name}_r_{n}")
        mats = sb("mats", [P, G, KM, P])
        xc = sb("xc", [P, J, C, D])
        same, shift = sb("same", [P, P]), sb("shift", [P, C, C])
        TOEP, INTO, OUT = LV, LV + 1, LV + 2
        psum = [ctx.enter_context(nc.psum_tensor(f"{name}_b{i}", [P, 512], F32)) for i in range(8)]
        loaded, xc_loaded = sem("ld2"), sem("xc_loaded")
        with ExitStack() as c2:
            sb2 = lambda n, s, d=F32: c2.enter_context(nc.sbuf_tensor(f"{name}_{n}", s, d))
            a0, bp, cp, dp1 = sb2("a0", [P, G, C]), sb2("bp", [P, G]), sb2("cp", [P, G]), sb2("dp1", [P, G])
            pw = sb2("pw", [P, 2, G, P])
            pwT = sb2("pwT", [P, 2, G, P])
            aT = sb2("aT", [P, G, P])
            vb, wc, wc1 = sb2("vb", [P, G, C]), sb2("wc", [P, G, C]), sb2("wc1", [P, G, C])
            bw, taps = sb2("bw", [P, G, C]), sb2("taps", [P, G, C])
            t0, term = sb2("t0", [P, G, C]), sb2("term", [P, G, C])
            dve_step, pe_step = sem("dve_step"), sem("pe_step")
            with nc.Block() as block:
                @block.sync
                def _(sp):
                    with nc.allow_non_contiguous_dma(reason="small weights"):
                        for d in range(DG):
                            at = slice(d * C, (d + 1) * C)
                            sp.dma_start(a0[at, :, :], A.rearrange("(g d) n m -> d n g m", d=DG)[d]).then_inc(loaded, 16)
                            sp.dma_start(bp[at, :], Bp.rearrange("(g d) n -> d n g", d=DG)[d]).then_inc(loaded, 16)
                            sp.dma_start(cp[at, :], Cp.rearrange("(g d) n -> d n g", d=DG)[d]).then_inc(loaded, 16)
                            sp.dma_start(dp1[at, :], Dp.rearrange("(g d) -> d g", d=DG)[d:d + 1, :].broadcast_to([C, G])).then_inc(loaded, 16)
                        sp.dma_start(same[:], same_in).then_inc(loaded, 16)
                        sp.dma_start(shift[:].rearrange("p j t -> p (j t)"), shift_in).then_inc(loaded, 16)
                    chunks = xg_dram.rearrange("(j p c) d -> p j (c d)", p=P, c=C)
                    for j in range(J):
                        sp.dma_start(xc[:, j, :, :].rearrange("p c d -> p (c d)"), chunks[:, j, :]).then_inc(xc_loaded, 16)
                    sp.wait_ge(xc_loaded, 16 * J)

                def wide(m):
                    return m.unsqueeze(2).broadcast_to([P, G, DG, C])
                same_wide = same[:].rearrange("p (d c) -> p d c", d=DG).unsqueeze(1).broadcast_to([P, G, DG, C])

                @block.vector
                def _(dve):
                    n = [0]

                    def done(ins):
                        n[0] += 1
                        ins.then_inc(dve_step, 1)
                        dve.wait_ge(dve_step, n[0])

                    def expand(out, m):
                        for g0 in range(0, G, 4):
                            done(nc.vector.tensor_tensor(out[:, g0:g0 + 4, :].rearrange("p g (d c) -> p g d c", d=DG),
                                                         wide(m[:])[:, g0:g0 + 4], same_wide[:, g0:g0 + 4], ALU.mult))
                    rounds = [0]

                    def pe_done():
                        rounds[0] += 1
                        dve.wait_ge(pe_step, rounds[0])
                    dve.wait_ge(loaded, 16 * (4 * DG + 2))
                    expand(pw[:, 0], a0)
                    done(nc.vector.tensor_copy(vb[:, :, C - 1], bp[:]))
                    done(nc.vector.tensor_copy(wc[:, :, 0], cp[:]))
                    done(nc.vector.tensor_scalar(dp1[:], dp1[:], 1.0, None, ALU.add))
                    pe_done()
                    for q in range(4):
                        done(nc.vector.tensor_copy(aT[:, 4 * q:4 * q + 4, :].rearrange("p g c -> p (g c)"), psum[q][:]))
                    k, cur = 1, 0
                    for level in range(8):
                        pe_done()
                        nxt = 1 - cur
                        for q in range(4):
                            dst = pw[:, nxt] if level < 3 else mats[:, :, level - 3, :]
                            done(nc.vector.tensor_copy(dst[:, 4 * q:4 * q + 4, :], psum[q][:].rearrange("p (g c) -> p g c", g=4)))
                        pe_done()
                        for q in range(4):
                            done(nc.vector.tensor_copy(pwT[:, nxt, 4 * q:4 * q + 4, :], psum[4 + q][:].rearrange("p (g c) -> p g c", g=4)))
                        if k < C:
                            pe_done()
                            done(nc.vector.tensor_copy(vb[:, :, C - 2 * k:C - k], psum[0][:, 0:G * k].rearrange("p (g c) -> p g c", g=G)))
                            done(nc.vector.tensor_copy(wc[:, :, k:2 * k], psum[1][:, 0:G * k].rearrange("p (g c) -> p g c", g=G)))
                        k, cur = 2 * k, nxt
                    pe_done()
                    done(nc.vector.tensor_copy(wc1[:], psum[0][:, 0:G * C].rearrange("p (g c) -> p g c", g=G)))
                    done(nc.vector.tensor_tensor(bw[:], wc[:], bp[:].unsqueeze(2).broadcast_to([P, G, C]), ALU.mult))
                    pe_done()
                    done(nc.vector.tensor_copy(taps[:], psum[1][:, 0:G * C].rearrange("p (g c) -> p g c", g=G)))
                    for j in range(C):
                        tap = taps[:, :, j:j + 1].broadcast_to([P, G, C])
                        sh = shift[:, j:j + 1, :].broadcast_to([P, G, C])
                        done(nc.vector.tensor_tensor(t0[:] if j == 0 else term[:], tap, sh, ALU.mult))
                        if j:
                            done(nc.vector.tensor_tensor(t0[:], t0[:], term[:], ALU.add))
                    expand(mats[:, :, TOEP, :], t0)
                    for g in range(G):
                        done(nc.vector.scalar_tensor_tensor(mats[:, g, TOEP, :], core.ident[:], dp1[:, g:g + 1], mats[:, g, TOEP, :],
                                                            ALU.mult, ALU.add))
                    expand(mats[:, :, OUT, :], wc1)
                    expand(pw[:, 0], vb)
                    pe_done()
                    for q in range(4):
                        done(nc.vector.tensor_copy(mats[:, 4 * q:4 * q + 4, INTO, :], psum[q][:].rearrange("p (g c) -> p g c", g=4)))

                @block.tensor
                def _(pe):
                    n = [0]

                    def need(k):
                        n[0] += k
                        pe.wait_ge(dve_step, n[0])
                    need(7)
                    for g in range(G):
                        last = nc.tensor.transpose(psum[g // 4][:, g % 4 * P:g % 4 * P + P], pw[:, 0, g, :], core.ident[:])
                    last.then_inc(pe_step, 1)
                    need(4)
                    k, cur = 1, 0
                    for level in range(8):
                        now = pw[:, cur] if level < 4 else mats[:, :, level - 4, :]
                        nowT = pwT[:, cur] if level else aT[:]
                        for g in range(G):
                            last = nc.tensor.matmul(psum[g // 4][:, g % 4 * P:g % 4 * P + P], nowT[:, g, :], now[:, g, :], start=True, stop=True)
                        last.then_inc(pe_step, 1)
                        for g in range(G):
                            last = nc.tensor.matmul(psum[4 + g // 4][:, g % 4 * P:g % 4 * P + P], now[:, g, :], nowT[:, g, :], start=True, stop=True)
                        last.then_inc(pe_step, 1)
                        need(8)
                        if k < C:
                            for g in range(G):
                                nc.tensor.matmul(psum[0][:, g * k:(g + 1) * k], now[:, g, :], vb[:, g, C - k:C], start=True, stop=True)
                            for g in range(G):
                                last = nc.tensor.matmul(psum[1][:, g * k:(g + 1) * k], nowT[:, g, :], wc[:, g, 0:k], start=True, stop=True)
                            last.then_inc(pe_step, 1)
                            need(2)
                        k, cur = 2 * k, 1 - cur
                    for g in range(G):
                        last = nc.tensor.matmul(psum[0][:, g * C:(g + 1) * C], aT[:, g, :], wc[:, g, :], start=True, stop=True)
                    last.then_inc(pe_step, 1)
                    need(2)
                    nc.tensor.matmul(psum[1][:, 0:G * C], same[:], bw[:].rearrange("p g c -> p (g c)"), start=True, stop=True).then_inc(pe_step, 1)
                    need(1 + 1 + 2 * (C - 1) + 4 + G + 4 + 4)
                    for g in range(G):
                        last = nc.tensor.transpose(psum[g // 4][:, g % 4 * P:g % 4 * P + P], pw[:, 0, g, :], core.ident[:])
                    last.then_inc(pe_step, 1)

        with ExitStack() as c2:
            sb2 = lambda n, s, d=F32: c2.enter_context(nc.sbuf_tensor(f"{name}_{n}", s, d))
            cur = sb2("cur", [P, 2, 2, KM, P])
            xin = sb2("xin", [P, 2, 2, J, P])
            xT = sb2("xT", [P, 2, 2, J * P])
            u = sb2("u", [P, 2, J * P])
            y = sb2("yout", [P, 2, J * P])
            ps_x, ps_u, ps_y, ps_z = psum[0:2], psum[2:4], psum[4:6], psum[6:8]
            staged, turned, xT_ready, state_in, state_out, y_in, y_out, z_in, z_out, first = (
                sem(n) for n in ("staged", "turned", "xT_ready", "state_in", "state_out", "y_in", "y_out", "z_in", "z_out", "first"))
            state_out = [sem("state_out_a"), sem("state_out_b")]
            y_out = [sem("y_out_a"), sem("y_out_b")]
            z_out = [sem("z_out_a"), sem("z_out_b")]
            PAIRS = G // 2
            with nc.Block() as block:
                @block.gpsimd
                def _(pool):
                    def stage(i, s):
                        wait(pool, z_in, 2 * (i - 1))
                        nc.gpsimd.tensor_copy(cur[:, s].rearrange("p h k c -> p (h k c)"),
                                              mats[:, bass.ds(i * 2, 2), :, :].rearrange("p h k c -> p (h k c)")).then_inc(staged, 1)
                        for h in range(2):
                            chans = xc[:, :, :, bass.ds(i * 2 * DG + h * DG, DG)].rearrange("p j c d -> p j d c")
                            nc.gpsimd.tensor_copy(xin[:, s, h, :, :].rearrange("p j (d c) -> p j d c", d=DG), chans).then_inc(staged, 1)
                    pipeline(pool, PAIRS, 2, [(stage, 0)])

                @block.tensor
                def _(pe):
                    def turn(i, s):
                        pe.wait_ge(staged, 3 * (i + 1))
                        wait(pe, xT_ready, i)
                        for h in range(2):
                            for j in range(J):
                                last = nc.tensor.transpose(ps_x[h][:, j * P:(j + 1) * P], xin[:, s, h, j, :], core.ident[:])
                        last.then_inc(turned, 1)

                    def recur(i, s):
                        pe.wait_ge(xT_ready, i + 1)
                        for h in range(2):
                            wait(pe, state_out[h], (LV + 1) * i)
                            nc.tensor.matmul(ps_u[h][:], cur[:, s, h, INTO, :], xT[:, s, h, :], start=True, stop=False,
                                             skip_group_check=True).then_inc(state_in, 1)
                        for l in range(LV):
                            for h in range(2):
                                pe.wait_ge(state_out[h], (LV + 1) * i + l + 1)
                                ub = u[:, h, :].rearrange("p (b c) -> p b c", c=NCH)
                                pb_ = ps_u[h][:].rearrange("p (b c) -> p b c", c=NCH)
                                nc.tensor.matmul(pb_[:, :, 2 ** l:], cur[:, s, h, l, :], ub[:, :, 0:NCH - 2 ** l], start=False, stop=(l == LV - 1),
                                                 skip_group_check=True).then_inc(state_in, 1)
                        for h in range(2):
                            wait(pe, y_out[h], i)
                            nc.tensor.matmul(ps_y[h][:], cur[:, s, h, TOEP, :], xT[:, s, h, :], start=True, stop=False, skip_group_check=True)
                            pe.wait_ge(state_out[h], (LV + 1) * (i + 1))
                            ub = u[:, h, :].rearrange("p (b c) -> p b c", c=NCH)
                            yb = ps_y[h][:].rearrange("p (b c) -> p b c", c=NCH)
                            nc.tensor.matmul(yb[:, :, 1:], cur[:, s, h, OUT, :], ub[:, :, 0:NCH - 1], start=False, stop=True,
                                             skip_group_check=True).then_inc(y_in, 1)
                        for h in range(2):
                            pe.wait_ge(y_out[h], i + 1)
                            wait(pe, z_out[h], i)
                            for j in range(J):
                                last = nc.tensor.transpose(ps_z[h][:, j * P:(j + 1) * P], y[:, h, j * P:(j + 1) * P], core.ident[:])
                            last.then_inc(z_in, 1)
                    pipeline(pe, PAIRS, 2, [(recur, 1), (turn, 0)])

                def drain_half(eng, op, h):
                    def front(i, s):
                        eng.wait_ge(turned, i + 1)
                        wait(eng, z_in, 2 * (i - 1))
                        op(xT[:, s, h, :], ps_x[h][:]).then_inc(half_x[h], 1)
                        if h == 0:
                            eng.wait_ge(half_x[1], i + 1)
                            eng.wait_ge(half_x[0], i + 1)
                            eng.sem_inc(xT_ready, 1)

                    def rest(i, s):
                        for l in range(LV + 1):
                            eng.wait_ge(state_in, 2 * (LV + 1) * i + 2 * l + h + 1)
                            if l == 0:
                                wait(eng, y_in, 2 * i)
                            op(u[:, h, :], ps_u[h][:]).then_inc(state_out[h], 1)
                        eng.wait_ge(y_in, 2 * i + h + 1)
                        wait(eng, z_in, 2 * i)
                        op(y[:, h, :], ps_y[h][:]).then_inc(y_out[h], 1)
                        eng.wait_ge(z_in, 2 * i + h + 1)
                        out = xc[:, :, :, bass.ds(i * 2 * DG + h * DG, DG)].rearrange("p j c d -> p j d c")
                        op(out, ps_z[h][:].rearrange("p (j d c) -> p j d c", j=J, d=DG)).then_inc(z_out[h], 1)
                    pipeline(eng, PAIRS, 2, [(rest, 1), (front, 0)])
                half_x = [sem("half_xa"), sem("half_xb")]

                @block.scalar
                def _(act):
                    drain_half(act, nc.scalar.copy, 0)

                @block.vector
                def _(dve):
                    drain_half(dve, nc.vector.tensor_copy, 1)

        y_stored = sem("y_stored")
        with nc.Block() as block:
            @block.sync
            def _(sp):
                chunks = y_dram.rearrange("(j p c) d -> p j (c d)", p=P, c=C)
                for j in range(J):
                    sp.dma_start(chunks[:, j, :], xc[:, j, :, :].rearrange("p c d -> p (c d)")).then_inc(y_stored, 16)
                sp.wait_ge(y_stored, 16 * J)

    with ExitStack() as ctx:
        ctx.callback(core.release_semaphores)
        sb = lambda n, s, d=F32: ctx.enter_context(nc.sbuf_tensor(f"{name}_{n}", s, d))
        sem = lambda n: core.semaphore(f"{name}_y_{n}")
        norm = RowNorm(core, ctx, f"{name}_n3", 4)
        yn = sb("yn", [P, T, D])
        gam, bet = sb("gam", [P, D]), sb("bet", [P, D])
        scaled, shifted = sb("scaled", [P, 4, D]), sb("shifted", [P, 4, D])
        loaded, normed, scaled_done, shifted_done, added = (
            sem(n) for n in ("ld3", "normed3", "scaled3", "shifted3", "added3"))
        arrived = [sem(f"yn{q}") for q in range(4)]
        with nc.Block() as block:
            @block.sync
            def _(sp):
                sp.dma_start(gam[:], gamma.rearrange("(a d) -> a d", a=1).broadcast_to([P, D])).then_inc(loaded, 16)
                sp.dma_start(bet[:], beta.rearrange("(a d) -> a d", a=1).broadcast_to([P, D])).then_inc(loaded, 16)
                rows = y_dram.rearrange("(n p) d -> p n d", p=P)
                for q in range(4):
                    sp.dma_start(yn[:, q * 16:(q + 1) * 16, :], rows[:, q * 16:(q + 1) * 16, :]).then_inc(arrived[q], 16)

            @block.vector
            def _(dve):
                for q in range(4):
                    dve.wait_ge(arrived[q], 16)

                def stats(t, s):
                    wait(dve, normed, t - 3)
                    norm.stats(dve, t, s, tile_of(yn, t))

                def apply(t, s):
                    dve.wait_ge(norm.rstd_done, t + 1)
                    norm.apply(tile_of(yn, t), tile_of(yn, t), s).then_inc(normed, 1)

                def add(t, s):
                    dve.wait_ge(shifted_done, t + 1)
                    nc.vector.tensor_tensor(tile_of(X, t), tile_of(X, t), shifted[:, s, :], ALU.add).then_inc(added, 1)
                pipeline(dve, T, 4, [(add, 3), (apply, 1), (stats, 0)])

            @block.gpsimd
            def _(pool):
                pool.wait_ge(loaded, 32)

                def scale(t, s):
                    pool.wait_ge(normed, t + 1)
                    wait(pool, shifted_done, t - 3)
                    nc.gpsimd.tensor_tensor(scaled[:, s, :], tile_of(yn, t), gam[:], ALU.mult).then_inc(scaled_done, 1)

                def shift_(t, s):
                    pool.wait_ge(scaled_done, t + 1)
                    wait(pool, added, t - 3)
                    nc.gpsimd.tensor_tensor(shifted[:, s, :], scaled[:, s, :], bet[:], ALU.add).then_inc(shifted_done, 1)
                pipeline(pool, T, 4, [(shift_, 2), (scale, 1), (lambda t, s: norm.rstd(pool, t, s), 0)])


def slot_tables():
    p = np.arange(P)
    part = (p[:, None] // 32 == np.arange(4)[None, :]).astype(np.float32)
    causal = ((p[:, None] // 32 == p[None, :] // 32) & (p[None, :] >= p[:, None])).astype(np.float32)
    go_on = np.tile((np.arange(S) % 32 != 0).astype(np.float32), (P, 1))
    return part, causal, go_on


def gated_slots(core, name, Wq, Wk, Wv, Wf, g_w, Wo, part_in, causal_in, go_on_in):
    nc, X = core.nc, core.X
    H, K = 4, 32
    BL = 32
    NBK = S // BL
    TC = S // P
    NORM = 1.0 / 8.0
    LIMIT = 80.0 / NORM
    with ExitStack() as ctx:
        ctx.callback(core.release_semaphores)
        sb = lambda n, s, d=F32: ctx.enter_context(nc.sbuf_tensor(f"{name}_{n}", s, d))
        pb = lambda n, k=1: ctx.enter_context(nc.psum_tensor(f"{name}_{n}", [P, 512 * k], F32))
        sem = lambda n: core.semaphore(f"{name}_{n}")
        norm = RowNorm(core, ctx, f"{name}_n", 4)
        w_raw, wT = sb("w_raw", [P, 5, D]), sb("wT", [P, 5, D])
        gw = sb("gw", [P, 1])
        part, causal, go_on = sb("part", [P, 4]), sb("causal", [P, P]), sb("go_on", [P, S])
        xn, xT = sb("xn", [P, TC, D]), sb("xT", [P, S])
        e, r = sb("e", [P, 3 * S]), sb("r", [P, 3 * S])
        qkvT = sb("qkvT", [P, 2, 3, S])
        za, ze, zl = sb("za", [P, S]), sb("ze", [P, S]), sb("zl", [P, S])
        f, gs = sb("f", [P, S]), sb("gs", [P, S])
        dk, dq, ek, ef, sT = sb("dk", [P, S]), sb("dq", [P, S]), sb("ek", [P, S]), sb("ef", [P, S]), sb("sT", [P, S])
        eqT = sb("eqT", [P, 2, S])
        bT = sb("bT", [P, 2, S])
        e_mid, e_last = sb("e_mid", [P, 2, NBK]), sb("e_last", [P, 2, NBK])
        decay = sb("decay", [P, 2, K, NBK])
        bn, eqn = sb("bn", [P, 2, S]), sb("eqn", [P, 2, S])
        kn, vn = sb("kn", [P, S]), sb("vn", [P, 2, S])
        kx, vx = sb("kx", [P, TC, H, 4, K]), sb("vx", [P, TC, H, 4, K])
        qm = sb("qm", [P, H, S])
        am_all = sb("am_all", [P, TC, H, P])
        ds, send = sb("ds", [P, K, NBK]), sb("send", [P, K, NBK])
        s1, s1T = sb("s1", [P, NBK, K]), sb("s1T", [P, NBK, K])
        sbd = sb("sbd", [P, NBK, H, K])
        ok, mx, ex, sm_, rc, qv = sb("ok", [P, S]), sb("mx", [P, TC * H]), sb("ex", [P, S]), sb("sum", [P, TC * H]), sb("rc", [P, TC * H]), sb("qv", [P, S])
        q2T, q2m = sb("q2T", [P, S]), sb("q2m", [P, H, S])
        ds2, send2, s2, sbd2 = sb("ds2", [P, K, NBK]), sb("send2", [P, K, NBK]), sb("s2", [P, NBK, K]), sb("sbd2", [P, NBK, H, K])
        eo, ro, o, osq, ss, var, rs, on, onT = (sb("eo", [P, S]), sb("ro", [P, S]), sb("o", [P, S]), sb("osq", [P, TC, P]), sb("ss", [P, TC]),
                                                sb("var", [P, TC]), sb("rs", [P, TC]), sb("on", [P, S]), sb("onT", [P, S]))
        ps_q = pb("ps_q", 3)
        ps_z, ps_t, ps_a, ps_s, ps_o = pb("ps_z"), pb("ps_t"), pb("ps_a"), pb("ps_s"), pb("ps_o")
        loaded, prep = sem("loaded"), sem("prep")
        names = ("x_normed", "x_turned", "xT_ready", "qkv_in", "z_in", "e_done", "e1_done", "r_done", "silu_done", "abs_done", "ze_done",
                 "log_done", "f_done", "g_done", "dk_done", "d_done", "exp_done", "s_done", "bT_done", "turned", "copied",
                 "decay_done", "kx_done", "vx_done", "qm_done", "a_in", "am_done", "s_in", "ds_done", "send_done", "s1_done",
                 "s1T_done", "sbd_done", "ok_in", "ok_done", "mx_done", "sub_done", "ex_done", "sum_done", "rc_done", "qv_done",
                 "qv_turned", "q2_done", "q2m_done", "a2_in", "am2_done", "s2_in", "ds2_done", "send2_done", "s2_done", "sbd2_done",
                 "ov_in", "eo_done", "eo1_done", "ro_done", "o_done", "ss_done", "var_done", "rs_done", "on_done", "on_turned",
                 "onT_ready", "y_in", "added")
        sg = {n: sem(n) for n in names}

        def blocks(m):
            return m.rearrange("p (j t) -> p j t", t=BL)

        with nc.Block() as block:
            @block.sync
            def _(sp):
                for n, w in enumerate((Wq, Wk, Wv, Wf, Wo)):
                    sp.dma_start(w_raw[:, n, :], w).then_inc(loaded, 16)
                with nc.allow_non_contiguous_dma(reason="small vector"):
                    sp.dma_start(gw[:], g_w.rearrange("(p a) -> p a", a=1)).then_inc(loaded, 16)
                sp.dma_start(part[:], part_in).then_inc(loaded, 16)
                sp.dma_start(causal[:], causal_in).then_inc(loaded, 16)
                sp.dma_start(go_on[:], go_on_in).then_inc(loaded, 16)

            @block.tensor
            def _(pe):
                pe.wait_ge(loaded, 144)
                for n in range(5):
                    last = nc.tensor.transpose((ps_a if n < 4 else ps_t)[:, n % 4 * P:n % 4 * P + P], w_raw[:, n, :], core.ident[:])
                last.then_inc(prep, 1)
                pe.wait_ge(prep, 5)

                def turn_x(i, s):
                    pe.wait_ge(sg["x_normed"], TC * (i + 1))
                    wait(pe, sg["f_done"], i)
                    for c in range(TC):
                        last = nc.tensor.transpose(ps_z[:, c * P:(c + 1) * P], xn[:, c, :], core.ident[:])
                    last.then_inc(sg["x_turned"], 1)

                def project(i, s):
                    pe.wait_ge(sg["xT_ready"], i + 1)
                    wait(pe, sg["silu_done"], i)
                    nc.tensor.matmul(ps_z[:], wT[:, 3, :], xT[:], start=True, stop=True).then_inc(sg["z_in"], 1)
                    for n in range(3):
                        last = nc.tensor.matmul(ps_q[:, n * S:(n + 1) * S], wT[:, n, :], xT[:], start=True, stop=True)
                    last.then_inc(sg["qkv_in"], 1)

                def turn(i, s, k, src, need):
                    pe.wait_ge(sg[need], i + 1)
                    wait(pe, sg["copied"], 4 * i + k)
                    for c in range(TC):
                        last = nc.tensor.transpose(ps_t[:, c * P:(c + 1) * P], src[:, c * P:(c + 1) * P], core.ident[:])
                    last.then_inc(sg["turned"], 1)

                def turns(i, s):
                    turn(i, s, 0, qkvT[:, s, 1], "silu_done")
                    turn(i, s, 1, qkvT[:, s, 2], "silu_done")
                    turn(i, s, 2, bT[:, s], "bT_done")
                    turn(i, s, 3, eqT[:, s], "exp_done")
                    pe.wait_ge(sg["copied"], 4 * i + 4)

                def scores(i, s, lhs, rhs, mask_done, signal):
                    for c in range(TC):
                        wait(pe, sg[mask_done], TC * i + c)
                        nc.tensor.matmul(ps_a[:].rearrange("p (h t) -> p h t", h=H), lhs[:, c * P:(c + 1) * P], rhs[:, :, c * P:(c + 1) * P],
                                         start=True, stop=True).then_inc(sg[signal], 1)
                        yield c

                def add_states(c, s, x):
                    for h in range(H):
                        last = nc.tensor.matmul(ps_s[h * K:(h + 1) * K, c * P:(c + 1) * P], bn[:, s, c * P + h * K:c * P + (h + 1) * K],
                                                x[:, c, h].rearrange("p j k -> p (j k)"), start=True, stop=True)
                    return last

                def outputs(i, s, q, states, a, rhs, mask_done):
                    for c in range(TC):
                        for j in range(4):
                            at = c * P + j * BL
                            nc.tensor.matmul(ps_o[j * BL:(j + 1) * BL, c * P:(c + 1) * P], q[:, at:at + BL],
                                             states[:, c * 4 + j].rearrange("p h k -> p (h k)"), start=True, stop=False, skip_group_check=True)
                        for h in range(H):
                            at = c * P + h * K
                            last = nc.tensor.matmul(ps_o[:, at:at + K], a[:, c, h, :], rhs[:, at:at + K],
                                                    start=False, stop=(h == H - 1), skip_group_check=True)
                    return last

                def step1(i, s):
                    pe.wait_ge(sg["kx_done"], i + 1)
                    wait(pe, sg["ds2_done"], i)
                    for c in range(TC):
                        last = add_states(c, s, kx)
                    last.then_inc(sg["s_in"], 1)

                def scores1(i, s):
                    pe.wait_ge(sg["qm_done"], i + 1)
                    for c in scores(i, s, qkvT[:, s, 1], qm, "am_done", "a_in"):
                        pass

                def out1(i, s):
                    pe.wait_ge(sg["am_done"], TC * (i + 1))
                    pe.wait_ge(sg["sbd_done"], i + 1)
                    wait(pe, sg["added"], i)
                    outputs(i, s, qkvT[:, s, 0], sbd, am_all, bn[:, s], None).then_inc(sg["ok_in"], 1)

                def turn_qv(i, s):
                    pe.wait_ge(sg["qv_done"], i + 1)
                    for c in range(TC):
                        last = nc.tensor.transpose(ps_t[:, c * P:(c + 1) * P], qv[:, c * P:(c + 1) * P], core.ident[:])
                    last.then_inc(sg["qv_turned"], 1)

                def step2(i, s):
                    pe.wait_ge(sg["vx_done"], i + 1)
                    pe.wait_ge(sg["ds_done"], i + 1)
                    for c in range(TC):
                        last = add_states(c, s, vx)
                    last.then_inc(sg["s2_in"], 1)

                def scores2(i, s):
                    pe.wait_ge(sg["q2m_done"], i + 1)
                    pe.wait_ge(sg["am_done"], TC * (i + 1))
                    for c in scores(i, s, bT[:, s], q2m, "am2_done", "a2_in"):
                        pass

                def out2(i, s):
                    pe.wait_ge(sg["am2_done"], TC * (i + 1))
                    pe.wait_ge(sg["sbd2_done"], i + 1)
                    pe.wait_ge(sg["ok_done"], i + 1)
                    outputs(i, s, q2T, sbd2, am_all, vn[:, s], None).then_inc(sg["ov_in"], 1)

                def turn_o(i, s):
                    pe.wait_ge(sg["on_done"], TC * (i + 1))
                    for c in range(TC):
                        last = nc.tensor.transpose(ps_t[:, c * P:(c + 1) * P], on[:, c * P:(c + 1) * P], core.ident[:])
                    last.then_inc(sg["on_turned"], 1)

                def project_o(i, s):
                    pe.wait_ge(sg["onT_ready"], i + 1)
                    for c in range(TC):
                        last = nc.tensor.matmul(ps_o[:, c * P:(c + 1) * P], onT[:, c * P:(c + 1) * P], wT[:, 4, :], start=True, stop=True)
                    last.then_inc(sg["y_in"], 1)

                def attend(i, s):
                    step1(i, s)
                    step2(i, s)
                    scores1(i, s)
                    out1(i, s)
                    turn_qv(i, s)
                    scores2(i, s)
                    out2(i, s)
                    turn_o(i, s)
                    project_o(i, s)
                pipeline(pe, NB, 2, [(attend, 1), (turn_x, 0), (project, 0), (turns, 0)])

            @block.scalar
            def _(act):
                def front(i, s):
                    act.wait_ge(sg["x_turned"], i + 1)
                    nc.scalar.copy(xT[:], ps_z[:]).then_inc(sg["xT_ready"], 1)
                    act.wait_ge(sg["z_in"], i + 1)
                    wait(act, sg["f_done"], i)
                    nc.scalar.activation(za[:], ps_z[:], ACT.Abs).then_inc(sg["abs_done"], 1)
                    act.wait_ge(sg["qkv_in"], i + 1)
                    wait(act, sg["r_done"], i)
                    nc.scalar.activation(e[:], ps_q[:], ACT.Exp, scale=-1.0).then_inc(sg["e_done"], 1)
                    act.wait_ge(sg["abs_done"], i + 1)
                    nc.scalar.activation(ze[:], za[:], ACT.Exp, scale=-1.0).then_inc(sg["ze_done"], 1)
                    act.wait_ge(sg["ze_done"], i + 1)
                    nc.scalar.activation(zl[:], ze[:], ACT.Ln, bias=core.ones[:, 0:1]).then_inc(sg["log_done"], 1)

                def exps(i, s):
                    act.wait_ge(sg["g_done"], i + 1)
                    wait(act, sg["bT_done"], i)
                    wait(act, sg["added"], i - 1)
                    nc.scalar.activation(ef[:], f[:], ACT.Exp, scale=NORM)
                    nc.scalar.activation(e_mid[:, s, :], blocks(gs[:])[:, :, BL // 2 - 1], ACT.Exp, scale=NORM)
                    nc.scalar.activation(e_last[:, s, :], blocks(gs[:])[:, :, BL - 1], ACT.Exp, scale=NORM)
                    act.wait_ge(sg["d_done"], i + 1)
                    nc.scalar.activation(ek[:], dk[:], ACT.Exp, scale=NORM)
                    nc.scalar.activation(eqT[:, s], dq[:], ACT.Exp, scale=NORM).then_inc(sg["exp_done"], 1)

                def copies(i, s):
                    for k, dst in enumerate((kn[:], vn[:, s], bn[:, s], eqn[:, s])):
                        act.wait_ge(sg["turned"], 4 * i + k + 1)
                        if k == 0:
                            wait(act, sg["kx_done"], i)
                        nc.scalar.copy(dst, ps_t[:]).then_inc(sg["copied"], 1)

                def softmax_exp(i, s):
                    act.wait_ge(sg["sub_done"], i + 1)
                    nc.scalar.activation(ex[:], ok[:], ACT.Exp).then_inc(sg["ex_done"], 1)

                def silu_exp(i, s):
                    act.wait_ge(sg["ov_in"], i + 1)
                    nc.scalar.activation(eo[:], ps_o[:], ACT.Exp, scale=-1.0).then_inc(sg["eo_done"], 1)

                def copy_onT(i, s):
                    act.wait_ge(sg["on_turned"], i + 1)
                    nc.scalar.copy(onT[:], ps_t[:]).then_inc(sg["onT_ready"], 1)

                def back(i, s):
                    softmax_exp(i, s)
                    silu_exp(i, s)
                    copy_onT(i, s)
                pipeline(act, NB, 2, [(back, 1), (front, 0), (exps, 0), (copies, 0)])

            @block.gpsimd
            def _(pool):
                def rstds(i, s):
                    for c in range(TC):
                        norm.rstd(pool, i * TC + c, c)

                def front(i, s):
                    pool.wait_ge(sg["e_done"], i + 1)
                    nc.gpsimd.tensor_tensor(e[:], e[:], core.ones[:, 0:1].broadcast_to([P, 3 * S]), ALU.add).then_inc(sg["e1_done"], 1)

                def expands(i, s):
                    pool.wait_ge(sg["silu_done"], i + 1)
                    wait(pool, sg["a_in"], TC * i)
                    nc.gpsimd.tensor_tensor(qm[:], qkvT[:, s, 0, :].unsqueeze(1).broadcast_to([P, H, S]),
                                            part[:].unsqueeze(2).broadcast_to([P, H, S]), ALU.mult).then_inc(sg["qm_done"], 1)
                    pool.wait_ge(sg["exp_done"], i + 1)
                    nc.gpsimd.tensor_tensor(decay[:, s], e_last[:, s, :].unsqueeze(1).broadcast_to([P, K, NBK]),
                                            blocks(go_on[:])[:, 0:1, 0:NBK].broadcast_to([P, K, NBK]), ALU.mult).then_inc(sg["decay_done"], 1)
                    for k, (x, src, signal) in enumerate(((kx, kn[:], "kx_done"), (vx, vn[:, s], "vx_done"))):
                        wait(pool, sg["s_in" if k == 0 else "s2_in"], i)
                        pool.wait_ge(sg["copied"], 4 * i + k + 1)
                        for c in range(TC):
                            rows = src[:, c * P:(c + 1) * P].rearrange("p (h k) -> p h k", h=H)
                            last = nc.gpsimd.tensor_tensor(x[:, c], rows.unsqueeze(2).broadcast_to([P, H, 4, K]),
                                                           part[:].unsqueeze(1).unsqueeze(3).broadcast_to([P, H, 4, K]), ALU.mult)
                        last.then_inc(sg[signal], 1)

                def spread(out, states):
                    for q in range(4):
                        at = slice(q * 4, q * 4 + 4)
                        last = nc.gpsimd.tensor_tensor(out[:, at], states[:, at, :].unsqueeze(2).broadcast_to([P, 4, H, K]),
                                                       part[:].unsqueeze(1).unsqueeze(3).broadcast_to([P, 4, H, K]), ALU.mult)
                    return last

                def back(i, s):
                    pool.wait_ge(sg["s1T_done"], i + 1)
                    spread(sbd, s1T).then_inc(sg["sbd_done"], 1)
                    pool.wait_ge(sg["s2_done"], i + 1)
                    spread(sbd2, s2).then_inc(sg["sbd2_done"], 1)
                    pool.wait_ge(sg["q2_done"], i + 1)
                    nc.gpsimd.tensor_tensor(q2m[:], q2T[:].unsqueeze(1).broadcast_to([P, H, S]),
                                            part[:].unsqueeze(2).broadcast_to([P, H, S]), ALU.mult).then_inc(sg["q2m_done"], 1)
                    pool.wait_ge(sg["eo_done"], i + 1)
                    nc.gpsimd.tensor_tensor(eo[:], eo[:], core.ones[:, 0:1].broadcast_to([P, S]), ALU.add).then_inc(sg["eo1_done"], 1)
                    pool.wait_ge(sg["var_done"], i + 1)
                    nc.gpsimd.tensor_tensor(rs[:], var[:], core.minus_half[:, 0:TC], ALU.pow).then_inc(sg["rs_done"], 1)
                pipeline(pool, NB, 2, [(back, 1), (rstds, 0), (front, 0), (expands, 0)])

            @block.vector
            def _(dve):
                dve.wait_ge(loaded, 144)
                nc.vector.memset(s1[:], 0.0).then_inc(prep, 1)
                nc.vector.memset(s2[:], 0.0).then_inc(prep, 1)
                dve.wait_ge(prep, 3)
                nc.vector.tensor_copy(wT[:, 0:4, :].rearrange("p n d -> p (n d)"), ps_a[:]).then_inc(prep, 1)
                nc.vector.tensor_scalar(wT[:, 4, :], ps_t[:, 0:P], gw[:], None, ALU.mult).then_inc(prep, 1)
                dve.wait_ge(prep, 5)

                def layer_norm(i, s):
                    for c in range(TC):
                        norm.stats(dve, i * TC + c, c, tile_of(X, i * TC + c))
                    wait(dve, sg["x_turned"], i)
                    for c in range(TC):
                        dve.wait_ge(norm.rstd_done, i * TC + c + 1)
                        norm.apply(xn[:, c, :], tile_of(X, i * TC + c), c).then_inc(sg["x_normed"], 1)

                def gates(i, s):
                    dve.wait_ge(sg["log_done"], i + 1)
                    wait(dve, sg["exp_done"], i)
                    nc.vector.scalar_tensor_tensor(f[:], ps_z[:], 0.0, zl[:], ALU.min, ALU.subtract).then_inc(sg["f_done"], 1)
                    dve.wait_ge(sg["f_done"], i + 1)
                    nc.vector.tensor_tensor_scan(gs[:], go_on[:], f[:], 0.0, ALU.mult, ALU.add).then_inc(sg["g_done"], 1)
                    dve.wait_ge(sg["g_done"], i + 1)
                    mid = blocks(gs[:])[:, :, BL // 2 - 1:BL // 2].broadcast_to([P, NBK, BL])
                    nc.vector.tensor_tensor(blocks(dk[:]), mid, blocks(gs[:]), ALU.subtract).then_inc(sg["dk_done"], 1)
                    dve.wait_ge(sg["dk_done"], i + 1)
                    nc.vector.tensor_scalar(dq[:], dk[:], -1.0, LIMIT, ALU.mult, ALU.min).then_inc(sg["s_done"], 1)
                    dve.wait_ge(sg["s_done"], 2 * i + 1)
                    nc.vector.tensor_scalar(dk[:], dk[:], LIMIT, None, ALU.min).then_inc(sg["d_done"], 1)

                def silus(i, s):
                    dve.wait_ge(sg["e1_done"], i + 1)
                    nc.vector.reciprocal(r[:], e[:]).then_inc(sg["r_done"], 1)
                    dve.wait_ge(sg["r_done"], i + 1)
                    wait(dve, sg["added"], i - 1)
                    nc.vector.tensor_tensor(qkvT[:, s].rearrange("p n t -> p (n t)"), ps_q[:], r[:], ALU.mult).then_inc(sg["silu_done"], 1)

                def keys(i, s):
                    dve.wait_ge(sg["exp_done"], i + 1)
                    nc.vector.tensor_scalar(sT[:], ef[:], -1.0, 1.0, ALU.mult, ALU.add).then_inc(sg["s_done"], 1)
                    dve.wait_ge(sg["s_done"], 2 * i + 2)
                    nc.vector.tensor_tensor(bT[:, s], sT[:], ek[:], ALU.mult).then_inc(sg["bT_done"], 1)

                def states(i, s, ds_, send_, out, names):
                    s_in, ds_done, send_done, s_done_ = names
                    dve.wait_ge(sg[s_in], i + 1)
                    dve.wait_ge(sg["decay_done"], i + 1)
                    to_end = blocks(eqT[:, s])[:, :, BL - 1:BL].broadcast_to([P, NBK, K])
                    nc.vector.tensor_tensor(ds_[:].rearrange("p k j -> p j k"), ps_s[:].rearrange("p (j k) -> p j k", k=K), to_end,
                                            ALU.mult).then_inc(sg[ds_done], 1)
                    dve.wait_ge(sg[ds_done], i + 1)
                    nc.vector.tensor_tensor_scan(send_[:].rearrange("p k j -> p (k j)"), decay[:, s].rearrange("p k j -> p (k j)"),
                                                 ds_[:].rearrange("p k j -> p (k j)"), 0.0, ALU.mult, ALU.add).then_inc(sg[send_done], 1)
                    dve.wait_ge(sg[send_done], i + 1)
                    nc.vector.tensor_tensor(out[:, 1:, :], send_[:].rearrange("p k j -> p j k")[:, 0:NBK - 1, :],
                                            e_mid[:, s, 1:].unsqueeze(2).broadcast_to([P, NBK - 1, K]), ALU.mult).then_inc(sg[s_done_], 1)

                def mask_scores(i, s, a_in, done):
                    for c in range(TC):
                        dve.wait_ge(sg[a_in], TC * i + c + 1)
                        nc.vector.tensor_tensor(am_all[:, c], ps_a[:].rearrange("p (h t) -> p h t", h=H),
                                                causal[:].unsqueeze(1).broadcast_to([P, H, P]), ALU.mult).then_inc(sg[done], 1)

                def back1(i, s):
                    states(i, s, ds, send, s1, ("s_in", "ds_done", "send_done", "s1_done"))
                    dve.wait_ge(sg["s1_done"], i + 1)
                    wait(dve, sg["sbd_done"], i)
                    dve.sem_inc(norm.held, 1)
                    nc.vector.transpose(s1T[:].rearrange("p j k -> p (j k)"), s1[:].rearrange("p j k -> p (j k)")).then_inc(sg["s1T_done"], 1)
                    wait(dve, sg["sbd2_done"], i)
                    states(i, s, ds2, send2, s2, ("s2_in", "ds2_done", "send2_done", "s2_done"))
                    wait(dve, sg["ov_in"], i)
                    mask_scores(i, s, "a_in", "am_done")

                def back2(i, s):
                    dve.wait_ge(sg["ok_in"], i + 1)
                    nc.vector.tensor_tensor(ok[:], ps_o[:], eqn[:, s], ALU.mult).then_inc(sg["ok_done"], 1)
                    dve.wait_ge(sg["ok_done"], i + 1)
                    heads = lambda m: m.rearrange("p (g k) -> p g k", k=K)
                    wide = lambda m: m.unsqueeze(2).broadcast_to([P, TC * H, K])
                    nc.vector.tensor_reduce(mx[:], heads(ok[:]), AX.X, ALU.max).then_inc(sg["mx_done"], 1)
                    dve.wait_ge(sg["mx_done"], i + 1)
                    nc.vector.tensor_tensor(heads(ok[:]), heads(ok[:]), wide(mx[:]), ALU.subtract).then_inc(sg["sub_done"], 1)
                    dve.wait_ge(sg["ex_done"], i + 1)
                    nc.vector.tensor_reduce(sm_[:], heads(ex[:]), AX.X, ALU.add).then_inc(sg["sum_done"], 1)
                    dve.wait_ge(sg["sum_done"], i + 1)
                    nc.vector.reciprocal(rc[:], sm_[:]).then_inc(sg["rc_done"], 1)
                    dve.wait_ge(sg["rc_done"], i + 1)
                    nc.vector.tensor_tensor(heads(qv[:]), heads(ex[:]), wide(rc[:]), ALU.mult).then_inc(sg["qv_done"], 1)
                    dve.wait_ge(sg["qv_turned"], i + 1)
                    nc.vector.tensor_tensor(q2T[:], ps_t[:], eqT[:, s], ALU.mult).then_inc(sg["q2_done"], 1)
                    mask_scores(i, s, "a2_in", "am2_done")
                    dve.wait_ge(sg["eo1_done"], i + 1)
                    nc.vector.reciprocal(ro[:], eo[:]).then_inc(sg["ro_done"], 1)
                    dve.wait_ge(sg["ro_done"], i + 1)
                    nc.vector.tensor_tensor(o[:], ps_o[:], ro[:], ALU.mult).then_inc(sg["o_done"], 1)
                    dve.wait_ge(sg["o_done"], i + 1)
                    for c in range(TC):
                        oc = o[:, c * P:(c + 1) * P]
                        nc.vector.scalar_tensor_tensor(osq[:, c, :], oc, 1.0, oc, ALU.mult, ALU.mult, accum_out=ss[:, c:c + 1]).then_inc(sg["ss_done"], 1)
                    dve.wait_ge(sg["ss_done"], TC * (i + 1))
                    nc.vector.tensor_scalar(var[:], ss[:], 1.0 / D, EPS, ALU.mult, ALU.add).then_inc(sg["var_done"], 1)
                    dve.wait_ge(sg["rs_done"], i + 1)
                    for c in range(TC):
                        nc.vector.tensor_scalar(on[:, c * P:(c + 1) * P], o[:, c * P:(c + 1) * P], rs[:, c:c + 1], None, ALU.mult)\
                            .then_inc(sg["on_done"], 1)
                    dve.wait_ge(sg["y_in"], i + 1)
                    xb = X[:, bass.ds(i * TC, TC), :].rearrange("p c d -> p (c d)")
                    nc.vector.tensor_tensor(xb, ps_o[:], xb, ALU.add).then_inc(sg["added"], 1)
                pipeline(dve, NB, 2, [(back1, 1), (back2, 1), (layer_norm, 0), (silus, 0), (gates, 0), (keys, 0)])


def chunk_attention(core, name, Wq, Wk, Wv):
    nc, X = core.nc, core.X
    CG, DK = 16, 8
    CH = 32
    NC = 8
    HT = NC * CH
    NHALF = NB * S // HT
    THIRDS = ((0, 0), (1, 0), (0, 1), (2, 0), (0, 2), (1, 1))
    ROWS = DK * len(THIRDS)
    NS = 4 * NC
    UNITS = 2 * NC
    EARLY = 6
    bounce = nc.dram_tensor(f"{name}_bounce", (4, P, 3, 2 * HT), BF16, kind="Internal").ap()
    sbounce = nc.dram_tensor(f"{name}_sbounce", (4, 2, 4, P, NC), BF16, kind="Internal").ap()
    with ExitStack() as ctx:
        ctx.callback(core.release_semaphores)
        sb = lambda n, s, d=F32: ctx.enter_context(nc.sbuf_tensor(f"{name}_{n}", s, d))
        pb = lambda n, k=1: ctx.enter_context(nc.psum_tensor(f"{name}_{n}", [P, 512 * k], F32))
        sem = lambda n: core.semaphore(f"{name}_{n}")
        norm = RowNorm(core, ctx, f"{name}_n", 2)
        w_raw, wT = sb("w_raw", [P, 3, D]), sb("wT", [P, 3, D])
        xn = sb("xn", [P, T, D])
        xnow = sb("xnow", [P, 2, D])
        xT = sb("xT", [P, HT])
        thirds = sb("thirds", [P, 2, 3, 2 * HT], BF16)
        rest = sb("rest", [P, 2 * HT])
        qst = sb("qst", [64, 4, CG * HT], BF16)
        kst = sb("kst", [64, 4, CG * HT], BF16)
        vst = sb("vst", [P, 4, NC, 4, 32])
        mx = sb("mx", [P, 2, NS])
        shift = sb("shift", [P, 2, 2, NS], BF16)
        pT = sb("pT", [P, 4, 2, 512])
        oN = sb("oN", [P, 2, CG, 32])
        rc = sb("rc", [P, 2, CG])
        on = sb("on", [P, 2, D])
        yst = sb("yst", [P, T, 6])
        ps_m, ps_o = pb("ps_m"), pb("ps_o")
        ps_s = [pb(f"ps_s{i}") for i in range(2)]
        ps_p = [pb(f"ps_p{i}", 2) for i in range(2)]
        loaded, prep, memset_done = sem("loaded"), sem("prep"), sem("memset_done")
        held_sp, held_pool = sem("held_sp"), sem("held_pool")
        names = ("x_normed", "xn_kept", "x_turned", "xT_ready", "qk_in", "hi_done", "rest_done", "mid_done", "lo_done", "v_in", "v_ready",
                 "vst_done", "s_in", "max_done", "neg_done", "shift_done", "st_in", "exp_done", "pv_done", "o_turned", "rc_done", "on_done", "y_done", "y_stats")
        sg = {n: sem(n) for n in names}
        bounced = [sem(f"bounced{i}") for i in range(4)]
        sbounced = [sem(f"sbounced{i}") for i in range(4)]
        qk_ready = [sem(f"qk_ready{i}") for i in range(4)]
        shift_ready = [sem(f"shift_ready{i}") for i in range(4)]
        uses = lambda h, s, copies: copies * 4 * (h - s) + copies * 16

        with nc.Block() as block:
            @block.sync
            def _(sp):
                for n, w in enumerate((Wq, Wk, Wv)):
                    sp.dma_start(w_raw[:, n, :], w).then_inc(loaded, 16)
                sp.wait_ge(memset_done, 6)

                def body(front, top):
                    (h, s), (hm, sm) = front, top
                    if h is not None:
                        sp.wait_ge(sg["lo_done"], h + 1)
                        sp.sem_inc(held_sp, 1)
                        if not isinstance(h, int) or h >= 4:
                            sp.wait_ge(sg["pv_done"], 8 * (h - 3))
                        sp.sem_inc(held_sp, 1)
                        sp.dma_start(bounce[s], thirds[:, s % 2]).then_inc(bounced[s], 16)
                        sp.wait_ge(bounced[s], uses(h, s, 1))
                        sp.sem_inc(held_sp, 1)
                        for r, (tq, tk) in enumerate(THIRDS):
                            for t3, o, dst in ((tq, 0, qst), (tk, HT, kst)):
                                src = bounce[s, :, t3, o:o + HT].rearrange("(g d) t -> d g t", d=DK)
                                sp.dma_start(dst[r * DK:(r + 1) * DK, s].rearrange("d (g t) -> d g t", g=CG), src).then_inc(qk_ready[s], 16)
                    if hm is not None:
                        sp.wait_ge(sg["shift_done"], hm + 1)
                        sp.sem_inc(held_sp, 1)
                        sp.dma_start(sbounce[sm].rearrange("j q p a -> p (j q) a"), shift[:, sm % 2].rearrange("p j (q a) -> p (j q) a", a=NC)).then_inc(sbounced[sm], 16)
                        sp.wait_ge(sbounced[sm], uses(hm, sm, 1))
                        sp.sem_inc(held_sp, 1)
                        sp.dma_start(qst[ROWS:ROWS + 2, sm], sbounce[sm].rearrange("j q p a -> j (q p a)")).then_inc(shift_ready[sm], 16)
                staggered(sp, NHALF, 4, (0, 1), body)

            @block.gpsimd
            def _(pool):
                for n, (rows, value) in enumerate(((qst[32:64], 0.0), (kst[32:64], 1.0), (vst[:, 0:2], 0.0), (vst[:, 2:4], 0.0),
                                                   (vst[:, 0:2, :, :, DK:DK + 1], 1.0), (vst[:, 2:4, :, :, DK:DK + 1], 1.0))):
                    nc.gpsimd.memset(rows, value).then_inc(memset_done, 1)
                    pool.wait_ge(memset_done, n + 1)
                def body(front, prob):
                    (h, s), (hp, sp_) = front, prob
                    if h is not None:
                        for c in range(2):
                            norm.rstd(pool, 2 * h + c, c)
                    if hp is not None:
                        outputs(hp, 0)
                    if h is not None:
                        pool.wait_ge(sg["rest_done"], h + 1)
                        if not isinstance(h, int) or h >= 2:
                            qk = qk_ready[(s - 2) % 4]
                            pool.wait_ge(qk, uses(h - 2, (s - 2) % 4, 12))
                        pool.sem_inc(held_pool, 1)
                        nc.gpsimd.tensor_copy(thirds[:, s % 2, 1, :], rest[:]).then_inc(sg["mid_done"], 1)
                        pool.wait_ge(sg["mid_done"], h + 1)
                        nc.gpsimd.tensor_tensor(thirds[:, s % 2, 2, :], rest[:], thirds[:, s % 2, 1, :], ALU.subtract).then_inc(sg["lo_done"], 1)
                    if hp is not None:
                        outputs(hp, 1)

                def outputs(h, g):
                    n = 2 * h + g
                    pool.wait_ge(sg["rc_done"], n + 1)
                    nc.gpsimd.tensor_tensor(on[:, g, :].rearrange("p (c d) -> p c d", d=DK), oN[:, g, :, 0:DK],
                                            rc[:, g, :].unsqueeze(2).broadcast_to([P, CG, DK]), ALU.mult).then_inc(sg["on_done"], 1)
                    pool.wait_ge(sg["on_done"], n + 1)
                    nc.gpsimd.tensor_tensor(tile_of(xn, n), tile_of(xn, n), on[:, g, :], ALU.add).then_inc(sg["y_done"], 1)
                staggered(pool, NHALF, 4, (0, 2), body)

            @block.tensor
            def _(pe):
                pe.wait_ge(loaded, 48)
                for n in range(3):
                    last = nc.tensor.transpose(ps_m[:, n * P:(n + 1) * P], w_raw[:, n, :], core.ident[:])
                last.then_inc(prep, 1)
                pe.wait_ge(prep, 3)

                def front_part(u, h):
                    if u == 2:
                        pe.wait_ge(sg["x_normed"], 2 * (h + 1))
                        wait(pe, sg["vst_done"], h)
                        for c in range(2):
                            last = nc.tensor.transpose(ps_m[:, c * P:(c + 1) * P], xnow[:, c, :], core.ident[:])
                        last.then_inc(sg["x_turned"], 1)
                    if u == 4:
                        pe.wait_ge(sg["xT_ready"], h + 1)
                        for n in range(2):
                            last = nc.tensor.matmul(ps_m[:, n * HT:(n + 1) * HT], wT[:, n, :], xT[:], start=True, stop=True)
                        last.then_inc(sg["qk_in"], 1)
                    if u == 7:
                        pe.wait_ge(sg["rest_done"], h + 1)
                        for a in range(NC):
                            for g in range(4):
                                last = nc.tensor.matmul(ps_m[g * CH:(g + 1) * CH, a * CH:(a + 1) * CH], xT[:, a::NC],
                                                        wT[:, 2, g * CH:(g + 1) * CH], start=True, stop=True)
                        last.then_inc(sg["v_in"], 1)

                def chunk(stack, rows, s, a, tile=None):
                    cols = stack[0:rows, s, a::NC]
                    return cols if tile is None else cols[:, tile * P:(tile + 1) * P]

                def score(k, h, s):
                    a, qt = k // 4, k % 4
                    if k == 0:
                        pe.wait_ge(qk_ready[s], uses(h, s, 12))
                    if isinstance(h, int) and h == 0 and k < 2:
                        pass
                    else:
                        pe.wait_ge(sg["max_done"], NS * h + (k - 1))
                    nc.tensor.matmul(ps_s[k % 2][:], chunk(qst, ROWS, s, a, qt), chunk(kst, ROWS, s, a), start=True, stop=True).then_inc(sg["s_in"], 1)

                def shifted(u, h, s):
                    g, kt, pair = u // 8, u % 8 // 2, u % 2
                    if u == 0:
                        pe.wait_ge(shift_ready[s], uses(h, s, 1))
                    if isinstance(h, int) and h == 0 and u < 2:
                        pass
                    else:
                        pe.wait_ge(sg["exp_done"], UNITS * h + (u - 1))
                    for b in range(2):
                        a = 4 * g + 2 * pair + b
                        last = nc.tensor.matmul(ps_p[u % 2][:, b * 512:(b + 1) * 512], chunk(kst, ROWS + 2, s, a, kt), chunk(qst, ROWS + 2, s, a),
                                                start=True, stop=True)
                    last.then_inc(sg["st_in"], 1)

                def values(r, h, s):
                    g, kt = r // 4, r % 4
                    pe.wait_ge(sg["exp_done"], UNITS * h + 2 * r + 2)
                    if r == 0:
                        pe.wait_ge(sg["vst_done"], h + 1)
                    if kt == 0:
                        wait(pe, sg["o_turned"], 2 * h + g)
                    for b in range(4):
                        a = 4 * g + b
                        last = nc.tensor.matmul(ps_o[b * 32:(b + 1) * 32, :], vst[:, s, a, kt, :], pT[:, (2 * r + b // 2) % 4, b % 2, :],
                                                start=(kt == 0), stop=(kt == 3))
                    last.then_inc(sg["pv_done"], 1)

                def body(front, top, prob):
                    (h, s), (hm, sm), (hp, sp_) = front, top, prob
                    k = 0
                    if hm is not None:
                        for k in range(EARLY):
                            score(k, hm, sm)
                        k = EARLY
                    for u in range(UNITS):
                        if hp is not None:
                            shifted(u, hp, sp_)
                            if u % 2 and u >= 3:
                                values((u - 3) // 2, hp, sp_)
                        if h is not None:
                            front_part(u, h)
                        if hm is not None:
                            for _ in range(2):
                                if k < NS:
                                    score(k, hm, sm)
                                    k += 1
                    if hp is not None:
                        values(7, hp, sp_)
                staggered(pe, NHALF, 4, (0, 1, 2), body)

            @block.scalar
            def _(act):
                def front_part(u, h, s):
                    if u == 3:
                        act.wait_ge(sg["x_turned"], h + 1)
                        nc.scalar.copy(xT[:].rearrange("p (t a) -> p a t", a=NC), ps_m[:, 0:HT].rearrange("p (a t) -> p a t", a=NC)).then_inc(sg["xT_ready"], 1)
                    if u == 5:
                        act.wait_ge(sg["qk_in"], h + 1)
                        if not isinstance(h, int) or h >= 2:
                            act.wait_ge(qk_ready[(s - 2) % 4], uses(h - 2, (s - 2) % 4, 12))
                        nc.scalar.copy(thirds[:, s % 2, 0, :], ps_m[:]).then_inc(sg["hi_done"], 1)
                    if u == 9:
                        act.wait_ge(sg["v_in"], h + 1)
                        if not isinstance(h, int) or h >= 4:
                            act.wait_ge(sg["pv_done"], 8 * (h - 3))
                        nc.scalar.copy(vst[:, s, :, :, 0:DK], ps_m[:, 0:HT].rearrange("p (a k d) -> p a k d", a=NC, k=4)).then_inc(sg["vst_done"], 1)

                def body(front, prob):
                    (h, s), (hp, sp_) = front, prob
                    for u in range(UNITS):
                        if hp is not None:
                            act.wait_ge(sg["st_in"], UNITS * hp + u + 1)
                            if not (isinstance(hp, int) and hp == 0 and u < 4):
                                act.wait_ge(sg["pv_done"], 8 * hp + (u // 2 - 1))
                            nc.scalar.activation(pT[:, u % 4].rearrange("p b q -> p (b q)"), ps_p[u % 2][:], ACT.Exp).then_inc(sg["exp_done"], 1)
                        if h is not None:
                            front_part(u, h, s)
                staggered(act, NHALF, 4, (0, 2), body)

            @block.vector
            def _(dve):
                dve.wait_ge(prep, 1)
                nc.vector.tensor_copy(wT[:, 0:2, :].rearrange("p n d -> p (n d)"), ps_m[:, 0:2 * P]).then_inc(prep, 1)
                nc.vector.tensor_copy(wT[:, 2, :].rearrange("p (g k d) -> p k g d", g=4, d=DK),
                                      ps_m[:, 2 * P:3 * P].rearrange("p (k g d) -> p k g d", g=4, d=DK)).then_inc(prep, 1)

                def front_part(k, h, s):
                    if k == 0:
                        for c in range(2):
                            norm.stats(dve, 2 * h + c, c, tile_of(X, 2 * h + c))
                    if k == 3:
                        wait(dve, sg["x_turned"], h)
                        for c in range(2):
                            dve.wait_ge(norm.rstd_done, 2 * h + c + 1)
                            norm.apply(xnow[:, c, :], tile_of(X, 2 * h + c), c).then_inc(sg["x_normed"], 1)
                    if k == 4:
                        dve.wait_ge(sg["x_normed"], 2 * (h + 1))
                        nc.vector.tensor_copy(xn[:, bass.ds(2 * h, 2), :], xnow[:]).then_inc(sg["xn_kept"], 1)
                    if k == 18:
                        dve.wait_ge(sg["hi_done"], h + 1)
                        wait(dve, sg["lo_done"], h)
                        nc.vector.tensor_tensor(rest[:], ps_m[:], thirds[:, s % 2, 0, :], ALU.subtract).then_inc(sg["rest_done"], 1)

                def turn_outputs(h, g):
                    n = 2 * h + g
                    dve.wait_ge(sg["pv_done"], 8 * h + 4 * g + 4)
                    wait(dve, sg["on_done"], n - 1)
                    dve.sem_inc(norm.held, 1)
                    nc.vector.transpose(oN[:, g].rearrange("p c d -> p (c d)"), ps_o[:]).then_inc(sg["o_turned"], 1)
                    dve.wait_ge(sg["o_turned"], n + 1)
                    nc.vector.reciprocal(rc[:, g, :], oN[:, g, :, DK]).then_inc(sg["rc_done"], 1)

                def stats_of(n):
                    dve.wait_ge(sg["y_done"], n + 1)
                    nc.vector.bn_stats(yst[:, bass.ds(n, 1), :].rearrange("p a d -> p (a d)"), tile_of(xn, n)).then_inc(sg["y_stats"], 1)

                def body(front, top, prob):
                    (h, s), (hm, sm), (hp, sp_) = front, top, prob
                    for k in range(NS):
                        if h is not None:
                            front_part(k, h, s)
                        if hp is not None and k == 26:
                            turn_outputs(hp, 0)
                        if hm is not None:
                            dve.wait_ge(sg["s_in"], NS * hm + k + 1)
                            nc.vector.tensor_reduce(mx[:, sm % 2, k % 4 * NC + k // 4:k % 4 * NC + k // 4 + 1], ps_s[k % 2][:], AX.X, ALU.max).then_inc(sg["max_done"], 1)
                    if hm is not None:
                        dve.wait_ge(sg["max_done"], NS * (hm + 1))
                        if not isinstance(hm, int) or hm >= 2:
                            dve.wait_ge(shift_ready[(sm - 2) % 4], uses(hm - 2, (sm - 2) % 4, 1))
                        nc.vector.tensor_scalar(shift[:, sm % 2, 0, :], mx[:, sm % 2, :], -1.0, None, ALU.mult).then_inc(sg["neg_done"], 1)
                        dve.wait_ge(sg["neg_done"], hm + 1)
                        nc.vector.scalar_tensor_tensor(shift[:, sm % 2, 1, :], mx[:, sm % 2, :], -1.0, shift[:, sm % 2, 0, :],
                                                       ALU.mult, ALU.subtract).then_inc(sg["shift_done"], 1)
                    if hp is not None:
                        turn_outputs(hp, 1)
                        stats_of(2 * hp)
                        stats_of(2 * hp + 1)
                staggered(dve, NHALF, 4, (0, 1, 2), body)

        mv, sq, tot, msq = sb("mv", [P, NB, 2]), sb("sq", [P, NB, 2]), sb("tot", [P, NB, 2]), sb("msq", [P, NB])
        rs, half, yn = sb("rs", [P, NB]), sb("half", [P, NB]), sb("yn", [P, 2, 4 * D])
        dv, pw, nd, ad, nd2 = sem("dv"), sem("pw"), sem("nd"), sem("ad"), sem("nd2")
        with nc.Block() as block:
            @block.vector
            def _(dve):
                n = [0]

                def done(ins):
                    n[0] += 1
                    ins.then_inc(dv, 1)
                    dve.wait_ge(dv, n[0])
                for b in range(NB):
                    ins = nc.vector.bn_aggr(mv[:, b, :], yst[:, 4 * b:4 * b + 4, :].rearrange("p t s -> p (t s)"))
                    ins.then_inc(dv, 1)
                n[0] = NB
                dve.wait_ge(dv, NB)
                done(nc.vector.tensor_copy(sq[:, :, 0], mv[:, :, 0]))
                done(nc.vector.tensor_tensor(sq[:, :, 1], mv[:, :, 0], mv[:, :, 0], ALU.mult))
                done(nc.vector.tensor_tensor(sq[:, :, 1], sq[:, :, 1], mv[:, :, 1], ALU.add))
                dve.wait_ge(pw, 1)
                done(nc.vector.tensor_scalar(tot[:].rearrange("p b s -> p (b s)"), ps_m[:, 0:2 * NB], 1.0 / P, None, ALU.mult))
                done(nc.vector.tensor_tensor(msq[:], tot[:, :, 0], tot[:, :, 0], ALU.mult))
                done(nc.vector.tensor_tensor(msq[:], tot[:, :, 1], msq[:], ALU.subtract))
                done(nc.vector.tensor_scalar(msq[:], msq[:], EPS, None, ALU.add))
                dve.wait_ge(pw, 2)

                def add(b):
                    x = X[:, 4 * b:4 * b + 4, :].rearrange("p t d -> p (t d)")
                    dve.wait_ge(nd, b + 1)
                    nc.vector.tensor_tensor(x, x, yn[:, b % 2, :], ALU.add).then_inc(ad, 1)
                for b in range(NB):
                    y = xn[:, 4 * b:4 * b + 4, :].rearrange("p t d -> p (t d)")
                    wait(dve, ad, b - 1)
                    nc.vector.tensor_scalar(yn[:, b % 2, :], y, tot[:, b, 0:1], rs[:, b:b + 1], ALU.subtract, ALU.mult).then_inc(nd, 1)
                    if b >= 1:
                        add(b - 1)
                add(NB - 1)

            @block.tensor
            def _(pe):
                pe.wait_ge(dv, NB + 3)
                nc.tensor.matmul(ps_m[:, 0:2 * NB], core.ones[:], sq[:].rearrange("p b s -> p (b s)"), start=True, stop=True).then_inc(pw, 1)

            @block.gpsimd
            def _(pool):
                nc.gpsimd.memset(half[:], -0.5).then_inc(nd2, 1)
                pool.wait_ge(dv, NB + 7)
                pool.wait_ge(nd2, 1)
                nc.gpsimd.tensor_tensor(rs[:], msq[:], half[:], ALU.pow).then_inc(pw, 1)


def rope_attention(core, name, Wq, Wk, Wv, Wo, bo, cos_in, sin_in):
    nc, X = core.nc, core.X
    HEADS, DH = 16, 64
    NP = HEADS // 2
    N = NB * NP
    TC = S // P
    UNITS = 2 * TC
    ORDER = (3, 0, 2, 1)
    MASKED = 1e30
    LN, FRONT, SCORE, VALUE, OUT = 0, 4, 5, 6, 7
    with ExitStack() as ctx:
        ctx.callback(core.release_semaphores)
        sb = lambda n, s, d=F32: ctx.enter_context(nc.sbuf_tensor(f"{name}_{n}", s, d))
        pb = lambda n, k=1: ctx.enter_context(nc.psum_tensor(f"{name}_{n}", [P, 512 * k], F32))
        sem = lambda n: core.semaphore(f"{name}_{n}")
        norm = RowNorm(core, ctx, f"{name}_n", TC)
        w = sb("w", [P, 4, NP, P])
        wv, wo = sb("wv", [P, NP, P]), sb("wo", [P, NP, D])
        bias = sb("bias", [1, D])
        cos, sin = sb("cos", [P, S]), sb("sin", [P, S])
        mask = sb("mask", [P, P], BF16)
        xn, xT = sb("xn", [P, TC, D]), sb("xT", [P, S])
        by_cos, by_sin = sb("by_cos", [P, 2, S]), sb("by_sin", [P, 2, S])
        rot = sb("rot", [P, 2, 2, S])
        v = sb("v", [P, 4, TC, P])
        low = sb("low", [P, 2, UNITS])
        prob = sb("prob", [P, UNITS, S])
        total = sb("total", [P, 2, UNITS])
        inverse = sb("inverse", [P, UNITS])
        probT = sb("probT", [P, 2, S])
        on, oT = sb("on", [P, 2, S]), sb("oT", [P, S])
        ps_r, ps_o = pb("ps_r"), pb("ps_o")
        ps_s = [pb(f"ps_s{i}") for i in range(4)]
        ps_t = [pb(f"ps_t{i}") for i in range(2)]
        loaded, prep = sem("loaded"), sem("prep")
        names = ("x_normed", "x_turned", "xT_ready", "qk_in", "multiplied", "rotated", "v_in", "v_ready", "s_in", "low_done", "exp_done",
                 "p_turned", "probT_dve", "probT_act", "pv_done", "inverse_done", "on_done", "o_turned", "oT_ready", "y_in", "added")
        sg = {n: sem(n) for n in names}

        def unit(u):
            head, tile = u % 2, ORDER[u // 2]
            return head, tile, (tile + 1) * P, 2 * tile + head

        def steps(engine, body):
            item_steps(engine, NP, OUT, body)

        with nc.Block() as block:
            @block.sync
            def _(sp):
                for k, src in ((0, Wq), (2, Wk)):
                    sp.dma_start(w[:, k], src.rearrange("c (h d) -> c h d", d=P)).then_inc(loaded, 16)
                sp.dma_start(wv[:], Wv.rearrange("c (h d) -> c h d", d=P)).then_inc(loaded, 16)
                sp.dma_start(wo[:], Wo.rearrange("(h d) c -> d h c", d=P)).then_inc(loaded, 16)
                sp.dma_start(bias[:], bo.rearrange("(a c) -> a c", a=1)).then_inc(loaded, 16)
                sp.dma_start(cos[:], cos_in).then_inc(loaded, 16)
                sp.dma_start(sin[:], sin_in).then_inc(loaded, 16)

            @block.gpsimd
            def _(pool):
                nc.gpsimd.memset(mask[:], 0.0).then_inc(prep, 1)
                pool.wait_ge(prep, 1)
                nc.gpsimd.affine_select(out=mask[:], in_=mask[:], compare_op=ALU.is_ge, fill=MASKED, base=0,
                                        pattern=[[-1, P]], channel_multiplier=1).then_inc(prep, 1)
                pool.wait_ge(loaded, 112)
                nc.gpsimd.tensor_tensor(w[:, 0].rearrange("p h d -> p (h d)"), w[:, 0].rearrange("p h d -> p (h d)"),
                                        core.minus_eighth[:, 0:1].broadcast_to([P, NP * P]), ALU.mult).then_inc(prep, 1)
                pool.wait_ge(prep, 3)
                for k in (0, 2):
                    for a in range(2):
                        nc.gpsimd.tensor_copy(w[:, k + 1, :, a::2], w[:, k, :, 1 - a::2]).then_inc(prep, 1)

                def body(item):
                    ln, front = item(LN), item(FRONT)
                    if ln and ln[2] == 0:
                        for c in range(TC):
                            norm.rstd(pool, TC * ln[1] + c, c)
                    if front:
                        n = front[0]
                        for k in range(2):
                            pool.wait_ge(sg["multiplied"], 4 * n + 2 * k + 2)
                            nc.gpsimd.tensor_tensor(rot[:, front[2] % 2, k], by_cos[:, k], by_sin[:, k], ALU.add).then_inc(sg["rotated"], 1)
                steps(pool, body)

            @block.tensor
            def _(pe):
                pe.wait_ge(prep, 7)

                def front_part(u, n, b, p):
                    if u == 0 and p == 0:
                        pe.wait_ge(sg["x_normed"], TC * (b + 1))
                        wait(pe, sg["v_ready"], n)
                        wait(pe, sg["added"], n - (OUT - FRONT))
                        for c in range(TC):
                            last = nc.tensor.transpose(ps_r[:, c * P:(c + 1) * P], xn[:, c, :], core.ident[:])
                        last.then_inc(sg["x_turned"], 1)
                    if 1 <= u <= 4:
                        if u == 1:
                            if p == 0:
                                pe.wait_ge(sg["xT_ready"], b + 1)
                            else:
                                wait(pe, sg["v_ready"], n)
                                wait(pe, sg["added"], n - (OUT - FRONT))
                        else:
                            pe.wait_ge(sg["multiplied"], 4 * n + u - 1)
                        nc.tensor.matmul(ps_r[:], w[:, u - 1, p, :], xT[:], start=True, stop=True).then_inc(sg["qk_in"], 1)
                    if u == 5:
                        pe.wait_ge(sg["multiplied"], 4 * n + 4)
                        for c in range(TC):
                            last = nc.tensor.matmul(ps_r[:, c * P:(c + 1) * P], xT[:, c * P:(c + 1) * P], wv[:, p, :], start=True, stop=True)
                        last.then_inc(sg["v_in"], 1)

                def scores(u, n, b, p):
                    head, tile, keys, _ = unit(u)
                    rows = slice(head * DH, (head + 1) * DH)
                    if u == 0:
                        pe.wait_ge(sg["rotated"], 2 * (n + 1))
                    wait(pe, sg["exp_done"], UNITS * n + u - 3)
                    out = ps_s[2 * head + u // 2 % 2]
                    nc.tensor.matmul(out[:, 0:keys], rot[rows, p % 2, 0, tile * P:(tile + 1) * P], rot[rows, p % 2, 1, 0:keys],
                                     start=True, stop=False, skip_group_check=True)
                    nc.tensor.matmul(out[:, tile * P:keys], core.identb[:], mask[:], start=False, stop=True,
                                     skip_group_check=True).then_inc(sg["s_in"], 1)

                def turn(u, n, b, p):
                    head, tile, keys, _ = unit(u)
                    pe.wait_ge(sg["exp_done"], UNITS * n + u + 1)
                    wait(pe, sg["probT_act" if head else "probT_dve"], TC * n + u // 2)
                    for c in range(tile + 1):
                        last = nc.tensor.transpose(ps_t[head][:, c * P:(c + 1) * P], prob[:, u, c * P:(c + 1) * P], core.ident[:])
                    last.then_inc(sg["p_turned"], 1)

                def values(u, n, b, p):
                    head, tile, keys, _ = unit(u)
                    if u == 0:
                        wait(pe, sg["on_done"], n)
                    pe.wait_ge(sg["probT_act" if head else "probT_dve"], TC * n + u // 2 + 1)
                    at = tile * P + head * DH
                    for c in range(tile + 1):
                        last = nc.tensor.matmul(ps_o[:, at:at + DH], probT[:, head, c * P:(c + 1) * P], v[:, p % 4, c, head * DH:(head + 1) * DH],
                                                start=(c == 0), stop=(c == tile))
                    last.then_inc(sg["pv_done"], 1)

                def out_part(u, n, b, p, front):
                    if u == 6:
                        pe.wait_ge(sg["on_done"], n + 1)
                        if front:
                            pe.wait_ge(sg["v_ready"], front[0] + 1)
                        else:
                            pe.wait_ge(sg["added"], n)
                        for c in range(TC):
                            last = nc.tensor.transpose(ps_r[:, c * P:(c + 1) * P], on[:, p % 2, c * P:(c + 1) * P], core.ident[:])
                        last.then_inc(sg["o_turned"], 1)
                    if u == 7:
                        pe.wait_ge(sg["oT_ready"], n + 1)
                        for c in range(TC):
                            at = slice(c * P, (c + 1) * P)
                            if p == 0:
                                nc.tensor.matmul(ps_r[:, at], core.ones[0:1, :], bias[:], start=True, stop=False)
                            last = nc.tensor.matmul(ps_r[:, at], oT[:, at], wo[:, p, :], start=(p != 0), stop=True)
                        last.then_inc(sg["y_in"], 1)

                def body(item):
                    front, score, value, out = item(FRONT), item(SCORE), item(VALUE), item(OUT)
                    for u in range(UNITS):
                        if value:
                            turn(u, *value)
                        if front:
                            front_part(u, *front)
                        if out:
                            out_part(u, *out, front)
                        if score:
                            scores(u, *score)
                        if value:
                            values(u, *value)
                steps(pe, body)

            @block.scalar
            def _(act):
                def exps(u, n, b, p):
                    head, tile, keys, at = unit(u)
                    act.wait_ge(sg["low_done"], UNITS * n + u + 1)
                    wait(act, sg["p_turned"], UNITS * (n - 1) + u + 1)
                    if u == 0:
                        wait(act, sg["inverse_done"], n - 1)
                    nc.scalar.activation(prob[:, u, 0:keys], ps_s[2 * head + u // 2 % 2][:, 0:keys], ACT.Exp, bias=low[:, p % 2, u:u + 1],
                                         scale=-1.0, accum_out=total[:, p % 2, at:at + 1]).then_inc(sg["exp_done"], 1)

                def body(item):
                    front, score, value, out = item(FRONT), item(SCORE), item(VALUE), item(OUT)
                    for u in range(UNITS):
                        if value and u % 2:
                            keys = unit(u)[2]
                            act.wait_ge(sg["p_turned"], UNITS * value[0] + u + 1)
                            wait(act, sg["pv_done"], UNITS * value[0] + u - 1)
                            nc.scalar.copy(probT[:, 1, 0:keys], ps_t[1][:, 0:keys]).then_inc(sg["probT_act"], 1)
                        if front and u == 0 and front[2] == 0:
                            act.wait_ge(sg["x_turned"], front[1] + 1)
                            wait(act, sg["v_in"], front[0])
                            nc.scalar.copy(xT[:], ps_r[:]).then_inc(sg["xT_ready"], 1)
                        if front and u == 5:
                            act.wait_ge(sg["v_in"], front[0] + 1)
                            wait(act, sg["pv_done"], UNITS * (front[0] - 3))
                            nc.scalar.copy(v[:, front[2] % 4].rearrange("p c d -> p (c d)"), ps_r[:]).then_inc(sg["v_ready"], 1)
                        if out and u == 6:
                            act.wait_ge(sg["o_turned"], out[0] + 1)
                            wait(act, sg["y_in"], out[0])
                            nc.scalar.copy(oT[:], ps_r[:]).then_inc(sg["oT_ready"], 1)
                        if score:
                            exps(u, *score)
                steps(act, body)

            @block.vector
            def _(dve):
                def body(item):
                    ln, front, score, value, out = item(LN), item(FRONT), item(SCORE), item(VALUE), item(OUT)
                    if ln and ln[2] == 0:
                        for c in range(TC):
                            norm.stats(dve, TC * ln[1] + c, c, tile_of(X, TC * ln[1] + c))
                    if ln and ln[2] == 1:
                        wait(dve, sg["x_turned"], ln[1])
                        for c in range(TC):
                            dve.wait_ge(norm.rstd_done, TC * ln[1] + c + 1)
                            norm.apply(xn[:, c, :], tile_of(X, TC * ln[1] + c), c).then_inc(sg["x_normed"], 1)
                    for u in range(UNITS):
                        if value and u % 2 == 0:
                            keys = unit(u)[2]
                            dve.wait_ge(sg["p_turned"], UNITS * value[0] + u + 1)
                            wait(dve, sg["pv_done"], UNITS * value[0] + u - 1)
                            nc.vector.tensor_copy(probT[:, 0, 0:keys], ps_t[0][:, 0:keys]).then_inc(sg["probT_dve"], 1)
                        if front and 1 <= u <= 4:
                            n = front[0]
                            k, odd = (u - 1) // 2, (u - 1) % 2
                            dve.wait_ge(sg["qk_in"], 4 * n + u)
                            wait(dve, sg["rotated"], 2 * (n - 1) + k + 1)
                            nc.vector.tensor_tensor((by_sin if odd else by_cos)[:, k], ps_r[:], (sin if odd else cos)[:], ALU.mult)\
                                .then_inc(sg["multiplied"], 1)
                        if score:
                            head, tile, keys, _ = unit(u)
                            n, p = score[0], score[2]
                            dve.wait_ge(sg["s_in"], UNITS * n + u + 1)
                            if u == 0:
                                wait(dve, sg["exp_done"], UNITS * (n - 1))
                            nc.vector.tensor_reduce(low[:, p % 2, u:u + 1], ps_s[2 * head + u // 2 % 2][:, 0:keys], AX.X, ALU.min)\
                                .then_inc(sg["low_done"], 1)
                        if value and u == 0:
                            wait(dve, sg["on_done"], value[0])
                            dve.wait_ge(sg["exp_done"], UNITS * (value[0] + 1))
                            nc.vector.reciprocal(inverse[:], total[:, value[2] % 2]).then_inc(sg["inverse_done"], 1)
                    if out:
                        n, b = out[0], out[1]
                        dve.wait_ge(sg["y_in"], n + 1)
                        xb = X[:, bass.ds(b * TC, TC), :].rearrange("p c d -> p (c d)")
                        wait(dve, sg["added"], n)
                        nc.vector.tensor_tensor(xb, ps_r[:], xb, ALU.add).then_inc(sg["added"], 1)
                    if value:
                        n, p = value[0], value[2]
                        dve.wait_ge(sg["pv_done"], UNITS * (n + 1))
                        dve.wait_ge(sg["inverse_done"], n + 1)
                        wait(dve, sg["o_turned"], n - 1)
                        heads = lambda m: m.rearrange("p (g d) -> p g d", d=DH)
                        nc.vector.tensor_tensor(heads(on[:, p % 2]), heads(ps_o[:]), inverse[:].unsqueeze(2).broadcast_to([P, UNITS, DH]),
                                                ALU.mult).then_inc(sg["on_done"], 1)
                steps(dve, body)


def build(nc, a, out):
    with ExitStack() as ctx:
        core = Core(nc, ctx)
        core.load(a["L0_attn_a_x"].rearrange("b s d -> (b s) d"))
        chunk_attention(core, "ca", a["L0_attn_a_Wq"], a["L0_attn_a_Wk"], a["L0_attn_a_Wv"])
        expert_ffn(core, "moe1", a["L0_ffn_centroids"], a["L0_ffn_gamma"], a["L0_ffn_beta"], a["L0_ffn_W1"], a["L0_ffn_b1"], a["L0_ffn_W2"], a["L0_ffn_b2"])
        rope_attention(core, "ra", a["L0_attn_b_Wq"], a["L0_attn_b_Wk"], a["L0_attn_b_Wv"], a["L0_attn_b_Wo"], a["L0_attn_b_bo"], a["rope_cos"], a["rope_sin"])
        expert_ffn(core, "moe3", a["L0_ffn_centroids"], a["L0_ffn_gamma"], a["L0_ffn_beta"], a["L0_ffn_W1"], a["L0_ffn_b1"], a["L0_ffn_W2"], a["L0_ffn_b2"])
        gated_slots(core, "gsa", a["L1_attn_a_Wq"], a["L1_attn_a_Wk"], a["L1_attn_a_Wv"], a["L1_attn_a_Wf"], a["L1_attn_a_g_w"], a["L1_attn_a_Wo"], a["gsa_part"], a["gsa_causal"], a["gsa_go_on"])
        ternary_ffn(core, "ffn15", a["L1_ffn_W_fc"], a["L1_ffn_ln_w"], a["L1_ffn_ln_b"], a["L1_ffn_W_proj"])
        channel_ssm(core, "ssm", a["L1_attn_b_A"], a["L1_attn_b_Bp"], a["L1_attn_b_Cp"], a["L1_attn_b_Dp"], a["L1_attn_b_Wg"], a["L1_attn_b_bg"], a["L1_attn_b_gamma"], a["L1_attn_b_beta"], a["ssm_same"], a["ssm_shift"])
        ternary_ffn(core, "ffn17", a["L1_ffn_W_fc"], a["L1_ffn_ln_w"], a["L1_ffn_ln_b"], a["L1_ffn_W_proj"])
        core.store(out.rearrange("b s d -> (b s) d"))


def rope_tables():
    dim = 64
    freq = (1.0 / np.power(np.float32(10000.0), np.arange(0, dim, 2, dtype=np.float32) / np.float32(dim))).astype(np.float32)
    angle = (np.arange(S, dtype=np.float32)[None, :] * freq[:, None]).astype(np.float32)
    cos, sin = np.cos(angle), np.sin(angle)
    cos_t = np.repeat(cos, 2, axis=0)
    sin_t = np.repeat(sin, 2, axis=0)
    sin_t[0::2] *= -1
    return np.tile(cos_t, (2, 1)).astype(np.float32), np.tile(sin_t, (2, 1)).astype(np.float32)


def kernel(**inputs):
    import concourse.bacc as bacc
    from concourse.bass_utils import run_bass_kernel_spmd

    nc = bacc.Bacc("TRN2", target_bir_lowering=False, num_devices=1)
    given = {name: np.ascontiguousarray(v) for name, v in inputs.items()}
    given["rope_cos"], given["rope_sin"] = rope_tables()
    given["ssm_same"], given["ssm_shift"] = ssm_tables()
    given["gsa_part"], given["gsa_causal"], given["gsa_go_on"] = slot_tables()
    arrays, aps = {}, {}
    for name, v in given.items():
        arrays[f"in_{name}"] = v
        aps[name] = nc.dram_tensor(f"in_{name}", v.shape, mybir.dt.from_np(v.dtype), kind="ExternalInput").ap()
    out = nc.dram_tensor("out_x", (NB, S, D), F32, kind="ExternalOutput").ap()
    build(nc, aps, out)
    got = run_bass_kernel_spmd(nc, [arrays], core_ids=[0])
    return got.results[0]["out_x"]
```

```python
import numpy as np
import concourse.bass as bass
from concourse import mybir
from contextlib import ExitStack

F32 = mybir.dt.float32
BF16 = mybir.dt.bfloat16
ALU = mybir.AluOpType
ACT = mybir.ActivationFunctionType
AX = mybir.AxisListType

P = 128
D = 128
NB, S = 16, 512
T = NB * S // P
EPS = 1e-5


def pipeline(engine, n, unroll, stages):
    lag = max(l for _, l in stages)
    head = -(-(lag + unroll) // unroll) * unroll
    head = min(head, n)

    def step(s, at):
        for stage, l in stages:
            if not isinstance(s, int) or 0 <= s - l < n:
                stage(s - l, (at - l) % unroll)

    for s in range(head):
        step(s, s)
    if n > head:
        with engine.Fori(0, (n - head) // unroll) as i:
            for j in range(unroll):
                step(i * unroll + (head + j), j)
    for s in range(n, n + lag):
        step(s, s)


def wait(engine, sem, count):
    if not isinstance(count, int) or count > 0:
        engine.wait_ge(sem, count)


class Core:

    def __init__(self, nc, ctx):
        self.nc = nc
        self.held = []
        sb = lambda n, s, d: ctx.enter_context(nc.sbuf_tensor(n, s, d))
        self.X = sb("X", [P, T, D], F32)
        self.ident = sb("ident", [P, P], F32)
        self.identb = sb("identb", [P, P], BF16)
        self.ones = sb("ones", [P, P], F32)
        self.minus_half = sb("minus_half", [P, 8], F32)
        self.minus_eighth = sb("minus_eighth", [P, 1], F32)

    def semaphore(self, name):
        s = self.nc.alloc_semaphore(name=name)
        self.held.append(s)
        return s

    def release_semaphores(self):
        self.nc.clear_and_free_semaphores(self.held)
        self.held = []
        self.nc.all_engine_barrier()

    def load(self, x):
        nc = self.nc
        with ExitStack() as ctx:
            loaded = ctx.enter_context(nc.semaphore("x_loaded"))
            zeroed = ctx.enter_context(nc.semaphore("consts_zeroed"))
            with nc.Block() as block:
                @block.sync
                def _(sp):
                    xt = x.rearrange("(n p) d -> p n d", p=P)
                    for q in range(4):
                        sp.dma_start(self.X[:, q * 16:(q + 1) * 16, :], xt[:, q * 16:(q + 1) * 16, :]).then_inc(loaded, 16)
                    sp.wait_ge(loaded, 64)

                @block.gpsimd
                def _(pool):
                    nc.gpsimd.memset(self.ident[:], 0.0).then_inc(zeroed, 1)
                    nc.gpsimd.memset(self.identb[:], 0.0).then_inc(zeroed, 1)
                    nc.gpsimd.memset(self.ones[:], 1.0).then_inc(zeroed, 1)
                    nc.gpsimd.memset(self.minus_half[:], -0.5).then_inc(zeroed, 1)
                    nc.gpsimd.memset(self.minus_eighth[:], -0.125).then_inc(zeroed, 1)
                    pool.wait_ge(zeroed, 5)
                    for m in (self.ident, self.identb):
                        nc.gpsimd.affine_select(out=m[:], in_=m[:], compare_op=ALU.not_equal, fill=1.0, base=0,
                                                pattern=[[-1, P]], channel_multiplier=1).then_inc(zeroed, 1)
                    pool.wait_ge(zeroed, 7)

    def store(self, out):
        nc = self.nc
        with ExitStack() as ctx:
            stored = ctx.enter_context(nc.semaphore("x_stored"))
            with nc.Block() as block:
                @block.sync
                def _(sp):
                    xt = out.rearrange("(n p) d -> p n d", p=P)
                    for q in range(4):
                        sp.dma_start(xt[:, q * 16:(q + 1) * 16, :], self.X[:, q * 16:(q + 1) * 16, :]).then_inc(stored, 16)
                    sp.wait_ge(stored, 64)


class RowNorm:

    def __init__(self, core, ctx, name, slots=2):
        nc = self.nc = core.nc
        self.core, self.slots = core, slots
        sb = lambda n, s: ctx.enter_context(nc.sbuf_tensor(f"{name}_{n}", s, F32))
        sem = lambda n: core.semaphore(f"{name}_{n}")
        self.parts = sb("parts", [P, slots, 6])
        self.mv = sb("mv", [P, slots, 2])
        self.var = sb("var", [P, slots])
        self.rs = sb("rs", [P, slots])
        self.held = sem("held")
        self.parts_done, self.mean_done, self.var_done, self.rstd_done = (
            sem(n) for n in ("parts_done", "mean_done", "var_done", "rstd_done"))

    def stats(self, dve, t, s, rows):
        nc = self.nc
        nc.vector.bn_stats(self.parts[:, s, :], rows).then_inc(self.parts_done, 1)
        dve.wait_ge(self.parts_done, t + 1)
        dve.sem_inc(self.held, 1)
        nc.vector.bn_aggr(self.mv[:, s, :], self.parts[:, s, :]).then_inc(self.mean_done, 1)
        dve.wait_ge(self.mean_done, t + 1)
        nc.vector.tensor_scalar(self.var[:, s:s + 1], self.mv[:, s, 1:2], EPS, None, ALU.add).then_inc(self.var_done, 1)

    def rstd(self, pool, t, s):
        pool.wait_ge(self.var_done, t + 1)
        self.nc.gpsimd.tensor_tensor(self.rs[:, s:s + 1], self.var[:, s:s + 1], self.core.minus_half[:, 0:1], ALU.pow)\
            .then_inc(self.rstd_done, 1)

    def apply(self, out, rows, s):
        return self.nc.vector.tensor_scalar(out, rows, self.mv[:, s, 0:1], self.rs[:, s:s + 1], ALU.subtract, ALU.mult)


def tile_of(buf, t):
    return buf[:, bass.ds(t, 1), :].rearrange("p a d -> p (a d)")


def staggered(engine, n, unroll, lags, body):
    lag = max(lags)
    head = min(-(-(lag + unroll) // unroll) * unroll, n)

    def step(s, at):
        body(*[(None if isinstance(s, int) and not 0 <= s - l < n else s - l, (at - l) % unroll) for l in lags])

    for s in range(head):
        step(s, s)
    if n > head:
        with engine.Fori(0, (n - head) // unroll) as i:
            for j in range(unroll):
                step(i * unroll + (head + j), j)
    for s in range(n, n + lag):
        step(s, s)


def item_steps(engine, per_seq, last_lag, body):
    def step(b, p):
        def item(lag):
            part, seq = (p - lag) % per_seq, b + (p - lag) // per_seq
            if isinstance(b, int) and not 0 <= seq < NB:
                return None
            return seq * per_seq + part, seq, part
        body(item)

    head = -(-last_lag // per_seq)
    for b in range(head):
        for p in range(per_seq):
            step(b, p)
    with engine.Fori(0, NB - head) as i:
        for p in range(per_seq):
            step(i + head, p)
    for s in range(last_lag):
        step(NB + s // per_seq, s % per_seq)


def interleaved(engine, n, unroll, turns, stages):
    lag = max(l for l, _ in stages)
    head = lag + 2 + (n - lag - 2) % unroll

    def step(s, at):
        for turn in range(turns):
            for l, parts in stages:
                if turn in parts and (not isinstance(s, int) or 0 <= s - l < n):
                    parts[turn](s - l, (at - l) % unroll)

    for s in range(head):
        step(s, s)
    with engine.Fori(0, (n - head) // unroll) as i:
        for j in range(unroll):
            step(i * unroll + (head + j), head + j)
    for s in range(n, n + lag):
        step(s, s)


def ternary_ffn(core, name, w_fc, ln_w, ln_b, w_proj):
    nc, X = core.nc, core.X
    H = w_fc.shape[0]
    HC = H // P
    WEIGHT_EPS = 1e-6
    with ExitStack() as ctx:
        ctx.callback(core.release_semaphores)
        sb = lambda n, s, d=F32: ctx.enter_context(nc.sbuf_tensor(f"{name}_{n}", s, d))
        pb = lambda n, k=1: ctx.enter_context(nc.psum_tensor(f"{name}_{n}", [P, 512 * k], F32))
        sem = lambda n: core.semaphore(f"{name}_{n}")
        wfc = sb("wfc", [P, HC, D])
        wpj = sb("wpj", [P, HC, P])
        lnw = sb("lnw", [P, HC])
        lnb = sb("lnb", [P, HC])
        lnb_wide = sb("lnb_wide", [P, HC, P])
        mean_abs = sb("mean_abs", [P, 2])
        bound = sb("bound", [P, 2, 2])
        low = sb("low", [P, H])
        wfcT = sb("wfcT", [P, H])
        wpjT = sb("wpjT", [P, HC, D])
        wpjT_raw = sb("wpjT_raw", [P, HC, D])
        offset = sb("offset", [P, D])
        st = sb("st", [P, 2, 6])
        mv = sb("mv", [P, 2, 2])
        ve = sb("ve", [P, 2])
        rs = sb("rs", [P, 2])
        xn = sb("xn", [P, 2, D])
        xnT = sb("xnT", [P, 2, P])
        g = sb("g", [P, 2, H])
        st2 = sb("st2", [P, 2, 6])
        mv2 = sb("mv2", [P, 2, 2])
        ve2 = sb("ve2", [P, 2])
        rs2 = sb("rs2", [P, 2])
        gn = sb("gn", [P, 2, H])
        gT = sb("gT", [P, 2, H])
        ps_a = [pb(f"ps_a{i}") for i in range(2)]
        ps_h = [pb(f"ps_h{i}") for i in range(2)]
        ps_t = [pb(f"ps_t{i}") for i in range(2)]
        ps_y = [pb(f"ps_y{i}") for i in range(2)]
        loaded = sem("loaded")
        held = sem("held")
        prep = sem("prep")
        prep_pe = sem("prep_pe")
        mean_done, rstd_done, x_normed, x_turned, xT_ready, hidden = (
            sem(n) for n in ("mean_done", "rstd_done", "x_normed", "x_turned", "xT_ready", "hidden"))
        gelu_done, mean2_done, rstd2_done, g_normed, g_turned, gT_ready, projected, added = (
            sem(n) for n in ("gelu_done", "mean2_done", "rstd2_done", "g_normed", "g_turned", "gT_ready", "projected", "added"))
        stats_in, stats2_in = sem("stats_in"), sem("stats2_in")
        var_in, var2_in = sem("var_in"), sem("var2_in")

        with nc.Block() as block:
            @block.sync
            def _(sp):
                sp.dma_start(wfc[:], w_fc.rearrange("(c p) d -> p c d", p=P)).then_inc(loaded, 16)
                sp.dma_start(wpj[:], w_proj.rearrange("d (c p) -> d c p", p=P)).then_inc(loaded, 16)
                with nc.allow_non_contiguous_dma(reason="small vectors"):
                    sp.dma_start(lnw[:], ln_w.rearrange("(c p) -> p c", p=P)).then_inc(loaded, 16)
                    sp.dma_start(lnb[:], ln_b.rearrange("(c p) -> p c", p=P)).then_inc(loaded, 16)

            @block.vector
            def _(dve):
                n = [0]

                def done(ins):
                    n[0] += 1
                    ins.then_inc(prep, 1)
                    dve.wait_ge(prep, n[0])
                dve.wait_ge(loaded, 64)
                for k, w in enumerate((wfc, wpj)):
                    done(nc.vector.tensor_reduce(mean_abs[:, k:k + 1], w[:], AX.XY, ALU.add, apply_absolute_value=True))
                dve.wait_ge(prep_pe, 1)
                done(nc.vector.tensor_scalar(bound[:, 0, :], ps_a[0][:, 0:2], 1.0 / (H * D), WEIGHT_EPS, ALU.mult, ALU.add))
                done(nc.vector.tensor_scalar(bound[:, 1, :], bound[:, 0, :], -0.5, None, ALU.mult))
                done(nc.vector.tensor_scalar(bound[:, 0, :], bound[:, 0, :], 0.5, None, ALU.mult))
                for k, w in enumerate((wfc, wpj)):
                    flat = w[:].rearrange("p c d -> p (c d)")
                    done(nc.vector.tensor_scalar(low[:], flat, bound[:, 1, k:k + 1], None, ALU.is_lt))
                    done(nc.vector.scalar_tensor_tensor(flat, flat, bound[:, 0, k:k + 1], low[:], ALU.is_gt, ALU.subtract))
                dve.wait_ge(prep_pe, 2)
                done(nc.vector.tensor_copy(wfcT[:], ps_h[0][:, 0:H]))
                done(nc.vector.tensor_copy(wpjT_raw[:].rearrange("p c d -> p (c d)"), ps_h[1][:, 0:H]))
                for c in range(HC):
                    done(nc.vector.tensor_scalar(wpjT[:, c, :], wpjT_raw[:, c, :], lnw[:, c:c + 1], None, ALU.mult))
                    done(nc.vector.tensor_scalar(lnb_wide[:, c, :], core.ones[:], lnb[:, c:c + 1], None, ALU.mult))
                dve.wait_ge(prep_pe, 3)
                done(nc.vector.tensor_copy(offset[:], ps_t[0][:, 0:D]))

                def token_stats(t, s):
                    wait(dve, x_normed, t - 1)
                    nc.vector.bn_stats(st[:, s, :], X[:, bass.ds(t, 1), :].rearrange("p a d -> p (a d)")).then_inc(stats_in, 1)
                    dve.wait_ge(stats_in, t + 1)
                    dve.sem_inc(held, 1)
                    nc.vector.bn_aggr(mv[:, s, :], st[:, s, :]).then_inc(var_in, 1)
                    dve.wait_ge(var_in, t + 1)
                    nc.vector.tensor_scalar(ve[:, s:s + 1], mv[:, s, 1:2], EPS, None, ALU.add).then_inc(mean_done, 1)

                def norm_x(t, s):
                    dve.wait_ge(rstd_done, t + 1)
                    wait(dve, x_turned, t - 1)
                    nc.vector.tensor_scalar(xn[:, s, :], X[:, bass.ds(t, 1), :].rearrange("p a d -> p (a d)"), mv[:, s, 0:1], rs[:, s:s + 1],
                                            ALU.subtract, ALU.mult).then_inc(x_normed, 1)

                def g_stats(t, s):
                    dve.wait_ge(gelu_done, t + 1)
                    wait(dve, g_normed, t - 1)
                    nc.vector.bn_stats(st2[:, s, :], g[:, s, :]).then_inc(stats2_in, 1)
                    dve.wait_ge(stats2_in, t + 1)
                    dve.sem_inc(held, 1)
                    nc.vector.bn_aggr(mv2[:, s, :], st2[:, s, :]).then_inc(var2_in, 1)
                    dve.wait_ge(var2_in, t + 1)
                    nc.vector.tensor_scalar(ve2[:, s:s + 1], mv2[:, s, 1:2], EPS, None, ALU.add).then_inc(mean2_done, 1)

                def norm_g(t, s):
                    dve.wait_ge(rstd2_done, t + 1)
                    wait(dve, g_turned, t - 1)
                    nc.vector.tensor_scalar(gn[:, s, :], g[:, s, :], mv2[:, s, 0:1], rs2[:, s:s + 1],
                                            ALU.subtract, ALU.mult).then_inc(g_normed, 1)

                def add(t, s):
                    dve.wait_ge(projected, t + 1)
                    xt = X[:, bass.ds(t, 1), :].rearrange("p a d -> p (a d)")
                    nc.vector.tensor_tensor(xt, ps_y[s][:, 0:D], xt, ALU.add).then_inc(added, 1)

                pipeline(dve, T, 2, [(add, 6), (norm_g, 4), (g_stats, 3), (norm_x, 1), (token_stats, 0)])

            @block.gpsimd
            def _(pool):
                def rstd(t, s):
                    pool.wait_ge(mean_done, t + 1)
                    nc.gpsimd.tensor_tensor(rs[:, s:s + 1], ve[:, s:s + 1], core.minus_half[:, 0:1], ALU.pow).then_inc(rstd_done, 1)

                def rstd2(t, s):
                    pool.wait_ge(mean2_done, t + 1)
                    nc.gpsimd.tensor_tensor(rs2[:, s:s + 1], ve2[:, s:s + 1], core.minus_half[:, 0:1], ALU.pow).then_inc(rstd2_done, 1)

                pipeline(pool, T, 2, [(rstd2, 3), (rstd, 0)])

            @block.tensor
            def _(pe):
                pe.wait_ge(prep, 2)
                nc.tensor.matmul(ps_a[0][:, 0:2], core.ones[:], mean_abs[:], start=True, stop=True).then_inc(prep_pe, 1)
                pe.wait_ge(prep, 9)
                for c in range(HC):
                    nc.tensor.transpose(ps_h[0][:, c * P:(c + 1) * P], wfc[:, c, :], core.ident[:])
                for c in range(HC):
                    last = nc.tensor.transpose(ps_h[1][:, c * P:(c + 1) * P], wpj[:, c, :], core.ident[:])
                last.then_inc(prep_pe, 1)
                pe.wait_ge(prep, 9 + 2 + 2 * HC)
                for c in range(HC):
                    last = nc.tensor.matmul(ps_t[0][:, 0:D], lnb_wide[:, c, :], wpjT_raw[:, c, :], start=(c == 0), stop=(c == HC - 1))
                last.then_inc(prep_pe, 1)
                pe.wait_ge(prep, 9 + 2 + 2 * HC + 1)

                def turn_x(t, s):
                    pe.wait_ge(x_normed, t + 1)
                    wait(pe, xT_ready, t - 1)
                    nc.tensor.transpose(ps_a[s][:, 0:P], xn[:, s, :], core.ident[:]).then_inc(x_turned, 1)

                def expand(t, s):
                    pe.wait_ge(xT_ready, t + 1)
                    wait(pe, gelu_done, t - 1)
                    nc.tensor.matmul(ps_h[s][:, 0:H], xnT[:, s, :], wfcT[:], start=True, stop=True).then_inc(hidden, 1)

                def turn_g(t, s):
                    pe.wait_ge(g_normed, t + 1)
                    wait(pe, gT_ready, t - 1)
                    for c in range(HC):
                        last = nc.tensor.transpose(ps_t[s][:, c * P:(c + 1) * P], gn[:, s, c * P:(c + 1) * P], core.ident[:])
                    last.then_inc(g_turned, 1)

                def contract(t, s):
                    pe.wait_ge(gT_ready, t + 1)
                    wait(pe, added, t - 1)
                    nc.tensor.matmul(ps_y[s][:, 0:D], core.ones[0:1, :], offset[0:1, :], start=True, stop=False)
                    for c in range(HC):
                        last = nc.tensor.matmul(ps_y[s][:, 0:D], gT[:, s, c * P:(c + 1) * P], wpjT[:, c, :], start=False, stop=(c == HC - 1))
                    last.then_inc(projected, 1)

                pipeline(pe, T, 2, [(contract, 5), (turn_g, 4), (expand, 2), (turn_x, 1)])

            @block.scalar
            def _(act):
                def copy_xT(t, s):
                    act.wait_ge(x_turned, t + 1)
                    wait(act, hidden, t - 1)
                    nc.scalar.copy(xnT[:, s, :], ps_a[s][:, 0:P]).then_inc(xT_ready, 1)

                def gelu(t, s):
                    act.wait_ge(hidden, t + 1)
                    wait(act, g_normed, t - 1)
                    nc.scalar.activation(g[:, s, :], ps_h[s][:, 0:H], ACT.Gelu).then_inc(gelu_done, 1)

                def copy_gT(t, s):
                    act.wait_ge(g_turned, t + 1)
                    wait(act, projected, t - 1)
                    nc.scalar.copy(gT[:, s, :], ps_t[s][:, 0:H]).then_inc(gT_ready, 1)

                pipeline(act, T, 2, [(copy_gT, 4), (gelu, 2), (copy_xT, 1)])


def expert_ffn(core, name, centroids, gamma, beta, W1, b1, W2, b2):
    nc, X = core.nc, core.X
    E, H = W1.shape[0], W1.shape[1]
    HC = H // P
    TC = S // P
    EXPAND, CONTRACT, ADD = E, E + 1, E + 2
    with ExitStack() as ctx:
        ctx.callback(core.release_semaphores)
        sb = lambda n, s, d=F32: ctx.enter_context(nc.sbuf_tensor(f"{name}_{n}", s, d))
        pb = lambda n, k=1: ctx.enter_context(nc.psum_tensor(f"{name}_{n}", [P, 512 * k], F32))
        sem = lambda n: core.semaphore(f"{name}_{n}")
        norm, norm2 = RowNorm(core, ctx, f"{name}_n", TC), RowNorm(core, ctx, f"{name}_m", TC)
        raw = sb("raw", [P, 2, H])
        w1T = sb("w1T", [P, E, H])
        w2T = sb("w2T", [P, E, HC, D])
        small = sb("small", [E, 3, D])
        cgb = sb("cgb", [P, 3, E])
        b1T = sb("b1T", [P, E, HC])
        b1_beta = sb("b1_beta", [P, E, HC])
        b2_rows = sb("b2_rows", [E, D])
        rank = sb("rank", [P, E])
        xn, xnT = sb("xn", [P, TC, D]), sb("xnT", [P, S])
        xn_add = sb("xn_add", [P, TC, D])
        h, hT = sb("h", [P, TC, D]), sb("hT", [P, S])
        scores, top = sb("scores", [P, TC, E]), sb("top", [P, TC])
        ranked, best = sb("ranked", [P, TC, E]), sb("best", [P, TC])
        alpha, coef_next, coef = sb("alpha", [P, TC]), sb("coef_next", [P, TC, E]), sb("coef", [P, TC, E])
        coefT = sb("coefT", [E, S])
        act_h = sb("act_h", [P, 2, HC, S])
        ps_x, ps_c = pb("ps_x"), pb("ps_c")
        ps_h = [pb(f"ps_h{i}") for i in range(4)]
        ps_y = [pb(f"ps_y{i}") for i in range(2)]
        loaded, prep, prep_pe, raw_in = sem("loaded"), sem("prep"), sem("prep_pe"), sem("raw_in")
        names = ("x_normed", "h_normed", "x_turned", "xnT_ready", "scored", "scores_done", "top_done", "ranked_done", "best_done", "alpha_done",
                 "sel_done", "coef_next_done", "coef_done", "h_turned", "hT_ready", "hidden", "relu_act", "relu_dve", "y_in", "added", "coef_turned", "coefT_ready", "bias_in", "bias_added", "skip")
        sg = {n: sem(n) for n in names}

        with nc.Block() as block:
            @block.sync
            def _(sp):
                sp.dma_start(small[:, 0, :], centroids).then_inc(loaded, 16)
                sp.dma_start(small[:, 1, :], gamma).then_inc(loaded, 16)
                sp.dma_start(small[:, 2, :], beta).then_inc(loaded, 16)
                sp.dma_start(b2_rows[:], b2).then_inc(loaded, 16)
                with nc.allow_non_contiguous_dma(reason="small vectors"):
                    for e in range(E):
                        sp.dma_start(b1T[:, e, :], b1[e].rearrange("(c p) -> p c", p=P)).then_inc(loaded, 16)
                for k in range(2 * E):
                    if k >= 2:
                        sp.wait_ge(prep_pe, k - 1 + 1)
                    src = W1[k // 2].rearrange("(c p) d -> p c d", p=P) if k % 2 == 0 else W2[k // 2]
                    dst = raw[:, k % 2].rearrange("p (c d) -> p c d", c=HC) if k % 2 == 0 else raw[:, k % 2]
                    sp.dma_start(dst, src).then_inc(raw_in, 16)
                    sp.wait_ge(raw_in, 16 * (k + 1))

            @block.tensor
            def _(pe):
                pe.wait_ge(loaded, 16 * (4 + E))
                for k in range(3):
                    last = nc.tensor.transpose(ps_x[:, k * E:(k + 1) * E], small[:, k, :], core.ident[0:E, 0:E])
                last.then_inc(prep_pe, 1)
                for k in range(2 * E):
                    pe.wait_ge(raw_in, 16 * (k + 1))
                    if k >= 2:
                        pe.wait_ge(prep, 1 + k - 1)
                    for c in range(HC):
                        last = nc.tensor.transpose(ps_h[k % 2][:, c * P:(c + 1) * P], raw[:, k % 2, c * P:(c + 1) * P], core.ident[:])
                    last.then_inc(prep_pe, 1)
                pe.wait_ge(prep, 1 + 2 * E)
                for e in range(E):
                    for c in range(HC):
                        at = (e * HC + c) * E
                        last = nc.tensor.matmul(ps_y[0][:, at:at + E], w1T[:, e, c * P:(c + 1) * P], cgb[:, 2, :], start=True, stop=True)
                last.then_inc(prep_pe, 1)
                pe.wait_ge(prep, 1 + 2 * E + 2 * E)

                def body(item):
                    front, up, down = item(0), item(EXPAND), item(CONTRACT)
                    if front:
                        b, p = front[1], front[2]
                        if p == 4:
                            pe.wait_ge(sg["x_normed"], TC * (b + 1))
                            wait(pe, sg["hT_ready"], b)
                            for c in range(TC):
                                last = nc.tensor.transpose(ps_x[:, c * P:(c + 1) * P], xn[:, c, :], core.ident[:])
                            last.then_inc(sg["x_turned"], 1)
                        if p == 5:
                            pe.wait_ge(sg["xnT_ready"], b + 1)
                            wait(pe, sg["bias_added"], b)
                            for c in range(TC):
                                last = nc.tensor.matmul(ps_c[:, c * E:(c + 1) * E], xnT[:, c * P:(c + 1) * P], cgb[:, 0, :], start=True, stop=True)
                            last.then_inc(sg["scored"], 1)
                        if p == 7:
                            pe.wait_ge(sg["h_normed"], TC * (b + 1))
                            for c in range(TC):
                                last = nc.tensor.transpose(ps_x[:, c * P:(c + 1) * P], h[:, c, :], core.ident[:])
                            last.then_inc(sg["h_turned"], 1)
                            pe.wait_ge(sg["coef_next_done"], b + 1)
                            for c in range(TC):
                                last = nc.tensor.transpose(ps_c[0:E, c * P:(c + 1) * P], coef_next[:, c, :], core.ident[:])
                            last.then_inc(sg["coef_turned"], 1)
                    if up and up[2] == 0:
                        pe.wait_ge(sg["coefT_ready"], up[1] + 1)
                        for c in range(TC):
                            last = nc.tensor.matmul(ps_c[:, c * P:(c + 1) * P], coefT[:, c * P:(c + 1) * P], b2_rows[:], start=True, stop=True)
                        last.then_inc(sg["bias_in"], 1)
                    for c in range(HC):
                        if up:
                            n, b, e = up
                            if e == 0:
                                pe.wait_ge(sg["hT_ready"], b + 1)
                            wait(pe, sg["relu_dve" if c % 2 else "relu_act"], 2 * (n - 1) + c // 2 + 1)
                            nc.tensor.matmul(ps_h[c][:], w1T[:, e, c * P:(c + 1) * P], hT[:], start=True, stop=True).then_inc(sg["hidden"], 1)
                        if down:
                            n, b, e = down
                            if c == 0:
                                pe.wait_ge(sg["relu_act"], 2 * (n + 1))
                                pe.wait_ge(sg["relu_dve"], 2 * (n + 1))
                                wait(pe, sg["added"], TC * (n - 1))
                            at = slice(c * P, (c + 1) * P)
                            out = ps_y[e % 2][:, at]
                            for k in range(HC):
                                last = nc.tensor.matmul(out, act_h[:, e % 2, k, at], w2T[:, e, k, :], start=(k == 0), stop=(k == HC - 1))
                            last.then_inc(sg["y_in"], 1)
                item_steps(pe, E, ADD, body)

            @block.scalar
            def _(act):
                def body(item):
                    front, up = item(0), item(EXPAND)
                    if front and front[2] == 4:
                        act.wait_ge(sg["x_turned"], front[1] + 1)
                        wait(act, sg["scored"], front[1])
                        nc.scalar.copy(xnT[:], ps_x[:]).then_inc(sg["xnT_ready"], 1)
                    if front and front[2] == 6:
                        act.wait_ge(sg["top_done"], front[1] + 1)
                        wait(act, sg["coef_next_done"], front[1])
                        nc.scalar.activation(alpha[:], top[:], ACT.Sigmoid).then_inc(sg["alpha_done"], 1)
                    if front and front[2] == 7:
                        act.wait_ge(sg["coef_turned"], front[1] + 1)
                        wait(act, sg["bias_in"], front[1])
                        nc.scalar.copy(coefT[:], ps_c[0:E, :]).then_inc(sg["coefT_ready"], 1)
                    if up:
                        n, b, e = up
                        if e == 0:
                            act.wait_ge(sg["h_turned"], b + 1)
                            wait(act, sg["hidden"], HC * n)
                            nc.scalar.copy(hT[:], ps_x[:]).then_inc(sg["hT_ready"], 1)
                        for c in (0, 2):
                            act.wait_ge(sg["hidden"], HC * n + c + 1)
                            wait(act, sg["y_in"], TC * (n - 1))
                            nc.scalar.activation(act_h[:, e % 2, c, :], ps_h[c][:], ACT.Relu, bias=b1_beta[:, e, c:c + 1]).then_inc(sg["relu_act"], 1)
                item_steps(act, E, ADD, body)

            @block.gpsimd
            def _(pool):
                def body(item):
                    front = item(0)
                    if front:
                        b, p = front[1], front[2]
                        if p == 0 or p == 2:
                            for c in range(TC):
                                (norm if p == 0 else norm2).rstd(pool, TC * b + c, c)
                item_steps(pool, E, ADD, body)

            @block.vector
            def _(dve):
                for e in range(E):
                    nc.vector.memset(rank[:, e:e + 1], float(E - e))
                dve.wait_ge(prep_pe, 1)
                nc.vector.tensor_copy(cgb[:].rearrange("p k e -> p (k e)"), ps_x[:, 0:3 * E]).then_inc(prep, 1)
                for k in range(2 * E):
                    dve.wait_ge(prep_pe, k + 2)
                    dst = w1T[:, k // 2, :] if k % 2 == 0 else w2T[:, k // 2].rearrange("p c d -> p (c d)")
                    nc.vector.tensor_copy(dst, ps_h[k % 2][:]).then_inc(prep, 1)
                dve.wait_ge(prep_pe, 2 + 2 * E)
                dve.wait_ge(prep, 1 + 2 * E)
                for e in range(E):
                    beta_part = ps_y[0][:, e * HC * E:(e + 1) * HC * E].rearrange("p (c f) -> p c f", f=E)[:, :, e]
                    nc.vector.tensor_tensor(b1_beta[:, e, :], beta_part, b1T[:, e, :], ALU.add).then_inc(prep, 1)
                    nc.vector.tensor_scalar(w1T[:, e, :], w1T[:, e, :], cgb[:, 1, e:e + 1], None, ALU.mult).then_inc(prep, 1)
                dve.wait_ge(prep, 1 + 4 * E)

                wide = lambda m: m.unsqueeze(2).broadcast_to([P, TC, E])

                def front_part(b, p):
                    for q, nrm in ((0, norm), (2, norm2)):
                        if p == q:
                            for c in range(TC):
                                if q == 2:
                                    dve.wait_ge(sg["x_normed"], TC * (b + 1))
                                nrm.stats(dve, TC * b + c, c, tile_of(X, TC * b + c) if q == 0 else xn[:, c, :])
                    if p == 1:
                        wait(dve, sg["x_turned"], b)
                        wait(dve, sg["skip"], b)
                        for c in range(TC):
                            dve.wait_ge(norm.rstd_done, TC * b + c + 1)
                            norm.apply(xn[:, c, :], tile_of(X, TC * b + c), c).then_inc(sg["x_normed"], 1)
                    if p == 3:
                        wait(dve, sg["h_turned"], b)
                        for c in range(TC):
                            dve.wait_ge(norm2.rstd_done, TC * b + c + 1)
                            norm2.apply(h[:, c, :], xn[:, c, :], c).then_inc(sg["h_normed"], 1)
                    if p == 6:
                        dve.wait_ge(sg["scored"], b + 1)
                        wait(dve, sg["coef_next_done"], b)
                        nc.vector.tensor_copy(scores[:].rearrange("p c e -> p (c e)"), ps_c[:, 0:TC * E]).then_inc(sg["scores_done"], 1)
                        dve.wait_ge(sg["scores_done"], b + 1)
                        nc.vector.tensor_reduce(top[:], scores[:], AX.X, ALU.max).then_inc(sg["top_done"], 1)
                        dve.wait_ge(sg["top_done"], b + 1)
                        nc.vector.tensor_tensor(ranked[:], scores[:], wide(top[:]), ALU.is_equal).then_inc(sg["ranked_done"], 1)
                        dve.wait_ge(sg["ranked_done"], 2 * b + 1)
                        nc.vector.tensor_tensor(ranked[:], ranked[:], rank[:].unsqueeze(1).broadcast_to([P, TC, E]), ALU.mult)\
                            .then_inc(sg["ranked_done"], 1)
                        dve.wait_ge(sg["ranked_done"], 2 * b + 2)
                        nc.vector.tensor_reduce(best[:], ranked[:], AX.X, ALU.max).then_inc(sg["best_done"], 1)
                        dve.wait_ge(sg["best_done"], b + 1)
                        wait(dve, sg["coef_done"], b)
                        nc.vector.tensor_tensor(coef_next[:], ranked[:], wide(best[:]), ALU.is_equal).then_inc(sg["sel_done"], 1)
                        dve.wait_ge(sg["sel_done"], b + 1)
                        dve.wait_ge(sg["alpha_done"], b + 1)
                        nc.vector.tensor_tensor(coef_next[:], coef_next[:], wide(alpha[:]), ALU.mult).then_inc(sg["coef_next_done"], 1)

                def body(item):
                    front, up, down, add = item(0), item(EXPAND), item(CONTRACT), item(ADD)
                    if down and down[2] == 0:
                        b = down[1]
                        xb = X[:, bass.ds(b * TC, TC), :]
                        nc.vector.tensor_tensor(xb, xb, xn[:], ALU.add).then_inc(sg["skip"], 1)
                        dve.wait_ge(sg["skip"], b + 1)
                        dve.wait_ge(sg["bias_in"], b + 1)
                        flat = xb.rearrange("p c d -> p (c d)")
                        nc.vector.tensor_tensor(flat, ps_c[:], flat, ALU.add).then_inc(sg["bias_added"], 1)
                    if front:
                        front_part(front[1], front[2])
                    if add and add[2] == 0:
                        b = add[1]
                        wait(dve, sg["added"], E * TC * b)
                        dve.wait_ge(sg["coef_next_done"], b + 1)
                        nc.vector.tensor_copy(coef[:], coef_next[:]).then_inc(sg["coef_done"], 1)
                        dve.wait_ge(sg["coef_done"], b + 1)
                        dve.wait_ge(sg["bias_added"], b + 1)
                    for c in range(HC):
                        if up and c % 2:
                            n, b, e = up
                            dve.wait_ge(sg["hidden"], HC * n + c + 1)
                            wait(dve, sg["y_in"], TC * (n - 1))
                            nc.vector.tensor_scalar(act_h[:, e % 2, c, :], ps_h[c][:], b1_beta[:, e, c:c + 1], 0.0, ALU.add, ALU.max)\
                                .then_inc(sg["relu_dve"], 1)
                        if add:
                            n, b, e = add
                            dve.wait_ge(sg["y_in"], TC * (n + 1))
                            wait(dve, sg["added"], TC * (n - 1) + c + 1)
                            xt = tile_of(X, b * TC + c)
                            nc.vector.scalar_tensor_tensor(xt, ps_y[e % 2][:, c * P:(c + 1) * P], coef[:, c, e:e + 1], xt, ALU.mult, ALU.add)\
                                .then_inc(sg["added"], 1)
                item_steps(dve, E, ADD, body)


def ssm_tables():
    p = np.arange(P)
    same = (p[:, None] // 16 == p[None, :] // 16).astype(np.float32)
    j, t = np.arange(16)[:, None], np.arange(16)[None, :]
    shift = (t[None] - (p % 16)[:, None, None] == j[None]).astype(np.float32)
    return same, shift.reshape(P, 256)


def channel_ssm(core, name, A, Bp, Cp, Dp, Wg, bg, gamma, beta, same_in, shift_in):
    nc, X = core.nc, core.X
    C = 16
    G, DG = 16, D // 16
    NCH = S // C
    LV = 5
    J = NB * NCH // P
    KM = LV + 3
    xg_dram = nc.dram_tensor(f"{name}_xg", (T * P, D), F32, kind="Internal").ap()
    y_dram = nc.dram_tensor(f"{name}_y", (T * P, D), F32, kind="Internal").ap()

    with ExitStack() as ctx:
        ctx.callback(core.release_semaphores)
        sb = lambda n, s, d=F32: ctx.enter_context(nc.sbuf_tensor(f"{name}_{n}", s, d))
        pb = lambda n: ctx.enter_context(nc.psum_tensor(f"{name}_{n}", [P, 512], F32))
        sem = lambda n: core.semaphore(f"{name}_{n}")
        norm = RowNorm(core, ctx, f"{name}_n1", 4)
        wg, wgT, bgr = sb("wg", [P, D]), sb("wgT", [P, D]), sb("bgr", [1, D])
        xn, xnT, gate, xg = sb("xn", [P, 4, D]), sb("xnT", [P, 2, P]), sb("gate", [P, 2, D]), sb("xgb", [P, 4, D])
        ps_t, ps_z = [pb(f"pt{i}") for i in range(2)], [pb(f"pz{i}") for i in range(2)]
        loaded, prep, x_normed, x_turned, xT_ready, gate_in, gated, product, stored = (
            sem(n) for n in ("loaded", "prep", "x_normed", "x_turned", "xT_ready", "gate_in", "gated", "product", "stored"))
        sent = [sem(f"sent{i}") for i in range(4)]
        with nc.Block() as block:
            @block.sync
            def _(sp):
                sp.dma_start(wg[:], Wg).then_inc(loaded, 16)
                sp.dma_start(bgr[:], bg.rearrange("(a d) -> a d", a=1)).then_inc(loaded, 16)
                rows = xg_dram.rearrange("(n p) d -> n p d", p=P)

                def send(t, s):
                    sp.wait_ge(product, t + 1)
                    sp.dma_start(rows[bass.ds(t, 1), :, :].rearrange("a p d -> (a p) d"), xg[:, s, :]).then_inc(sent[s], 16)
                pipeline(sp, T, 4, [(send, 4)])
                for s in range(4):
                    sp.wait_ge(sent[s], 16 * (T // 4))

            @block.vector
            def _(dve):
                dve.wait_ge(prep, 1)
                nc.vector.tensor_copy(wgT[:], ps_t[0][:, 0:D]).then_inc(prep, 1)
                dve.wait_ge(prep, 2)

                def stats(t, s):
                    wait(dve, x_normed, t - 3)
                    norm.stats(dve, t, s, tile_of(X, t))

                def norm_x(t, s):
                    dve.wait_ge(norm.rstd_done, t + 1)
                    wait(dve, product, t - 3)
                    norm.apply(xn[:, s, :], tile_of(X, t), s).then_inc(x_normed, 1)

                def multiply(t, s):
                    dve.wait_ge(gated, t + 1)
                    if isinstance(t, int) and t < 4:
                        pass
                    else:
                        dve.wait_ge(sent[s], (t - s) * 4)
                    nc.vector.tensor_tensor(xg[:, s, :], xn[:, s, :], gate[:, s % 2, :], ALU.mult).then_inc(product, 1)
                pipeline(dve, T, 4, [(multiply, 3), (norm_x, 1), (stats, 0)])

            @block.gpsimd
            def _(pool):
                pipeline(pool, T, 4, [(lambda t, s: norm.rstd(pool, t, s), 0)])

            @block.tensor
            def _(pe):
                pe.wait_ge(loaded, 32)
                nc.tensor.transpose(ps_t[0][:, 0:D], wg[:], core.ident[:]).then_inc(prep, 1)
                pe.wait_ge(prep, 2)

                def turn(t, s):
                    pe.wait_ge(x_normed, t + 1)
                    wait(pe, xT_ready, t - 1)
                    nc.tensor.transpose(ps_t[s % 2][:, 0:P], xn[:, s, :], core.ident[:]).then_inc(x_turned, 1)

                def gates(t, s):
                    pe.wait_ge(xT_ready, t + 1)
                    wait(pe, gated, t - 1)
                    nc.tensor.matmul(ps_z[s % 2][:, 0:D], core.ones[0:1, :], bgr[:], start=True, stop=False)
                    nc.tensor.matmul(ps_z[s % 2][:, 0:D], xnT[:, s % 2, :], wgT[:], start=False, stop=True).then_inc(gate_in, 1)
                pipeline(pe, T, 4, [(gates, 2), (turn, 1)])

            @block.scalar
            def _(act):
                def copy_xT(t, s):
                    act.wait_ge(x_turned, t + 1)
                    wait(act, gate_in, t - 1)
                    nc.scalar.copy(xnT[:, s % 2, :], ps_t[s % 2][:, 0:P]).then_inc(xT_ready, 1)

                def sigmoid(t, s):
                    act.wait_ge(gate_in, t + 1)
                    wait(act, product, t - 1)
                    nc.scalar.activation(gate[:, s % 2, :], ps_z[s % 2][:, 0:D], ACT.Sigmoid).then_inc(gated, 1)
                pipeline(act, T, 4, [(sigmoid, 2), (copy_xT, 1)])

    with ExitStack() as ctx:
        ctx.callback(core.release_semaphores)
        sb = lambda n, s, d=F32: ctx.enter_context(nc.sbuf_tensor(f"{name}_{n}", s, d))
        sem = lambda n: core.semaphore(f"{name}_r_{n}")
        mats = sb("mats", [P, G, KM, P])
        xc = sb("xc", [P, J, C, D])
        same, shift = sb("same", [P, P]), sb("shift", [P, C, C])
        TOEP, INTO, OUT = LV, LV + 1, LV + 2
        psum = [ctx.enter_context(nc.psum_tensor(f"{name}_b{i}", [P, 512], F32)) for i in range(8)]
        loaded, xc_loaded = sem("ld2"), sem("xc_loaded")
        with ExitStack() as c2:
            sb2 = lambda n, s, d=F32: c2.enter_context(nc.sbuf_tensor(f"{name}_{n}", s, d))
            a0, bp, cp, dp1 = sb2("a0", [P, G, C]), sb2("bp", [P, G]), sb2("cp", [P, G]), sb2("dp1", [P, G])
            pw = sb2("pw", [P, 2, G, P])
            pwT = sb2("pwT", [P, 2, G, P])
            aT = sb2("aT", [P, G, P])
            vb, wc, wc1 = sb2("vb", [P, G, C]), sb2("wc", [P, G, C]), sb2("wc1", [P, G, C])
            bw, taps = sb2("bw", [P, G, C]), sb2("taps", [P, G, C])
            t0, term = sb2("t0", [P, G, C]), sb2("term", [P, G, C])
            dve_step, pe_step = sem("dve_step"), sem("pe_step")
            with nc.Block() as block:
                @block.sync
                def _(sp):
                    with nc.allow_non_contiguous_dma(reason="small weights"):
                        for d in range(DG):
                            at = slice(d * C, (d + 1) * C)
                            sp.dma_start(a0[at, :, :], A.rearrange("(g d) n m -> d n g m", d=DG)[d]).then_inc(loaded, 16)
                            sp.dma_start(bp[at, :], Bp.rearrange("(g d) n -> d n g", d=DG)[d]).then_inc(loaded, 16)
                            sp.dma_start(cp[at, :], Cp.rearrange("(g d) n -> d n g", d=DG)[d]).then_inc(loaded, 16)
                            sp.dma_start(dp1[at, :], Dp.rearrange("(g d) -> d g", d=DG)[d:d + 1, :].broadcast_to([C, G])).then_inc(loaded, 16)
                        sp.dma_start(same[:], same_in).then_inc(loaded, 16)
                        sp.dma_start(shift[:].rearrange("p j t -> p (j t)"), shift_in).then_inc(loaded, 16)
                    chunks = xg_dram.rearrange("(j p c) d -> p j (c d)", p=P, c=C)
                    for j in range(J):
                        sp.dma_start(xc[:, j, :, :].rearrange("p c d -> p (c d)"), chunks[:, j, :]).then_inc(xc_loaded, 16)
                    sp.wait_ge(xc_loaded, 16 * J)

                def wide(m):
                    return m.unsqueeze(2).broadcast_to([P, G, DG, C])
                same_wide = same[:].rearrange("p (d c) -> p d c", d=DG).unsqueeze(1).broadcast_to([P, G, DG, C])

                @block.vector
                def _(dve):
                    n = [0]

                    def done(ins):
                        n[0] += 1
                        ins.then_inc(dve_step, 1)
                        dve.wait_ge(dve_step, n[0])

                    def expand(out, m):
                        for g0 in range(0, G, 4):
                            done(nc.vector.tensor_tensor(out[:, g0:g0 + 4, :].rearrange("p g (d c) -> p g d c", d=DG),
                                                         wide(m[:])[:, g0:g0 + 4], same_wide[:, g0:g0 + 4], ALU.mult))
                    rounds = [0]

                    def pe_done():
                        rounds[0] += 1
                        dve.wait_ge(pe_step, rounds[0])
                    dve.wait_ge(loaded, 16 * (4 * DG + 2))
                    expand(pw[:, 0], a0)
                    done(nc.vector.tensor_copy(vb[:, :, C - 1], bp[:]))
                    done(nc.vector.tensor_copy(wc[:, :, 0], cp[:]))
                    done(nc.vector.tensor_scalar(dp1[:], dp1[:], 1.0, None, ALU.add))
                    pe_done()
                    for q in range(4):
                        done(nc.vector.tensor_copy(aT[:, 4 * q:4 * q + 4, :].rearrange("p g c -> p (g c)"), psum[q][:]))
                    k, cur = 1, 0
                    for level in range(8):
                        pe_done()
                        nxt = 1 - cur
                        for q in range(4):
                            dst = pw[:, nxt] if level < 3 else mats[:, :, level - 3, :]
                            done(nc.vector.tensor_copy(dst[:, 4 * q:4 * q + 4, :], psum[q][:].rearrange("p (g c) -> p g c", g=4)))
                        pe_done()
                        for q in range(4):
                            done(nc.vector.tensor_copy(pwT[:, nxt, 4 * q:4 * q + 4, :], psum[4 + q][:].rearrange("p (g c) -> p g c", g=4)))
                        if k < C:
                            pe_done()
                            done(nc.vector.tensor_copy(vb[:, :, C - 2 * k:C - k], psum[0][:, 0:G * k].rearrange("p (g c) -> p g c", g=G)))
                            done(nc.vector.tensor_copy(wc[:, :, k:2 * k], psum[1][:, 0:G * k].rearrange("p (g c) -> p g c", g=G)))
                        k, cur = 2 * k, nxt
                    pe_done()
                    done(nc.vector.tensor_copy(wc1[:], psum[0][:, 0:G * C].rearrange("p (g c) -> p g c", g=G)))
                    done(nc.vector.tensor_tensor(bw[:], wc[:], bp[:].unsqueeze(2).broadcast_to([P, G, C]), ALU.mult))
                    pe_done()
                    done(nc.vector.tensor_copy(taps[:], psum[1][:, 0:G * C].rearrange("p (g c) -> p g c", g=G)))
                    for j in range(C):
                        tap = taps[:, :, j:j + 1].broadcast_to([P, G, C])
                        sh = shift[:, j:j + 1, :].broadcast_to([P, G, C])
                        done(nc.vector.tensor_tensor(t0[:] if j == 0 else term[:], tap, sh, ALU.mult))
                        if j:
                            done(nc.vector.tensor_tensor(t0[:], t0[:], term[:], ALU.add))
                    expand(mats[:, :, TOEP, :], t0)
                    for g in range(G):
                        done(nc.vector.scalar_tensor_tensor(mats[:, g, TOEP, :], core.ident[:], dp1[:, g:g + 1], mats[:, g, TOEP, :],
                                                            ALU.mult, ALU.add))
                    expand(mats[:, :, OUT, :], wc1)
                    expand(pw[:, 0], vb)
                    pe_done()
                    for q in range(4):
                        done(nc.vector.tensor_copy(mats[:, 4 * q:4 * q + 4, INTO, :], psum[q][:].rearrange("p (g c) -> p g c", g=4)))

                @block.tensor
                def _(pe):
                    n = [0]

                    def need(k):
                        n[0] += k
                        pe.wait_ge(dve_step, n[0])
                    need(7)
                    for g in range(G):
                        last = nc.tensor.transpose(psum[g // 4][:, g % 4 * P:g % 4 * P + P], pw[:, 0, g, :], core.ident[:])
                    last.then_inc(pe_step, 1)
                    need(4)
                    k, cur = 1, 0
                    for level in range(8):
                        now = pw[:, cur] if level < 4 else mats[:, :, level - 4, :]
                        nowT = pwT[:, cur] if level else aT[:]
                        for g in range(G):
                            last = nc.tensor.matmul(psum[g // 4][:, g % 4 * P:g % 4 * P + P], nowT[:, g, :], now[:, g, :], start=True, stop=True)
                        last.then_inc(pe_step, 1)
                        for g in range(G):
                            last = nc.tensor.matmul(psum[4 + g // 4][:, g % 4 * P:g % 4 * P + P], now[:, g, :], nowT[:, g, :], start=True, stop=True)
                        last.then_inc(pe_step, 1)
                        need(8)
                        if k < C:
                            for g in range(G):
                                nc.tensor.matmul(psum[0][:, g * k:(g + 1) * k], now[:, g, :], vb[:, g, C - k:C], start=True, stop=True)
                            for g in range(G):
                                last = nc.tensor.matmul(psum[1][:, g * k:(g + 1) * k], nowT[:, g, :], wc[:, g, 0:k], start=True, stop=True)
                            last.then_inc(pe_step, 1)
                            need(2)
                        k, cur = 2 * k, 1 - cur
                    for g in range(G):
                        last = nc.tensor.matmul(psum[0][:, g * C:(g + 1) * C], aT[:, g, :], wc[:, g, :], start=True, stop=True)
                    last.then_inc(pe_step, 1)
                    need(2)
                    nc.tensor.matmul(psum[1][:, 0:G * C], same[:], bw[:].rearrange("p g c -> p (g c)"), start=True, stop=True).then_inc(pe_step, 1)
                    need(1 + 1 + 2 * (C - 1) + 4 + G + 4 + 4)
                    for g in range(G):
                        last = nc.tensor.transpose(psum[g // 4][:, g % 4 * P:g % 4 * P + P], pw[:, 0, g, :], core.ident[:])
                    last.then_inc(pe_step, 1)

        with ExitStack() as c2:
            sb2 = lambda n, s, d=F32: c2.enter_context(nc.sbuf_tensor(f"{name}_{n}", s, d))
            cur = sb2("cur", [P, 2, 2, KM, P])
            xin = sb2("xin", [P, 2, 2, J, P])
            xT = sb2("xT", [P, 2, 2, J * P])
            u = sb2("u", [P, 2, J * P])
            y = sb2("yout", [P, 2, J * P])
            ps_x, ps_u, ps_y, ps_z = psum[0:2], psum[2:4], psum[4:6], psum[6:8]
            staged, turned, xT_ready, state_in, state_out, y_in, y_out, z_in, z_out, first = (
                sem(n) for n in ("staged", "turned", "xT_ready", "state_in", "state_out", "y_in", "y_out", "z_in", "z_out", "first"))
            state_out = [sem("state_out_a"), sem("state_out_b")]
            y_out = [sem("y_out_a"), sem("y_out_b")]
            z_out = [sem("z_out_a"), sem("z_out_b")]
            PAIRS = G // 2
            with nc.Block() as block:
                @block.gpsimd
                def _(pool):
                    def stage(i, s):
                        wait(pool, z_in, 2 * (i - 1))
                        nc.gpsimd.tensor_copy(cur[:, s].rearrange("p h k c -> p (h k c)"),
                                              mats[:, bass.ds(i * 2, 2), :, :].rearrange("p h k c -> p (h k c)")).then_inc(staged, 1)
                        for h in range(2):
                            chans = xc[:, :, :, bass.ds(i * 2 * DG + h * DG, DG)].rearrange("p j c d -> p j d c")
                            nc.gpsimd.tensor_copy(xin[:, s, h, :, :].rearrange("p j (d c) -> p j d c", d=DG), chans).then_inc(staged, 1)
                    pipeline(pool, PAIRS, 2, [(stage, 0)])

                @block.tensor
                def _(pe):
                    def turn(i, s):
                        pe.wait_ge(staged, 3 * (i + 1))
                        wait(pe, xT_ready, i)
                        for h in range(2):
                            for j in range(J):
                                last = nc.tensor.transpose(ps_x[h][:, j * P:(j + 1) * P], xin[:, s, h, j, :], core.ident[:])
                        last.then_inc(turned, 1)

                    def recur(i, s):
                        pe.wait_ge(xT_ready, i + 1)
                        for h in range(2):
                            wait(pe, state_out[h], (LV + 1) * i)
                            nc.tensor.matmul(ps_u[h][:], cur[:, s, h, INTO, :], xT[:, s, h, :], start=True, stop=False,
                                             skip_group_check=True).then_inc(state_in, 1)
                        for l in range(LV):
                            for h in range(2):
                                pe.wait_ge(state_out[h], (LV + 1) * i + l + 1)
                                ub = u[:, h, :].rearrange("p (b c) -> p b c", c=NCH)
                                pb_ = ps_u[h][:].rearrange("p (b c) -> p b c", c=NCH)
                                nc.tensor.matmul(pb_[:, :, 2 ** l:], cur[:, s, h, l, :], ub[:, :, 0:NCH - 2 ** l], start=False, stop=(l == LV - 1),
                                                 skip_group_check=True).then_inc(state_in, 1)
                        for h in range(2):
                            wait(pe, y_out[h], i)
                            nc.tensor.matmul(ps_y[h][:], cur[:, s, h, TOEP, :], xT[:, s, h, :], start=True, stop=False, skip_group_check=True)
                            pe.wait_ge(state_out[h], (LV + 1) * (i + 1))
                            ub = u[:, h, :].rearrange("p (b c) -> p b c", c=NCH)
                            yb = ps_y[h][:].rearrange("p (b c) -> p b c", c=NCH)
                            nc.tensor.matmul(yb[:, :, 1:], cur[:, s, h, OUT, :], ub[:, :, 0:NCH - 1], start=False, stop=True,
                                             skip_group_check=True).then_inc(y_in, 1)
                        for h in range(2):
                            pe.wait_ge(y_out[h], i + 1)
                            wait(pe, z_out[h], i)
                            for j in range(J):
                                last = nc.tensor.transpose(ps_z[h][:, j * P:(j + 1) * P], y[:, h, j * P:(j + 1) * P], core.ident[:])
                            last.then_inc(z_in, 1)
                    pipeline(pe, PAIRS, 2, [(recur, 1), (turn, 0)])

                def drain_half(eng, op, h):
                    def front(i, s):
                        eng.wait_ge(turned, i + 1)
                        wait(eng, z_in, 2 * (i - 1))
                        op(xT[:, s, h, :], ps_x[h][:]).then_inc(half_x[h], 1)
                        if h == 0:
                            eng.wait_ge(half_x[1], i + 1)
                            eng.wait_ge(half_x[0], i + 1)
                            eng.sem_inc(xT_ready, 1)

                    def rest(i, s):
                        for l in range(LV + 1):
                            eng.wait_ge(state_in, 2 * (LV + 1) * i + 2 * l + h + 1)
                            if l == 0:
                                wait(eng, y_in, 2 * i)
                            op(u[:, h, :], ps_u[h][:]).then_inc(state_out[h], 1)
                        eng.wait_ge(y_in, 2 * i + h + 1)
                        wait(eng, z_in, 2 * i)
                        op(y[:, h, :], ps_y[h][:]).then_inc(y_out[h], 1)
                        eng.wait_ge(z_in, 2 * i + h + 1)
                        out = xc[:, :, :, bass.ds(i * 2 * DG + h * DG, DG)].rearrange("p j c d -> p j d c")
                        op(out, ps_z[h][:].rearrange("p (j d c) -> p j d c", j=J, d=DG)).then_inc(z_out[h], 1)
                    pipeline(eng, PAIRS, 2, [(rest, 1), (front, 0)])
                half_x = [sem("half_xa"), sem("half_xb")]

                @block.scalar
                def _(act):
                    drain_half(act, nc.scalar.copy, 0)

                @block.vector
                def _(dve):
                    drain_half(dve, nc.vector.tensor_copy, 1)

        y_stored = sem("y_stored")
        with nc.Block() as block:
            @block.sync
            def _(sp):
                chunks = y_dram.rearrange("(j p c) d -> p j (c d)", p=P, c=C)
                for j in range(J):
                    sp.dma_start(chunks[:, j, :], xc[:, j, :, :].rearrange("p c d -> p (c d)")).then_inc(y_stored, 16)
                sp.wait_ge(y_stored, 16 * J)

    with ExitStack() as ctx:
        ctx.callback(core.release_semaphores)
        sb = lambda n, s, d=F32: ctx.enter_context(nc.sbuf_tensor(f"{name}_{n}", s, d))
        sem = lambda n: core.semaphore(f"{name}_y_{n}")
        norm = RowNorm(core, ctx, f"{name}_n3", 4)
        yn = sb("yn", [P, T, D])
        gam, bet = sb("gam", [P, D]), sb("bet", [P, D])
        scaled, shifted = sb("scaled", [P, 4, D]), sb("shifted", [P, 4, D])
        loaded, normed, scaled_done, shifted_done, added = (
            sem(n) for n in ("ld3", "normed3", "scaled3", "shifted3", "added3"))
        arrived = [sem(f"yn{q}") for q in range(4)]
        with nc.Block() as block:
            @block.sync
            def _(sp):
                sp.dma_start(gam[:], gamma.rearrange("(a d) -> a d", a=1).broadcast_to([P, D])).then_inc(loaded, 16)
                sp.dma_start(bet[:], beta.rearrange("(a d) -> a d", a=1).broadcast_to([P, D])).then_inc(loaded, 16)
                rows = y_dram.rearrange("(n p) d -> p n d", p=P)
                for q in range(4):
                    sp.dma_start(yn[:, q * 16:(q + 1) * 16, :], rows[:, q * 16:(q + 1) * 16, :]).then_inc(arrived[q], 16)

            @block.vector
            def _(dve):
                for q in range(4):
                    dve.wait_ge(arrived[q], 16)

                def stats(t, s):
                    wait(dve, normed, t - 3)
                    norm.stats(dve, t, s, tile_of(yn, t))

                def apply(t, s):
                    dve.wait_ge(norm.rstd_done, t + 1)
                    norm.apply(tile_of(yn, t), tile_of(yn, t), s).then_inc(normed, 1)

                def add(t, s):
                    dve.wait_ge(shifted_done, t + 1)
                    nc.vector.tensor_tensor(tile_of(X, t), tile_of(X, t), shifted[:, s, :], ALU.add).then_inc(added, 1)
                pipeline(dve, T, 4, [(add, 3), (apply, 1), (stats, 0)])

            @block.gpsimd
            def _(pool):
                pool.wait_ge(loaded, 32)

                def scale(t, s):
                    pool.wait_ge(normed, t + 1)
                    wait(pool, shifted_done, t - 3)
                    nc.gpsimd.tensor_tensor(scaled[:, s, :], tile_of(yn, t), gam[:], ALU.mult).then_inc(scaled_done, 1)

                def shift_(t, s):
                    pool.wait_ge(scaled_done, t + 1)
                    wait(pool, added, t - 3)
                    nc.gpsimd.tensor_tensor(shifted[:, s, :], scaled[:, s, :], bet[:], ALU.add).then_inc(shifted_done, 1)
                pipeline(pool, T, 4, [(shift_, 2), (scale, 1), (lambda t, s: norm.rstd(pool, t, s), 0)])


def slot_tables():
    p = np.arange(P)
    part = (p[:, None] // 32 == np.arange(4)[None, :]).astype(np.float32)
    causal = ((p[:, None] // 32 == p[None, :] // 32) & (p[None, :] >= p[:, None])).astype(np.float32)
    go_on = np.tile((np.arange(S) % 32 != 0).astype(np.float32), (P, 1))
    return part, causal, go_on


def gated_slots(core, name, Wq, Wk, Wv, Wf, g_w, Wo, part_in, causal_in, go_on_in):
    nc, X = core.nc, core.X
    H, K = 4, 32
    BL = 32
    NBK = S // BL
    TC = S // P
    NORM = 1.0 / 8.0
    TURNS = 24
    LIMIT = 80.0 / NORM
    with ExitStack() as ctx:
        ctx.callback(core.release_semaphores)
        sb = lambda n, s, d=F32: ctx.enter_context(nc.sbuf_tensor(f"{name}_{n}", s, d))
        pb = lambda n, k=1: ctx.enter_context(nc.psum_tensor(f"{name}_{n}", [P, 512 * k], F32))
        sem = lambda n: core.semaphore(f"{name}_{n}")
        norm = RowNorm(core, ctx, f"{name}_n", 4)
        w_raw, wT = sb("w_raw", [P, 5, D]), sb("wT", [P, 5, D])
        gw = sb("gw", [P, 1])
        part, causal, go_on = sb("part", [P, 4]), sb("causal", [P, P]), sb("go_on", [P, S])
        xn, xT = sb("xn", [P, TC, D]), sb("xT", [P, S])
        r = sb("r", [P, S])
        qkT = sb("qkT", [P, 3, 2, S])
        vT = sb("vT", [P, S])
        za, zl = sb("za", [P, S]), sb("zl", [P, S])
        f, gs = sb("f", [P, S]), sb("gs", [P, S])
        dk, dq, ek, sT = sb("dk", [P, S]), sb("dq", [P, S]), sb("ek", [P, S]), sb("sT", [P, S])
        eqT = sb("eqT", [P, 3, S])
        bT = sb("bT", [P, 3, S])
        e_mid, e_last = sb("e_mid", [P, 3, NBK]), sb("e_last", [P, 3, NBK])
        decay = sb("decay", [P, 3, K, NBK])
        bn, eqn = sb("bn", [P, 3, S]), sb("eqn", [P, 3, S])
        kn, vn = sb("kn", [P, S]), sb("vn", [P, 3, S])
        kx, vx = sb("kx", [P, TC, H, 4, K]), sb("vx", [P, TC, H, 4, K])
        qm = sb("qm", [P, H, S])
        am1, am2 = sb("am1", [P, TC, H, P]), sb("am2", [P, TC, H, P])
        ds, send = sb("ds", [P, K, NBK]), sb("send", [P, K, NBK])
        s1, s1T = sb("s1", [P, NBK, K]), sb("s1T", [P, NBK, K])
        sbd = sb("sbd", [P, NBK, H, K])
        ok, mx, ex, sm_, rc, qv = sb("ok", [P, S]), sb("mx", [P, TC * H]), sb("ex", [P, S]), sb("sum", [P, TC * H]), sb("rc", [P, TC * H]), sb("qv", [P, S])
        q2T, q2m = sb("q2T", [P, S]), sb("q2m", [P, H, S])
        s2, sbd2 = sb("s2", [P, NBK, K]), sb("sbd2", [P, NBK, H, K])
        ro, o, osq, ss, var, rs, on, onT = (sb("ro", [P, S]), sb("o", [P, S]), sb("osq", [P, TC, P]), sb("ss", [P, TC]),
                                            sb("var", [P, TC]), sb("rs", [P, TC]), sb("on", [P, S]), sb("onT", [P, S]))
        ps_q, ps_z, ps_t, ps_s, ps_a1, ps_a2, ps_o1, ps_o2 = (pb(f"ps_{n}") for n in ("q", "z", "t", "s", "a1", "a2", "o1", "o2"))
        loaded, prep = sem("loaded"), sem("prep")
        names = ("x_normed", "x_turned", "xT_ready", "qkv_in", "z_in", "r_done", "silu_done", "abs_done", "ze_done",
                 "log_done", "f_done", "g_done", "dk_done", "d_done", "exp_done", "s_done", "bT_done", "turned", "copied",
                 "decay_done", "kx_done", "vx_done", "qm_done", "a_in", "am_done", "s_in", "ds_done", "send_done", "s1_done",
                 "s1T_done", "sbd_done", "ok_in", "ok_done", "mx_done", "sub_done", "ex_done", "sum_done", "rc_done", "qv_done",
                 "qv_turned", "q2_done", "q2m_done", "a2_in", "am2_done", "s2_in", "ds2_done", "send2_done", "s2_done", "sbd2_done",
                 "ov_in", "ro_done", "o_done", "ss_done", "var_done", "rs_done", "on_done", "on_turned",
                 "onT_ready", "y_in", "added")
        sg = {n: sem(n) for n in names}

        def blocks(m):
            return m.rearrange("p (j t) -> p j t", t=BL)

        with nc.Block() as block:
            @block.sync
            def _(sp):
                for n, w in enumerate((Wq, Wk, Wv, Wf, Wo)):
                    sp.dma_start(w_raw[:, n, :], w).then_inc(loaded, 16)
                with nc.allow_non_contiguous_dma(reason="small vector"):
                    sp.dma_start(gw[:], g_w.rearrange("(p a) -> p a", a=1)).then_inc(loaded, 16)
                sp.dma_start(part[:], part_in).then_inc(loaded, 16)
                sp.dma_start(causal[:], causal_in).then_inc(loaded, 16)
                sp.dma_start(go_on[:], go_on_in).then_inc(loaded, 16)

            @block.tensor
            def _(pe):
                pe.wait_ge(loaded, 144)
                for n in range(5):
                    last = nc.tensor.transpose((ps_a1 if n < 4 else ps_t)[:, n % 4 * P:n % 4 * P + P], w_raw[:, n, :], core.ident[:])
                last.then_inc(prep, 1)
                pe.wait_ge(prep, 5)

                def turn_x(i, s):
                    pe.wait_ge(sg["x_normed"], TC * (i + 1))
                    wait(pe, sg["f_done"], i)
                    for c in range(TC):
                        last = nc.tensor.transpose(ps_z[:, c * P:(c + 1) * P], xn[:, c, :], core.ident[:])
                    last.then_inc(sg["x_turned"], 1)

                def project_z(i, s):
                    pe.wait_ge(sg["xT_ready"], i + 1)
                    nc.tensor.matmul(ps_z[:], wT[:, 3, :], xT[:], start=True, stop=True).then_inc(sg["z_in"], 1)

                def project(n):
                    def part(i, s):
                        pe.wait_ge(sg["xT_ready"], i + 1)
                        wait(pe, sg["silu_done"], 3 * i + n)
                        nc.tensor.matmul(ps_q[:], wT[:, n, :], xT[:], start=True, stop=True).then_inc(sg["qkv_in"], 1)
                    return part

                def turn(k):
                    def part(i, s):
                        src, need, count = ((qkT[:, s, 1], "silu_done", 3 * i + 2), (vT, "silu_done", 3 * i + 3),
                                            (bT[:, s], "bT_done", i + 1), (eqT[:, s], "exp_done", i + 1))[k]
                        pe.wait_ge(sg[need], count)
                        wait(pe, sg["copied"], 4 * i + k)
                        if k == 0:
                            wait(pe, sg["q2_done"], i - 1)
                            wait(pe, sg["onT_ready"], i - 2)
                        for c in range(TC):
                            last = nc.tensor.transpose(ps_t[:, c * P:(c + 1) * P], src[:, c * P:(c + 1) * P], core.ident[:])
                        last.then_inc(sg["turned"], 1)
                    return part

                def scores(i, c, out, lhs, rhs, mask_done, signal):
                    wait(pe, sg[mask_done], TC * i + c)
                    nc.tensor.matmul(out[:].rearrange("p (h t) -> p h t", h=H), lhs[:, c * P:(c + 1) * P], rhs[:, :, c * P:(c + 1) * P],
                                     start=True, stop=True).then_inc(sg[signal], 1)

                def add_states(c, s, x):
                    for h in range(H):
                        last = nc.tensor.matmul(ps_s[h * K:(h + 1) * K, c * P:(c + 1) * P], bn[:, s, c * P + h * K:c * P + (h + 1) * K],
                                                x[:, c, h].rearrange("p j k -> p (j k)"), start=True, stop=True)
                    return last

                def outputs(out, q, states, a, rhs):
                    for c in range(TC):
                        for j in range(4):
                            at = c * P + j * BL
                            nc.tensor.matmul(out[j * BL:(j + 1) * BL, c * P:(c + 1) * P], q[:, at:at + BL],
                                             states[:, c * 4 + j].rearrange("p h k -> p (h k)"), start=True, stop=False, skip_group_check=True)
                        for h in range(H):
                            at = c * P + h * K
                            last = nc.tensor.matmul(out[:, at:at + K], a[:, c, h, :], rhs[:, at:at + K],
                                                    start=False, stop=(h == H - 1), skip_group_check=True)
                    return last

                def step1(i, s):
                    pe.wait_ge(sg["kx_done"], i + 1)
                    wait(pe, sg["ds2_done"], i)
                    for c in range(TC):
                        last = add_states(c, s, kx)
                    last.then_inc(sg["s_in"], 1)

                def scores1(c):
                    def part(i, s):
                        pe.wait_ge(sg["qm_done"], i + 1)
                        scores(i, c, ps_a1, qkT[:, s, 1], qm, "am_done", "a_in")
                    return part

                def out1(i, s):
                    pe.wait_ge(sg["am_done"], TC * (i + 1))
                    pe.wait_ge(sg["sbd_done"], i + 1)
                    wait(pe, sg["ok_done"], i)
                    outputs(ps_o1, qkT[:, s, 0], sbd, am1, bn[:, s]).then_inc(sg["ok_in"], 1)

                def turn_qv(i, s):
                    pe.wait_ge(sg["qv_done"], i + 1)
                    wait(pe, sg["onT_ready"], i)
                    pe.wait_ge(sg["copied"], TC * (i + 2) if not isinstance(i, int) else min(TC * (i + 2), TC * NB))
                    for c in range(TC):
                        last = nc.tensor.transpose(ps_t[:, c * P:(c + 1) * P], qv[:, c * P:(c + 1) * P], core.ident[:])
                    last.then_inc(sg["qv_turned"], 1)

                def step2(i, s):
                    pe.wait_ge(sg["vx_done"], i + 1)
                    pe.wait_ge(sg["ds_done"], i + 1)
                    for c in range(TC):
                        last = add_states(c, s, vx)
                    last.then_inc(sg["s2_in"], 1)

                def scores2(c):
                    def part(i, s):
                        pe.wait_ge(sg["q2m_done"], i + 1)
                        scores(i, c, ps_a2, bT[:, s], q2m, "am2_done", "a2_in")
                    return part

                def out2(i, s):
                    pe.wait_ge(sg["am2_done"], TC * (i + 1))
                    pe.wait_ge(sg["sbd2_done"], i + 1)
                    wait(pe, sg["added"], i)
                    outputs(ps_o2, q2T, sbd2, am2, vn[:, s]).then_inc(sg["ov_in"], 1)

                def turn_o(i, s):
                    pe.wait_ge(sg["on_done"], TC * (i + 1))
                    pe.wait_ge(sg["copied"], TC * (i + 3) if not isinstance(i, int) else min(TC * (i + 3), TC * NB))
                    for c in range(TC):
                        last = nc.tensor.transpose(ps_t[:, c * P:(c + 1) * P], on[:, c * P:(c + 1) * P], core.ident[:])
                    last.then_inc(sg["on_turned"], 1)

                def project_o(i, s):
                    pe.wait_ge(sg["onT_ready"], i + 1)
                    for c in range(TC):
                        last = nc.tensor.matmul(ps_o2[:, c * P:(c + 1) * P], onT[:, c * P:(c + 1) * P], wT[:, 4, :], start=True, stop=True)
                    last.then_inc(sg["y_in"], 1)

                interleaved(pe, NB, 3, TURNS, [
                    (2, {0: turn_qv, 5: scores2(0), 7: scores2(1), 9: scores2(2), 11: scores2(3), 14: out2, 20: turn_o, 22: project_o}),
                    (1, {0: step1, 2: step2, 3: scores1(0), 5: scores1(1), 7: scores1(2), 9: scores1(3), 12: out1}),
                    (0, {3: turn_x, 5: project_z, 6: project(0), 8: project(1), 10: project(2),
                         11: turn(0), 13: turn(1), 17: turn(2), 18: turn(3)})])

            @block.scalar
            def _(act):
                def copy_xT(i, s):
                    act.wait_ge(sg["x_turned"], i + 1)
                    nc.scalar.copy(xT[:], ps_z[:]).then_inc(sg["xT_ready"], 1)

                def sigmoid(n):
                    def part(i, s):
                        act.wait_ge(sg["qkv_in"], 3 * i + n + 1)
                        wait(act, sg["silu_done"], 3 * i + n)
                        nc.scalar.activation(r[:], ps_q[:], ACT.Sigmoid).then_inc(sg["r_done"], 1)
                    return part

                def log_gate(i, s):
                    act.wait_ge(sg["z_in"], i + 1)
                    nc.scalar.activation(za[:], ps_z[:], ACT.Abs).then_inc(sg["abs_done"], 1)
                    act.wait_ge(sg["abs_done"], i + 1)
                    nc.scalar.activation(za[:], za[:], ACT.Exp, scale=-1.0).then_inc(sg["ze_done"], 1)
                    act.wait_ge(sg["ze_done"], i + 1)
                    wait(act, sg["f_done"], i)
                    nc.scalar.activation(zl[:], za[:], ACT.Ln, bias=core.ones[:, 0:1]).then_inc(sg["log_done"], 1)

                def exps(i, s):
                    act.wait_ge(sg["g_done"], i + 1)
                    wait(act, sg["bT_done"], i)
                    wait(act, sg["added"], i - 2)
                    nc.scalar.activation(sT[:], f[:], ACT.Exp, scale=NORM)
                    nc.scalar.activation(e_mid[:, s, :], blocks(gs[:])[:, :, BL // 2 - 1], ACT.Exp, scale=NORM)
                    nc.scalar.activation(e_last[:, s, :], blocks(gs[:])[:, :, BL - 1], ACT.Exp, scale=NORM)
                    act.wait_ge(sg["d_done"], i + 1)
                    nc.scalar.activation(ek[:], dk[:], ACT.Exp, scale=NORM)
                    nc.scalar.activation(eqT[:, s], dq[:], ACT.Exp, scale=NORM).then_inc(sg["exp_done"], 1)

                def copy(k):
                    def part(i, s):
                        act.wait_ge(sg["turned"], 4 * i + k + 1)
                        if k == 0:
                            wait(act, sg["kx_done"], i)
                        nc.scalar.copy((kn[:], vn[:, s], bn[:, s], eqn[:, s])[k], ps_t[:]).then_inc(sg["copied"], 1)
                    return part

                def softmax_exp(i, s):
                    act.wait_ge(sg["sub_done"], i + 1)
                    nc.scalar.activation(ex[:], ok[:], ACT.Exp).then_inc(sg["ex_done"], 1)

                def out_sigmoid(i, s):
                    act.wait_ge(sg["ov_in"], i + 1)
                    nc.scalar.activation(ro[:], ps_o2[:], ACT.Sigmoid).then_inc(sg["ro_done"], 1)

                def copy_onT(i, s):
                    act.wait_ge(sg["on_turned"], i + 1)
                    nc.scalar.copy(onT[:], ps_t[:]).then_inc(sg["onT_ready"], 1)

                interleaved(act, NB, 3, TURNS, [
                    (2, {17: out_sigmoid, 21: copy_onT}),
                    (1, {18: softmax_exp}),
                    (0, {4: copy_xT, 6: sigmoid(0), 8: sigmoid(1), 10: sigmoid(2), 11: log_gate, 12: copy(0), 14: exps, 15: copy(1), 18: copy(2), 19: copy(3)})])

            @block.gpsimd
            def _(pool):
                def rstds(i, s):
                    for c in range(TC):
                        norm.rstd(pool, i * TC + c, c)

                def mask_queries(i, s):
                    pool.wait_ge(sg["silu_done"], 3 * i + 1)
                    wait(pool, sg["a_in"], TC * i)
                    nc.gpsimd.tensor_tensor(qm[:], qkT[:, s, 0, :].unsqueeze(1).broadcast_to([P, H, S]),
                                            part[:].unsqueeze(2).broadcast_to([P, H, S]), ALU.mult).then_inc(sg["qm_done"], 1)

                def decays(i, s):
                    pool.wait_ge(sg["exp_done"], i + 1)
                    nc.gpsimd.tensor_tensor(decay[:, s], e_last[:, s, :].unsqueeze(1).broadcast_to([P, K, NBK]),
                                            blocks(go_on[:])[:, 0:1, 0:NBK].broadcast_to([P, K, NBK]), ALU.mult).then_inc(sg["decay_done"], 1)

                def by_block(k):
                    def part_(i, s):
                        x, src, signal = ((kx, kn[:], "kx_done"), (vx, vn[:, s], "vx_done"))[k]
                        wait(pool, sg["s_in" if k == 0 else "s2_in"], i)
                        pool.wait_ge(sg["copied"], 4 * i + k + 1)
                        for c in range(TC):
                            rows = src[:, c * P:(c + 1) * P].rearrange("p (h k) -> p h k", h=H)
                            last = nc.gpsimd.tensor_tensor(x[:, c], rows.unsqueeze(2).broadcast_to([P, H, 4, K]),
                                                           part[:].unsqueeze(1).unsqueeze(3).broadcast_to([P, H, 4, K]), ALU.mult)
                        last.then_inc(sg[signal], 1)
                    return part_

                def spread(out, states):
                    for q in range(4):
                        at = slice(q * 4, q * 4 + 4)
                        last = nc.gpsimd.tensor_tensor(out[:, at], states[:, at, :].unsqueeze(2).broadcast_to([P, 4, H, K]),
                                                       part[:].unsqueeze(1).unsqueeze(3).broadcast_to([P, 4, H, K]), ALU.mult)
                    return last

                def spread1(i, s):
                    pool.wait_ge(sg["s1T_done"], i + 1)
                    spread(sbd, s1T).then_inc(sg["sbd_done"], 1)

                def spread2(i, s):
                    pool.wait_ge(sg["s2_done"], i + 1)
                    wait(pool, sg["ov_in"], i)
                    spread(sbd2, s2).then_inc(sg["sbd2_done"], 1)

                def mask_queries2(i, s):
                    pool.wait_ge(sg["q2_done"], i + 1)
                    nc.gpsimd.tensor_tensor(q2m[:], q2T[:].unsqueeze(1).broadcast_to([P, H, S]),
                                            part[:].unsqueeze(2).broadcast_to([P, H, S]), ALU.mult).then_inc(sg["q2m_done"], 1)

                def out_rstd(i, s):
                    pool.wait_ge(sg["var_done"], i + 1)
                    nc.gpsimd.tensor_tensor(rs[:], var[:], core.minus_half[:, 0:TC], ALU.pow).then_inc(sg["rs_done"], 1)
                interleaved(pool, NB, 3, TURNS, [
                    (2, {1: mask_queries2, 3: spread2, 19: out_rstd}),
                    (1, {6: spread1}),
                    (0, {0: rstds, 10: mask_queries, 14: by_block(0), 16: by_block(1), 17: decays})])

            @block.vector
            def _(dve):
                dve.wait_ge(loaded, 144)
                nc.vector.memset(s1[:], 0.0).then_inc(prep, 1)
                nc.vector.memset(s2[:], 0.0).then_inc(prep, 1)
                dve.wait_ge(prep, 3)
                nc.vector.tensor_copy(wT[:, 0:4, :].rearrange("p n d -> p (n d)"), ps_a1[:]).then_inc(prep, 1)
                nc.vector.tensor_scalar(wT[:, 4, :], ps_t[:, 0:P], gw[:], None, ALU.mult).then_inc(prep, 1)
                dve.wait_ge(prep, 5)

                def stats(i, s):
                    for c in range(TC):
                        norm.stats(dve, i * TC + c, c, tile_of(X, i * TC + c))

                def layer_norm(i, s):
                    wait(dve, sg["x_turned"], i)
                    for c in range(TC):
                        dve.wait_ge(norm.rstd_done, i * TC + c + 1)
                        norm.apply(xn[:, c, :], tile_of(X, i * TC + c), c).then_inc(sg["x_normed"], 1)

                def gates(i, s):
                    dve.wait_ge(sg["log_done"], i + 1)
                    wait(dve, sg["exp_done"], i)
                    nc.vector.scalar_tensor_tensor(f[:], ps_z[:], 0.0, zl[:], ALU.min, ALU.subtract).then_inc(sg["f_done"], 1)
                    dve.wait_ge(sg["f_done"], i + 1)
                    nc.vector.tensor_tensor_scan(gs[:], go_on[:], f[:], 0.0, ALU.mult, ALU.add).then_inc(sg["g_done"], 1)
                    dve.wait_ge(sg["g_done"], i + 1)
                    mid = blocks(gs[:])[:, :, BL // 2 - 1:BL // 2].broadcast_to([P, NBK, BL])
                    nc.vector.tensor_tensor(blocks(dk[:]), mid, blocks(gs[:]), ALU.subtract).then_inc(sg["dk_done"], 1)
                    dve.wait_ge(sg["dk_done"], i + 1)
                    nc.vector.tensor_scalar(dq[:], dk[:], -1.0, LIMIT, ALU.mult, ALU.min).then_inc(sg["s_done"], 1)
                    dve.wait_ge(sg["s_done"], 2 * i + 1)
                    nc.vector.tensor_scalar(dk[:], dk[:], LIMIT, None, ALU.min).then_inc(sg["d_done"], 1)

                def silu(n):
                    def part(i, s):
                        dve.wait_ge(sg["r_done"], 3 * i + n + 1)
                        if n == 2:
                            wait(dve, sg["turned"], 4 * i - 2)
                        nc.vector.tensor_tensor(vT[:] if n == 2 else qkT[:, s, n, :], ps_q[:], r[:], ALU.mult).then_inc(sg["silu_done"], 1)
                    return part

                def keys(i, s):
                    dve.wait_ge(sg["exp_done"], i + 1)
                    nc.vector.tensor_scalar(sT[:], sT[:], -1.0, 1.0, ALU.mult, ALU.add).then_inc(sg["s_done"], 1)
                    dve.wait_ge(sg["s_done"], 2 * i + 2)
                    nc.vector.tensor_tensor(bT[:, s], sT[:], ek[:], ALU.mult).then_inc(sg["bT_done"], 1)

                def states(i, s, out, names):
                    s_in, ds_done, send_done, s_done_ = names
                    dve.wait_ge(sg[s_in], i + 1)
                    dve.wait_ge(sg["decay_done"], i + 1)
                    to_end = blocks(eqT[:, s])[:, :, BL - 1:BL].broadcast_to([P, NBK, K])
                    nc.vector.tensor_tensor(ds[:].rearrange("p k j -> p j k"), ps_s[:].rearrange("p (j k) -> p j k", k=K), to_end,
                                            ALU.mult).then_inc(sg[ds_done], 1)
                    dve.wait_ge(sg[ds_done], i + 1)
                    nc.vector.tensor_tensor_scan(send[:].rearrange("p k j -> p (k j)"), decay[:, s].rearrange("p k j -> p (k j)"),
                                                 ds[:].rearrange("p k j -> p (k j)"), 0.0, ALU.mult, ALU.add).then_inc(sg[send_done], 1)
                    dve.wait_ge(sg[send_done], i + 1)
                    nc.vector.tensor_tensor(out[:, 1:, :], send[:].rearrange("p k j -> p j k")[:, 0:NBK - 1, :],
                                            e_mid[:, s, 1:].unsqueeze(2).broadcast_to([P, NBK - 1, K]), ALU.mult).then_inc(sg[s_done_], 1)

                def mask_scores(c, out, bank, a_in, done):
                    def part(i, s):
                        dve.wait_ge(sg[a_in], TC * i + c + 1)
                        nc.vector.tensor_tensor(out[:, c], bank[:].rearrange("p (h t) -> p h t", h=H),
                                                causal[:].unsqueeze(1).broadcast_to([P, H, P]), ALU.mult).then_inc(sg[done], 1)
                    return part

                def states1(i, s):
                    states(i, s, s1, ("s_in", "ds_done", "send_done", "s1_done"))
                    dve.wait_ge(sg["s1_done"], i + 1)
                    wait(dve, sg["sbd_done"], i)
                    dve.sem_inc(norm.held, 1)
                    nc.vector.transpose(s1T[:].rearrange("p j k -> p (j k)"), s1[:].rearrange("p j k -> p (j k)")).then_inc(sg["s1T_done"], 1)

                def states2(i, s):
                    wait(dve, sg["sbd2_done"], i)
                    states(i, s, s2, ("s2_in", "ds2_done", "send2_done", "s2_done"))

                heads = lambda m: m.rearrange("p (g k) -> p g k", k=K)
                wide = lambda m: m.unsqueeze(2).broadcast_to([P, TC * H, K])

                def slots_max(i, s):
                    dve.wait_ge(sg["ok_in"], i + 1)
                    nc.vector.tensor_tensor(ok[:], ps_o1[:], eqn[:, s], ALU.mult).then_inc(sg["ok_done"], 1)
                    dve.wait_ge(sg["ok_done"], i + 1)
                    nc.vector.tensor_reduce(mx[:], heads(ok[:]), AX.X, ALU.max).then_inc(sg["mx_done"], 1)
                    dve.wait_ge(sg["mx_done"], i + 1)
                    nc.vector.tensor_tensor(heads(ok[:]), heads(ok[:]), wide(mx[:]), ALU.subtract).then_inc(sg["sub_done"], 1)

                def slots_softmax(i, s):
                    dve.wait_ge(sg["ex_done"], i + 1)
                    nc.vector.tensor_reduce(sm_[:], heads(ex[:]), AX.X, ALU.add).then_inc(sg["sum_done"], 1)
                    dve.wait_ge(sg["sum_done"], i + 1)
                    nc.vector.reciprocal(rc[:], sm_[:]).then_inc(sg["rc_done"], 1)
                    dve.wait_ge(sg["rc_done"], i + 1)
                    nc.vector.tensor_tensor(heads(qv[:]), heads(ex[:]), wide(rc[:]), ALU.mult).then_inc(sg["qv_done"], 1)

                def queries2(i, s):
                    dve.wait_ge(sg["qv_turned"], i + 1)
                    nc.vector.tensor_tensor(q2T[:], ps_t[:], eqT[:, s], ALU.mult).then_inc(sg["q2_done"], 1)

                def out_norm(i, s):
                    dve.wait_ge(sg["ro_done"], i + 1)
                    nc.vector.tensor_tensor(o[:], ps_o2[:], ro[:], ALU.mult).then_inc(sg["o_done"], 1)
                    dve.wait_ge(sg["o_done"], i + 1)
                    for c in range(TC):
                        oc = o[:, c * P:(c + 1) * P]
                        nc.vector.scalar_tensor_tensor(osq[:, c, :], oc, 1.0, oc, ALU.mult, ALU.mult, accum_out=ss[:, c:c + 1]).then_inc(sg["ss_done"], 1)
                    dve.wait_ge(sg["ss_done"], TC * (i + 1))
                    nc.vector.tensor_scalar(var[:], ss[:], 1.0 / D, EPS, ALU.mult, ALU.add).then_inc(sg["var_done"], 1)

                def out_scale(i, s):
                    dve.wait_ge(sg["rs_done"], i + 1)
                    for c in range(TC):
                        nc.vector.tensor_scalar(on[:, c * P:(c + 1) * P], o[:, c * P:(c + 1) * P], rs[:, c:c + 1], None, ALU.mult)\
                            .then_inc(sg["on_done"], 1)

                def add(i, s):
                    dve.wait_ge(sg["y_in"], i + 1)
                    xb = X[:, bass.ds(i * TC, TC), :].rearrange("p c d -> p (c d)")
                    nc.vector.tensor_tensor(xb, ps_o2[:], xb, ALU.add).then_inc(sg["added"], 1)
                mask1 = lambda c: mask_scores(c, am1, ps_a1, "a_in", "am_done")
                mask2 = lambda c: mask_scores(c, am2, ps_a2, "a2_in", "am2_done")
                interleaved(dve, NB, 3, TURNS, [
                    (2, {0: queries2, 6: mask2(0), 8: mask2(1), 10: mask2(2), 12: mask2(3), 17: out_norm, 19: out_scale, 23: add}),
                    (1, {1: states1, 3: states2, 4: mask1(0), 6: mask1(1), 8: mask1(2), 10: mask1(3), 17: slots_max, 18: slots_softmax}),
                    (0, {0: stats, 2: layer_norm, 7: silu(0), 9: silu(1), 11: silu(2), 13: gates, 16: keys})])


def chunk_attention(core, name, Wq, Wk, Wv):
    nc, X = core.nc, core.X
    CG, DK = 16, 8
    CH = 32
    NC = 8
    HT = NC * CH
    NHALF = NB * S // HT
    THIRDS = ((0, 0), (1, 0), (0, 1), (2, 0), (0, 2), (1, 1), (1, 2), (2, 1))
    ROWS = DK * len(THIRDS)
    COPIES = 2 * len(THIRDS)
    NS = 4 * NC
    UNITS = 2 * NC
    EARLY = 5
    bounce = nc.dram_tensor(f"{name}_bounce", (4, P, 3, 2 * HT), BF16, kind="Internal").ap()
    sbounce = nc.dram_tensor(f"{name}_sbounce", (4, 2, 4, P, NC), BF16, kind="Internal").ap()
    with ExitStack() as ctx:
        ctx.callback(core.release_semaphores)
        sb = lambda n, s, d=F32: ctx.enter_context(nc.sbuf_tensor(f"{name}_{n}", s, d))
        pb = lambda n, k=1: ctx.enter_context(nc.psum_tensor(f"{name}_{n}", [P, 512 * k], F32))
        sem = lambda n: core.semaphore(f"{name}_{n}")
        norm = RowNorm(core, ctx, f"{name}_n", 2)
        w_raw, wT = sb("w_raw", [P, 3, D]), sb("wT", [P, 3, D])
        xn = sb("xn", [P, T, D])
        xnow = sb("xnow", [P, 2, D])
        xT = sb("xT", [P, HT])
        thirds = sb("thirds", [P, 2, 3, 2 * HT], BF16)
        rest = sb("rest", [P, 2 * HT])
        qst = sb("qst", [96, 4, CG * HT], BF16)
        kst = sb("kst", [96, 4, CG * HT], BF16)
        vst = sb("vst", [P, 4, NC, 4, 32])
        mx = sb("mx", [P, 2, NS])
        shift = sb("shift", [P, 2, 2, NS], BF16)
        pT = sb("pT", [P, 4, 2, 512])
        oN = sb("oN", [P, 2, CG, 32])
        rc = sb("rc", [P, 2, CG])
        on = sb("on", [P, 2, D])
        yst = sb("yst", [P, T, 6])
        ps_m, ps_o = pb("ps_m"), pb("ps_o")
        ps_s = [pb(f"ps_s{i}") for i in range(2)]
        ps_p = [pb(f"ps_p{i}", 2) for i in range(2)]
        loaded, prep, memset_done = sem("loaded"), sem("prep"), sem("memset_done")
        held_sp, held_pool = sem("held_sp"), sem("held_pool")
        names = ("x_normed", "xn_kept", "x_turned", "xT_ready", "qk_in", "hi_done", "rest_done", "mid_done", "lo_done", "v_in", "v_ready",
                 "vst_done", "s_in", "max_done", "neg_done", "shift_done", "st_in", "exp_done", "pv_done", "o_turned", "rc_done", "on_done", "y_done", "y_stats")
        sg = {n: sem(n) for n in names}
        bounced = [sem(f"bounced{i}") for i in range(4)]
        sbounced = [sem(f"sbounced{i}") for i in range(4)]
        qk_ready = [sem(f"qk_ready{i}") for i in range(4)]
        shift_ready = [sem(f"shift_ready{i}") for i in range(4)]
        uses = lambda h, s, copies: copies * 4 * (h - s) + copies * 16

        with nc.Block() as block:
            @block.sync
            def _(sp):
                for n, w in enumerate((Wq, Wk, Wv)):
                    sp.dma_start(w_raw[:, n, :], w).then_inc(loaded, 16)
                sp.wait_ge(memset_done, 6)

                def body(front, top):
                    (h, s), (hm, sm) = front, top
                    if h is not None:
                        sp.wait_ge(sg["lo_done"], h + 1)
                        sp.sem_inc(held_sp, 1)
                        if not isinstance(h, int) or h >= 4:
                            sp.wait_ge(sg["pv_done"], 8 * (h - 3))
                        sp.sem_inc(held_sp, 1)
                        sp.dma_start(bounce[s], thirds[:, s % 2]).then_inc(bounced[s], 16)
                        sp.wait_ge(bounced[s], uses(h, s, 1))
                        sp.sem_inc(held_sp, 1)
                        for r, (tq, tk) in enumerate(THIRDS):
                            for t3, o, dst in ((tq, 0, qst), (tk, HT, kst)):
                                src = bounce[s, :, t3, o:o + HT].rearrange("(g d) t -> d g t", d=DK)
                                sp.dma_start(dst[r * DK:(r + 1) * DK, s].rearrange("d (g t) -> d g t", g=CG), src).then_inc(qk_ready[s], 16)
                    if hm is not None:
                        sp.wait_ge(sg["shift_done"], hm + 1)
                        sp.sem_inc(held_sp, 1)
                        sp.dma_start(sbounce[sm].rearrange("j q p a -> p (j q) a"), shift[:, sm % 2].rearrange("p j (q a) -> p (j q) a", a=NC)).then_inc(sbounced[sm], 16)
                        sp.wait_ge(sbounced[sm], uses(hm, sm, 1))
                        sp.sem_inc(held_sp, 1)
                        sp.dma_start(qst[ROWS:ROWS + 2, sm], sbounce[sm].rearrange("j q p a -> j (q p a)")).then_inc(shift_ready[sm], 16)
                staggered(sp, NHALF, 4, (0, 1), body)

            @block.gpsimd
            def _(pool):
                for n, (rows, value) in enumerate(((qst[64:96], 0.0), (kst[64:96], 1.0), (vst[:, 0:2], 0.0), (vst[:, 2:4], 0.0),
                                                   (vst[:, 0:2, :, :, DK:DK + 1], 1.0), (vst[:, 2:4, :, :, DK:DK + 1], 1.0))):
                    nc.gpsimd.memset(rows, value).then_inc(memset_done, 1)
                    pool.wait_ge(memset_done, n + 1)
                def body(front, prob, last_part):
                    (h, s), (hp, sp_), (hl, sl) = front, prob, last_part
                    if h is not None:
                        for c in range(2):
                            norm.rstd(pool, 2 * h + c, c)
                    if hl is not None:
                        outputs(hl, 1)
                    if h is not None:
                        pool.wait_ge(sg["rest_done"], h + 1)
                        if not isinstance(h, int) or h >= 2:
                            qk = qk_ready[(s - 2) % 4]
                            pool.wait_ge(qk, uses(h - 2, (s - 2) % 4, COPIES))
                        pool.sem_inc(held_pool, 1)
                        nc.gpsimd.tensor_copy(thirds[:, s % 2, 1, :], rest[:]).then_inc(sg["mid_done"], 1)
                        pool.wait_ge(sg["mid_done"], h + 1)
                        nc.gpsimd.tensor_tensor(thirds[:, s % 2, 2, :], rest[:], thirds[:, s % 2, 1, :], ALU.subtract).then_inc(sg["lo_done"], 1)
                    if hp is not None:
                        outputs(hp, 0)

                def outputs(h, g):
                    n = 2 * h + g
                    pool.wait_ge(sg["rc_done"], n + 1)
                    nc.gpsimd.tensor_tensor(on[:, g, :].rearrange("p (c d) -> p c d", d=DK), oN[:, g, :, 0:DK],
                                            rc[:, g, :].unsqueeze(2).broadcast_to([P, CG, DK]), ALU.mult).then_inc(sg["on_done"], 1)
                    pool.wait_ge(sg["on_done"], n + 1)
                    nc.gpsimd.tensor_tensor(tile_of(xn, n), tile_of(xn, n), on[:, g, :], ALU.add).then_inc(sg["y_done"], 1)
                staggered(pool, NHALF, 4, (0, 2, 3), body)

            @block.tensor
            def _(pe):
                pe.wait_ge(loaded, 48)
                for n in range(3):
                    last = nc.tensor.transpose(ps_m[:, n * P:(n + 1) * P], w_raw[:, n, :], core.ident[:])
                last.then_inc(prep, 1)
                pe.wait_ge(prep, 3)

                def front_part(u, h):
                    if u == 0:
                        pe.wait_ge(sg["x_normed"], 2 * (h + 1))
                        wait(pe, sg["vst_done"], h)
                        for c in range(2):
                            last = nc.tensor.transpose(ps_m[:, c * P:(c + 1) * P], xnow[:, c, :], core.ident[:])
                        last.then_inc(sg["x_turned"], 1)
                    if u == 2:
                        pe.wait_ge(sg["xT_ready"], h + 1)
                        for n in range(2):
                            last = nc.tensor.matmul(ps_m[:, n * HT:(n + 1) * HT], wT[:, n, :], xT[:], start=True, stop=True)
                        last.then_inc(sg["qk_in"], 1)
                    if u == 5:
                        pe.wait_ge(sg["rest_done"], h + 1)
                        for a in range(NC):
                            for g in range(4):
                                last = nc.tensor.matmul(ps_m[g * CH:(g + 1) * CH, a * CH:(a + 1) * CH], xT[:, a::NC],
                                                        wT[:, 2, g * CH:(g + 1) * CH], start=True, stop=True)
                        last.then_inc(sg["v_in"], 1)

                def chunk(stack, rows, s, a, tile=None):
                    cols = stack[0:rows, s, a::NC]
                    return cols if tile is None else cols[:, tile * P:(tile + 1) * P]

                def score(k, h, s):
                    a, qt = k // 4, k % 4
                    if k == 0:
                        pe.wait_ge(qk_ready[s], uses(h, s, COPIES))
                    if isinstance(h, int) and h == 0 and k < 2:
                        pass
                    else:
                        pe.wait_ge(sg["max_done"], NS * h + (k - 1))
                    nc.tensor.matmul(ps_s[k % 2][:], chunk(qst, ROWS, s, a, qt), chunk(kst, ROWS, s, a), start=True, stop=True).then_inc(sg["s_in"], 1)

                def shifted(u, h, s):
                    g, kt, pair = u // 8, u % 8 // 2, u % 2
                    if u == 0:
                        pe.wait_ge(shift_ready[s], uses(h, s, 1))
                    if isinstance(h, int) and h == 0 and u < 2:
                        pass
                    else:
                        pe.wait_ge(sg["exp_done"], UNITS * h + (u - 1))
                    for b in range(2):
                        a = 4 * g + 2 * pair + b
                        last = nc.tensor.matmul(ps_p[u % 2][:, b * 512:(b + 1) * 512], chunk(kst, ROWS + 2, s, a, kt), chunk(qst, ROWS + 2, s, a),
                                                start=True, stop=True)
                    last.then_inc(sg["st_in"], 1)

                def values(r, h, s):
                    g, kt = r // 4, r % 4
                    pe.wait_ge(sg["exp_done"], UNITS * h + 2 * r + 2)
                    if r == 0:
                        pe.wait_ge(sg["vst_done"], h + 1)
                    if kt == 0:
                        wait(pe, sg["o_turned"], 2 * h + g)
                    for b in range(4):
                        a = 4 * g + b
                        last = nc.tensor.matmul(ps_o[b * 32:(b + 1) * 32, :], vst[:, s, a, kt, :], pT[:, (2 * r + b // 2) % 4, b % 2, :],
                                                start=(kt == 0), stop=(kt == 3))
                    last.then_inc(sg["pv_done"], 1)

                def body(front, top, prob, last_part):
                    (h, s), (hm, sm), (hp, sp_), (hl, sl) = front, top, prob, last_part
                    k = 0
                    if hm is not None:
                        for k in range(EARLY):
                            score(k, hm, sm)
                        k = EARLY
                    if hl is not None:
                        values(7, hl, sl)
                    for u in range(UNITS):
                        if hp is not None:
                            shifted(u, hp, sp_)
                            if u % 2 and u >= 3:
                                values((u - 3) // 2, hp, sp_)
                        if h is not None:
                            front_part(u, h)
                        if hm is not None:
                            for _ in range(2):
                                if k < NS:
                                    score(k, hm, sm)
                                    k += 1
                staggered(pe, NHALF, 4, (0, 1, 2, 3), body)

            @block.scalar
            def _(act):
                def front_part(u, h, s):
                    if u == 1:
                        act.wait_ge(sg["x_turned"], h + 1)
                        nc.scalar.copy(xT[:].rearrange("p (t a) -> p a t", a=NC), ps_m[:, 0:HT].rearrange("p (a t) -> p a t", a=NC)).then_inc(sg["xT_ready"], 1)
                    if u == 3:
                        act.wait_ge(sg["qk_in"], h + 1)
                        if not isinstance(h, int) or h >= 2:
                            act.wait_ge(qk_ready[(s - 2) % 4], uses(h - 2, (s - 2) % 4, COPIES))
                        nc.scalar.copy(thirds[:, s % 2, 0, :], ps_m[:]).then_inc(sg["hi_done"], 1)
                    if u == 6:
                        act.wait_ge(sg["v_in"], h + 1)
                        if not isinstance(h, int) or h >= 4:
                            act.wait_ge(sg["pv_done"], 8 * (h - 3))
                        nc.scalar.copy(vst[:, s, :, :, 0:DK], ps_m[:, 0:HT].rearrange("p (a k d) -> p a k d", a=NC, k=4)).then_inc(sg["vst_done"], 1)

                def body(front, prob):
                    (h, s), (hp, sp_) = front, prob
                    for u in range(UNITS):
                        if hp is not None:
                            act.wait_ge(sg["st_in"], UNITS * hp + u + 1)
                            if not (isinstance(hp, int) and hp == 0 and u < 4):
                                act.wait_ge(sg["pv_done"], 8 * hp + (u // 2 - 1))
                            nc.scalar.activation(pT[:, u % 4].rearrange("p b q -> p (b q)"), ps_p[u % 2][:], ACT.Exp).then_inc(sg["exp_done"], 1)
                        if h is not None:
                            front_part(u, h, s)
                staggered(act, NHALF, 4, (0, 2), body)

            @block.vector
            def _(dve):
                dve.wait_ge(prep, 1)
                nc.vector.tensor_copy(wT[:, 0:2, :].rearrange("p n d -> p (n d)"), ps_m[:, 0:2 * P]).then_inc(prep, 1)
                nc.vector.tensor_copy(wT[:, 2, :].rearrange("p (g k d) -> p k g d", g=4, d=DK),
                                      ps_m[:, 2 * P:3 * P].rearrange("p (k g d) -> p k g d", g=4, d=DK)).then_inc(prep, 1)

                def front_part(k, h, s):
                    if k == 0:
                        for c in range(2):
                            norm.stats(dve, 2 * h + c, c, tile_of(X, 2 * h + c))
                    if k == 3:
                        wait(dve, sg["x_turned"], h)
                        for c in range(2):
                            dve.wait_ge(norm.rstd_done, 2 * h + c + 1)
                            norm.apply(xnow[:, c, :], tile_of(X, 2 * h + c), c).then_inc(sg["x_normed"], 1)
                    if k == 4:
                        dve.wait_ge(sg["x_normed"], 2 * (h + 1))
                        nc.vector.tensor_copy(xn[:, bass.ds(2 * h, 2), :], xnow[:]).then_inc(sg["xn_kept"], 1)
                    if k == 14:
                        dve.wait_ge(sg["hi_done"], h + 1)
                        wait(dve, sg["lo_done"], h)
                        nc.vector.tensor_tensor(rest[:], ps_m[:], thirds[:, s % 2, 0, :], ALU.subtract).then_inc(sg["rest_done"], 1)

                def turn_outputs(h, g):
                    n = 2 * h + g
                    dve.wait_ge(sg["pv_done"], 8 * h + 4 * g + 4)
                    wait(dve, sg["on_done"], n - 1)
                    dve.sem_inc(norm.held, 1)
                    nc.vector.transpose(oN[:, g].rearrange("p c d -> p (c d)"), ps_o[:]).then_inc(sg["o_turned"], 1)
                    dve.wait_ge(sg["o_turned"], n + 1)
                    nc.vector.reciprocal(rc[:, g, :], oN[:, g, :, DK]).then_inc(sg["rc_done"], 1)

                def stats_of(n):
                    dve.wait_ge(sg["y_done"], n + 1)
                    nc.vector.bn_stats(yst[:, bass.ds(n, 1), :].rearrange("p a d -> p (a d)"), tile_of(xn, n)).then_inc(sg["y_stats"], 1)

                def body(front, top, prob, last_part):
                    (h, s), (hm, sm), (hp, sp_), (hl, sl) = front, top, prob, last_part
                    for k in range(NS):
                        if h is not None:
                            front_part(k, h, s)
                        if hl is not None and k == EARLY + 1:
                            turn_outputs(hl, 1)
                        if hl is not None and k == EARLY + 4:
                            stats_of(2 * hl)
                            stats_of(2 * hl + 1)
                        if hp is not None and k == 26:
                            turn_outputs(hp, 0)
                        if hm is not None:
                            dve.wait_ge(sg["s_in"], NS * hm + k + 1)
                            nc.vector.tensor_reduce(mx[:, sm % 2, k % 4 * NC + k // 4:k % 4 * NC + k // 4 + 1], ps_s[k % 2][:], AX.X, ALU.max).then_inc(sg["max_done"], 1)
                    if hm is not None:
                        dve.wait_ge(sg["max_done"], NS * (hm + 1))
                        if not isinstance(hm, int) or hm >= 2:
                            dve.wait_ge(shift_ready[(sm - 2) % 4], uses(hm - 2, (sm - 2) % 4, 1))
                        nc.vector.tensor_scalar(shift[:, sm % 2, 0, :], mx[:, sm % 2, :], -1.0, None, ALU.mult).then_inc(sg["neg_done"], 1)
                        dve.wait_ge(sg["neg_done"], hm + 1)
                        nc.vector.scalar_tensor_tensor(shift[:, sm % 2, 1, :], mx[:, sm % 2, :], -1.0, shift[:, sm % 2, 0, :],
                                                       ALU.mult, ALU.subtract).then_inc(sg["shift_done"], 1)
                staggered(dve, NHALF, 4, (0, 1, 2, 3), body)

        mv, sq, tot, msq = sb("mv", [P, NB, 2]), sb("sq", [P, NB, 2]), sb("tot", [P, NB, 2]), sb("msq", [P, NB])
        rs, half, yn = sb("rs", [P, NB]), sb("half", [P, NB]), sb("yn", [P, 2, 4 * D])
        dv, pw, nd, ad, nd2 = sem("dv"), sem("pw"), sem("nd"), sem("ad"), sem("nd2")
        with nc.Block() as block:
            @block.vector
            def _(dve):
                n = [0]

                def done(ins):
                    n[0] += 1
                    ins.then_inc(dv, 1)
                    dve.wait_ge(dv, n[0])
                for b in range(NB):
                    ins = nc.vector.bn_aggr(mv[:, b, :], yst[:, 4 * b:4 * b + 4, :].rearrange("p t s -> p (t s)"))
                    ins.then_inc(dv, 1)
                n[0] = NB
                dve.wait_ge(dv, NB)
                done(nc.vector.tensor_copy(sq[:, :, 0], mv[:, :, 0]))
                done(nc.vector.tensor_tensor(sq[:, :, 1], mv[:, :, 0], mv[:, :, 0], ALU.mult))
                done(nc.vector.tensor_tensor(sq[:, :, 1], sq[:, :, 1], mv[:, :, 1], ALU.add))
                dve.wait_ge(pw, 1)
                done(nc.vector.tensor_scalar(tot[:].rearrange("p b s -> p (b s)"), ps_m[:, 0:2 * NB], 1.0 / P, None, ALU.mult))
                done(nc.vector.tensor_tensor(msq[:], tot[:, :, 0], tot[:, :, 0], ALU.mult))
                done(nc.vector.tensor_tensor(msq[:], tot[:, :, 1], msq[:], ALU.subtract))
                done(nc.vector.tensor_scalar(msq[:], msq[:], EPS, None, ALU.add))
                dve.wait_ge(pw, 2)

                def add(b):
                    x = X[:, 4 * b:4 * b + 4, :].rearrange("p t d -> p (t d)")
                    dve.wait_ge(nd, b + 1)
                    nc.vector.tensor_tensor(x, x, yn[:, b % 2, :], ALU.add).then_inc(ad, 1)
                for b in range(NB):
                    y = xn[:, 4 * b:4 * b + 4, :].rearrange("p t d -> p (t d)")
                    wait(dve, ad, b - 1)
                    nc.vector.tensor_scalar(yn[:, b % 2, :], y, tot[:, b, 0:1], rs[:, b:b + 1], ALU.subtract, ALU.mult).then_inc(nd, 1)
                    if b >= 1:
                        add(b - 1)
                add(NB - 1)

            @block.tensor
            def _(pe):
                pe.wait_ge(dv, NB + 3)
                nc.tensor.matmul(ps_m[:, 0:2 * NB], core.ones[:], sq[:].rearrange("p b s -> p (b s)"), start=True, stop=True).then_inc(pw, 1)

            @block.gpsimd
            def _(pool):
                nc.gpsimd.memset(half[:], -0.5).then_inc(nd2, 1)
                pool.wait_ge(dv, NB + 7)
                pool.wait_ge(nd2, 1)
                nc.gpsimd.tensor_tensor(rs[:], msq[:], half[:], ALU.pow).then_inc(pw, 1)


def rope_attention(core, name, Wq, Wk, Wv, Wo, bo, cos_in, sin_in):
    nc, X = core.nc, core.X
    HEADS, DH = 16, 64
    NP = HEADS // 2
    N = NB * NP
    TC = S // P
    UNITS = 2 * TC
    MASKED = 1e30
    LN, FRONT, SCORE, VALUE, OUT = 0, 4, 5, 7, 8
    with ExitStack() as ctx:
        ctx.callback(core.release_semaphores)
        sb = lambda n, s, d=F32: ctx.enter_context(nc.sbuf_tensor(f"{name}_{n}", s, d))
        pb = lambda n, k=1: ctx.enter_context(nc.psum_tensor(f"{name}_{n}", [P, 512 * k], F32))
        sem = lambda n: core.semaphore(f"{name}_{n}")
        norm = RowNorm(core, ctx, f"{name}_n", TC)
        w = sb("w", [P, 4, NP, P])
        wv, wo = sb("wv", [P, NP, P]), sb("wo", [P, NP, D])
        bias = sb("bias", [1, D])
        cos, sin = sb("cos", [P, S]), sb("sin", [P, S])
        mask = sb("mask", [P, P], BF16)
        xn, xT = sb("xn", [P, TC, D]), sb("xT", [P, S])
        by_cos, by_sin = sb("by_cos", [P, 2, S]), sb("by_sin", [P, 2, S])
        rot = sb("rot", [P, 2, 2, S])
        v = sb("v", [P, 4, TC, P])
        low = sb("low", [P, 2, UNITS])
        prob = sb("prob", [P, 2, UNITS, S])
        total = sb("total", [P, 2, UNITS])
        inverse = sb("inverse", [P, 2, UNITS])
        probT = sb("probT", [P, 2, 2, S])
        oT = sb("oT", [P, S])
        ps_r, ps_o = pb("ps_r"), pb("ps_o")
        ps_s = [pb(f"ps_s{i}") for i in range(4)]
        ps_t = [pb(f"ps_t{i}") for i in range(2)]
        loaded, prep = sem("loaded"), sem("prep")
        names = ("x_normed", "x_turned", "xT_ready", "qk_in", "multiplied", "rotated", "v_in", "v_ready", "s_in", "low_done", "exp_done",
                 "p_turned", "probT_dve", "probT_act", "pv_done", "inverse_done", "divided", "oT_ready", "y_in", "added")
        sg = {n: sem(n) for n in names}

        def unit(u):
            head, tile = u % 2, u // 2
            return head, tile, (tile + 1) * P

        def steps(engine, body):
            item_steps(engine, NP, OUT, body)

        with nc.Block() as block:
            @block.sync
            def _(sp):
                for k, src in ((0, Wq), (2, Wk)):
                    sp.dma_start(w[:, k], src.rearrange("c (h d) -> c h d", d=P)).then_inc(loaded, 16)
                sp.dma_start(wv[:], Wv.rearrange("c (h d) -> c h d", d=P)).then_inc(loaded, 16)
                sp.dma_start(wo[:], Wo.rearrange("(h d) c -> d h c", d=P)).then_inc(loaded, 16)
                sp.dma_start(bias[:], bo.rearrange("(a c) -> a c", a=1)).then_inc(loaded, 16)
                sp.dma_start(cos[:], cos_in).then_inc(loaded, 16)
                sp.dma_start(sin[:], sin_in).then_inc(loaded, 16)

            @block.gpsimd
            def _(pool):
                nc.gpsimd.memset(mask[:], 0.0).then_inc(prep, 1)
                pool.wait_ge(prep, 1)
                nc.gpsimd.affine_select(out=mask[:], in_=mask[:], compare_op=ALU.is_ge, fill=MASKED, base=0,
                                        pattern=[[-1, P]], channel_multiplier=1).then_inc(prep, 1)
                pool.wait_ge(loaded, 112)
                nc.gpsimd.tensor_tensor(w[:, 0].rearrange("p h d -> p (h d)"), w[:, 0].rearrange("p h d -> p (h d)"),
                                        core.minus_eighth[:, 0:1].broadcast_to([P, NP * P]), ALU.mult).then_inc(prep, 1)
                pool.wait_ge(prep, 3)
                for k in (0, 2):
                    for a in range(2):
                        nc.gpsimd.tensor_copy(w[:, k + 1, :, a::2], w[:, k, :, 1 - a::2]).then_inc(prep, 1)

                def body(item):
                    ln, front, score = item(LN), item(FRONT), item(SCORE)
                    if ln and ln[2] == 0:
                        for c in range(TC):
                            norm.rstd(pool, TC * ln[1] + c, c)
                    for u in range(UNITS):
                        if front and u in (3, 6):
                            n, k = front[0], u // 4
                            pool.wait_ge(sg["multiplied"], 4 * n + 2 * k + 2)
                            nc.gpsimd.tensor_tensor(rot[:, front[2] % 2, k], by_cos[:, k], by_sin[:, k], ALU.add).then_inc(sg["rotated"], 1)
                        if score:
                            n, p, keys = score[0], score[2], unit(u)[2]
                            pool.wait_ge(sg["inverse_done"], UNITS * n + u + 1)
                            nc.gpsimd.tensor_tensor(prob[:, p % 2, u, 0:keys], prob[:, p % 2, u, 0:keys],
                                                    inverse[:, p % 2, u:u + 1].broadcast_to([P, keys]), ALU.mult).then_inc(sg["divided"], 1)
                steps(pool, body)

            @block.tensor
            def _(pe):
                pe.wait_ge(prep, 7)

                def front_part(u, n, b, p):
                    if u == 0 and p == 0:
                        pe.wait_ge(sg["x_normed"], TC * (b + 1))
                        wait(pe, sg["v_ready"], n)
                        wait(pe, sg["added"], n - (OUT - FRONT))
                        for c in range(TC):
                            last = nc.tensor.transpose(ps_r[:, c * P:(c + 1) * P], xn[:, c, :], core.ident[:])
                        last.then_inc(sg["x_turned"], 1)
                    if 1 <= u <= 4:
                        if u == 1:
                            if p == 0:
                                pe.wait_ge(sg["xT_ready"], b + 1)
                            else:
                                wait(pe, sg["v_ready"], n)
                                wait(pe, sg["added"], n - (OUT - FRONT))
                        else:
                            pe.wait_ge(sg["multiplied"], 4 * n + u - 1)
                        nc.tensor.matmul(ps_r[:], w[:, u - 1, p, :], xT[:], start=True, stop=True).then_inc(sg["qk_in"], 1)
                    if u == 5:
                        pe.wait_ge(sg["multiplied"], 4 * n + 4)
                        for c in range(TC):
                            last = nc.tensor.matmul(ps_r[:, c * P:(c + 1) * P], xT[:, c * P:(c + 1) * P], wv[:, p, :], start=True, stop=True)
                        last.then_inc(sg["v_in"], 1)

                def scores(u, n, b, p):
                    head, tile, keys = unit(u)
                    rows = slice(head * DH, (head + 1) * DH)
                    if u == 0:
                        pe.wait_ge(sg["rotated"], 2 * (n + 1))
                    wait(pe, sg["exp_done"], UNITS * n + u - 3)
                    out = ps_s[2 * head + u // 2 % 2]
                    nc.tensor.matmul(out[:, 0:keys], rot[rows, p % 2, 0, tile * P:(tile + 1) * P], rot[rows, p % 2, 1, 0:keys],
                                     start=True, stop=False, skip_group_check=True)
                    nc.tensor.matmul(out[:, tile * P:keys], core.identb[:], mask[:], start=False, stop=True,
                                     skip_group_check=True).then_inc(sg["s_in"], 1)

                def turn(u, n, b, p):
                    head, tile, _ = unit(u)
                    if u < 2:
                        pe.wait_ge(sg["divided"], UNITS * n + UNITS - 1 + u)
                    wait(pe, sg["probT_act" if head else "probT_dve"], TC * n + tile)
                    for c in range(tile, TC):
                        last = nc.tensor.transpose(ps_t[head][:, (c - tile) * P:(c - tile + 1) * P],
                                                   prob[:, p % 2, 2 * c + head, tile * P:(tile + 1) * P], core.ident[:])
                    last.then_inc(sg["p_turned"], 1)

                def values(tile, n, b, p):
                    if tile == 0:
                        wait(pe, sg["oT_ready"], n)
                    pe.wait_ge(sg["probT_dve"], TC * n + tile + 1)
                    pe.wait_ge(sg["probT_act"], TC * n + tile + 1)
                    for head in range(2):
                        rows = slice(head * DH, (head + 1) * DH)
                        last = nc.tensor.matmul(ps_o[rows, tile * P:], v[:, p % 4, tile, rows], probT[:, head, tile % 2, 0:S - tile * P],
                                                start=(tile == 0), stop=(tile == TC - 1), skip_group_check=True)
                    last.then_inc(sg["pv_done"], 1)

                def out_part(u, n, b, p, front):
                    if u == 6:
                        pe.wait_ge(sg["oT_ready"], n + 1)
                        if front:
                            pe.wait_ge(sg["v_ready"], front[0] + 1)
                        else:
                            pe.wait_ge(sg["added"], n)
                        for c in range(TC):
                            at = slice(c * P, (c + 1) * P)
                            if p == 0:
                                nc.tensor.matmul(ps_r[:, at], core.ones[0:1, :], bias[:], start=True, stop=False)
                            last = nc.tensor.matmul(ps_r[:, at], oT[:, at], wo[:, p, :], start=(p != 0), stop=True)
                        last.then_inc(sg["y_in"], 1)

                def body(item):
                    front, score, value, out = item(FRONT), item(SCORE), item(VALUE), item(OUT)
                    for u in range(UNITS):
                        if value:
                            turn(u, *value)
                        if front:
                            front_part(u, *front)
                        if out:
                            out_part(u, *out, front)
                        if score:
                            scores(u, *score)
                        if value and u in (2, 4, 6):
                            values(u // 2 - 1, *value)
                    if value:
                        values(TC - 1, *value)
                steps(pe, body)

            @block.scalar
            def _(act):
                def exps(u, n, b, p):
                    head, tile, keys = unit(u)
                    act.wait_ge(sg["low_done"], UNITS * n + u + 1)
                    wait(act, sg["p_turned"], UNITS * (n - 2) + u + 1)
                    if u == 0:
                        wait(act, sg["inverse_done"], UNITS * (n - 1))
                    nc.scalar.activation(prob[:, p % 2, u, 0:keys], ps_s[2 * head + u // 2 % 2][:, 0:keys], ACT.Exp, bias=low[:, p % 2, u:u + 1],
                                         scale=-1.0, accum_out=total[:, p % 2, u:u + 1]).then_inc(sg["exp_done"], 1)

                def body(item):
                    front, score, value = item(FRONT), item(SCORE), item(VALUE)
                    for u in range(UNITS):
                        if value and u % 2:
                            tile = unit(u)[1]
                            act.wait_ge(sg["p_turned"], UNITS * value[0] + u + 1)
                            wait(act, sg["pv_done"], TC * value[0] + tile - 1)
                            nc.scalar.copy(probT[:, 1, tile % 2, 0:S - tile * P], ps_t[1][:, 0:S - tile * P]).then_inc(sg["probT_act"], 1)
                        if front and u == 0 and front[2] == 0:
                            act.wait_ge(sg["x_turned"], front[1] + 1)
                            wait(act, sg["v_in"], front[0])
                            nc.scalar.copy(xT[:], ps_r[:]).then_inc(sg["xT_ready"], 1)
                        if front and u == 5:
                            act.wait_ge(sg["v_in"], front[0] + 1)
                            wait(act, sg["pv_done"], TC * (front[0] - 3))
                            nc.scalar.copy(v[:, front[2] % 4].rearrange("p c d -> p (c d)"), ps_r[:]).then_inc(sg["v_ready"], 1)
                        if score:
                            exps(u, *score)
                steps(act, body)

            @block.vector
            def _(dve):
                def invert(u, n, p):
                    dve.wait_ge(sg["exp_done"], UNITS * n + u + 1)
                    wait(dve, sg["divided"], UNITS * (n - 2) + u + 1)
                    nc.vector.reciprocal(inverse[:, p % 2, u:u + 1], total[:, p % 2, u:u + 1]).then_inc(sg["inverse_done"], 1)

                def body(item):
                    ln, front, score, value, out = item(LN), item(FRONT), item(SCORE), item(VALUE), item(OUT)
                    if ln and ln[2] == 0:
                        for c in range(TC):
                            norm.stats(dve, TC * ln[1] + c, c, tile_of(X, TC * ln[1] + c))
                    if ln and ln[2] == 1:
                        wait(dve, sg["x_turned"], ln[1])
                        for c in range(TC):
                            dve.wait_ge(norm.rstd_done, TC * ln[1] + c + 1)
                            norm.apply(xn[:, c, :], tile_of(X, TC * ln[1] + c), c).then_inc(sg["x_normed"], 1)
                    for u in range(UNITS):
                        if out and u == 0:
                            dve.wait_ge(sg["pv_done"], TC * (out[0] + 1))
                            wait(dve, sg["y_in"], out[0])
                            nc.vector.tensor_copy(oT[:], ps_o[:]).then_inc(sg["oT_ready"], 1)
                        if value and u % 2 == 0:
                            tile = unit(u)[1]
                            dve.wait_ge(sg["p_turned"], UNITS * value[0] + u + 1)
                            wait(dve, sg["pv_done"], TC * value[0] + tile - 1)
                            nc.vector.tensor_copy(probT[:, 0, tile % 2, 0:S - tile * P], ps_t[0][:, 0:S - tile * P]).then_inc(sg["probT_dve"], 1)
                        if front and 1 <= u <= 4:
                            n = front[0]
                            k, odd = (u - 1) // 2, (u - 1) % 2
                            dve.wait_ge(sg["qk_in"], 4 * n + u)
                            wait(dve, sg["rotated"], 2 * (n - 1) + k + 1)
                            nc.vector.tensor_tensor((by_sin if odd else by_cos)[:, k], ps_r[:], (sin if odd else cos)[:], ALU.mult)\
                                .then_inc(sg["multiplied"], 1)
                        if score:
                            head, tile, keys = unit(u)
                            n, p = score[0], score[2]
                            dve.wait_ge(sg["s_in"], UNITS * n + u + 1)
                            if u == 0:
                                wait(dve, sg["exp_done"], UNITS * (n - 1))
                            nc.vector.tensor_reduce(low[:, p % 2, u:u + 1], ps_s[2 * head + u // 2 % 2][:, 0:keys], AX.X, ALU.min)\
                                .then_inc(sg["low_done"], 1)
                            if u:
                                invert(u - 1, n, p)
                    if score:
                        invert(UNITS - 1, score[0], score[2])
                    if out:
                        n, b = out[0], out[1]
                        dve.wait_ge(sg["y_in"], n + 1)
                        xb = X[:, bass.ds(b * TC, TC), :].rearrange("p c d -> p (c d)")
                        wait(dve, sg["added"], n)
                        nc.vector.tensor_tensor(xb, ps_r[:], xb, ALU.add).then_inc(sg["added"], 1)
                steps(dve, body)


def build(nc, a, out):
    with ExitStack() as ctx:
        core = Core(nc, ctx)
        core.load(a["L0_attn_a_x"].rearrange("b s d -> (b s) d"))
        chunk_attention(core, "ca", a["L0_attn_a_Wq"], a["L0_attn_a_Wk"], a["L0_attn_a_Wv"])
        expert_ffn(core, "moe1", a["L0_ffn_centroids"], a["L0_ffn_gamma"], a["L0_ffn_beta"], a["L0_ffn_W1"], a["L0_ffn_b1"], a["L0_ffn_W2"], a["L0_ffn_b2"])
        rope_attention(core, "ra", a["L0_attn_b_Wq"], a["L0_attn_b_Wk"], a["L0_attn_b_Wv"], a["L0_attn_b_Wo"], a["L0_attn_b_bo"], a["rope_cos"], a["rope_sin"])
        expert_ffn(core, "moe3", a["L0_ffn_centroids"], a["L0_ffn_gamma"], a["L0_ffn_beta"], a["L0_ffn_W1"], a["L0_ffn_b1"], a["L0_ffn_W2"], a["L0_ffn_b2"])
        gated_slots(core, "gsa", a["L1_attn_a_Wq"], a["L1_attn_a_Wk"], a["L1_attn_a_Wv"], a["L1_attn_a_Wf"], a["L1_attn_a_g_w"], a["L1_attn_a_Wo"], a["gsa_part"], a["gsa_causal"], a["gsa_go_on"])
        ternary_ffn(core, "ffn15", a["L1_ffn_W_fc"], a["L1_ffn_ln_w"], a["L1_ffn_ln_b"], a["L1_ffn_W_proj"])
        channel_ssm(core, "ssm", a["L1_attn_b_A"], a["L1_attn_b_Bp"], a["L1_attn_b_Cp"], a["L1_attn_b_Dp"], a["L1_attn_b_Wg"], a["L1_attn_b_bg"], a["L1_attn_b_gamma"], a["L1_attn_b_beta"], a["ssm_same"], a["ssm_shift"])
        ternary_ffn(core, "ffn17", a["L1_ffn_W_fc"], a["L1_ffn_ln_w"], a["L1_ffn_ln_b"], a["L1_ffn_W_proj"])
        core.store(out.rearrange("b s d -> (b s) d"))


def rope_tables():
    dim = 64
    freq = (1.0 / np.power(np.float32(10000.0), np.arange(0, dim, 2, dtype=np.float32) / np.float32(dim))).astype(np.float32)
    angle = (np.arange(S, dtype=np.float32)[None, :] * freq[:, None]).astype(np.float32)
    cos, sin = np.cos(angle), np.sin(angle)
    cos_t = np.repeat(cos, 2, axis=0)
    sin_t = np.repeat(sin, 2, axis=0)
    sin_t[0::2] *= -1
    return np.tile(cos_t, (2, 1)).astype(np.float32), np.tile(sin_t, (2, 1)).astype(np.float32)


def kernel(**inputs):
    import concourse.bacc as bacc
    from concourse.bass_utils import run_bass_kernel_spmd

    nc = bacc.Bacc("TRN2", target_bir_lowering=False, num_devices=1)
    given = {name: np.ascontiguousarray(v) for name, v in inputs.items()}
    given["rope_cos"], given["rope_sin"] = rope_tables()
    given["ssm_same"], given["ssm_shift"] = ssm_tables()
    given["gsa_part"], given["gsa_causal"], given["gsa_go_on"] = slot_tables()
    arrays, aps = {}, {}
    for name, v in given.items():
        arrays[f"in_{name}"] = v
        aps[name] = nc.dram_tensor(f"in_{name}", v.shape, mybir.dt.from_np(v.dtype), kind="ExternalInput").ap()
    out = nc.dram_tensor("out_x", (NB, S, D), F32, kind="ExternalOutput").ap()
    build(nc, aps, out)
    got = run_bass_kernel_spmd(nc, [arrays], core_ids=[0])
    return got.results[0]["out_x"]
```
